# Optimizing a Trainium2 kernel written in Bass

```python
import numpy as np
import jax
import jax.numpy as jnp

def _softmax(x, axis=-1):
    return jax.nn.softmax(x, axis=axis)

def _gelu(x):
    return jax.nn.gelu(x, approximate=True)

def _silu(x):
    return jax.nn.silu(x)

def _sigmoid(x):
    return jax.nn.sigmoid(x)

def _layernorm(x, axis=-1, eps=1e-05):
    m = jnp.mean(x, axis=axis, keepdims=True)
    v = jnp.var(x, axis=axis, keepdims=True)
    return (x - m) / jnp.sqrt(v + eps)

def _scatter_add(tgt, idx, src, axis=0):
    return tgt.at[idx].add(src)

def _segment_sum(src, seg, n):
    return jax.ops.segment_sum(src, seg, n)
kernel_name = 'mk_prb_d2_jaxref_r8_12c26e'

def setup_inputs(seed: int=0):
    np.random.seed(seed)
    _w = jnp.asarray

    def _L0_attn_setup():
        import jax, jax.numpy as jnp
        import numpy as np
        import math
        B, S, DIM, HEADS = (2, 256, 128, 16)

        def _alibi_slopes(n_heads):

            def pow2_slopes(n):
                start = 2 ** (-2 ** (-(math.log2(n) - 3)))
                return [start * start ** i for i in range(n)]
            if math.log2(n_heads).is_integer():
                slopes = pow2_slopes(n_heads)
            else:
                closest = 2 ** math.floor(math.log2(n_heads))
                slopes = pow2_slopes(closest)
                slopes += pow2_slopes(2 * closest)[0::2][:n_heads - closest]
            return np.asarray(slopes, dtype=np.float32).reshape(n_heads, 1, 1)
        key = jax.random.key(seed)
        k1, k2, k3 = jax.random.split(key, 3)
        x = jax.random.normal(k1, (B, S, DIM), dtype=jnp.float32)
        W_qkv = jax.random.normal(k2, (3 * DIM, DIM), dtype=jnp.float32) * 0.02
        W_o = jax.random.normal(k3, (DIM, DIM), dtype=jnp.float32) * 0.02
        return {'x': x, 'W_qkv': W_qkv, 'W_o': W_o}
    _L0_attn_in = _L0_attn_setup()

    def _L0_ffn_setup():
        import jax, jax.numpy as jnp
        import numpy as np
        EPS = 1e-05

        def _quantize(W):
            gamma = jnp.mean(jnp.abs(W))
            return jnp.clip(jnp.round(W / (gamma + EPS)), -1.0, 1.0)
        key = jax.random.key(seed)
        k_x, k_w1, k_b1, k_w2, k_b2 = jax.random.split(key, 5)
        n_embd = 128
        d_ff = 4 * n_embd
        B, S = (4, 512)
        bound1 = 1.0 / np.sqrt(n_embd)
        bound2 = 1.0 / np.sqrt(d_ff)
        x = jax.random.normal(k_x, (B, S, n_embd), dtype=jnp.float32)
        W1 = jax.random.uniform(k_w1, (d_ff, n_embd), jnp.float32, -bound1, bound1)
        b1 = jax.random.uniform(k_b1, (d_ff,), jnp.float32, -bound1, bound1)
        W2 = jax.random.uniform(k_w2, (n_embd, d_ff), jnp.float32, -bound2, bound2)
        b2 = jax.random.uniform(k_b2, (n_embd,), jnp.float32, -bound2, bound2)
        return {'x': x, 'W1': W1, 'b1': b1, 'W2': W2, 'b2': b2}
    _L0_ffn_in = _L0_ffn_setup()

    def _L1_attn_setup():
        import jax, jax.numpy as jnp
        import numpy as np
        NL, H, N, B, L = (4, 128, 32, 8, 128)

        def _layernorm_channels(z, w, b):
            mu = jnp.mean(z, axis=1, keepdims=True)
            var = jnp.mean((z - mu) ** 2, axis=1, keepdims=True)
            zn = (z - mu) * jax.lax.rsqrt(var + 1e-05)
            return zn * w[None, :, None] + b[None, :, None]

        def _s4d_layer(z, log_dt, A_re_log, A_im, C_re, C_im, D_skip, W, bvec):
            Bz, Hh, Lz = z.shape
            dt = jnp.exp(log_dt)
            A = -jnp.exp(A_re_log) + 1j * A_im
            dtA = A * dt[:, None]
            C = (C_re + 1j * C_im) * (jnp.expm1(dtA) / A)
            l = jnp.arange(Lz, dtype=jnp.float32)
            K = 2.0 * jnp.einsum('hn,hnl->hl', C, jnp.exp(dtA[:, :, None] * l)).real
            kf = jnp.fft.rfft(K, n=2 * Lz)
            uf = jnp.fft.rfft(z, n=2 * Lz)
            y = jnp.fft.irfft(uf * kf, n=2 * Lz)[..., :Lz]
            y = y + z * D_skip[:, None]
            y = jax.nn.gelu(y)
            out = jnp.einsum('oh,bhl->bol', W, y) + bvec[None, :, None]
            return out[:, :Hh] * jax.nn.sigmoid(out[:, Hh:])
        key = jax.random.key(seed)
        ks = jax.random.split(key, 10)
        x = jax.random.normal(ks[0], (B, L, H), dtype=jnp.float32)
        ln_w = jnp.ones((NL, H), jnp.float32)
        ln_b = jnp.zeros((NL, H), jnp.float32)
        log_dt = (jax.random.uniform(ks[1], (NL, H)) * (np.log(0.1) - np.log(0.001)) + np.log(0.001)).astype(jnp.float32)
        A_re_log = jnp.full((NL, H, N), np.log(0.5), jnp.float32)
        A_im = jnp.broadcast_to(np.pi * jnp.arange(N, dtype=jnp.float32), (NL, H, N))
        C_re = jax.random.normal(ks[2], (NL, H, N), jnp.float32) * 0.5 ** 0.5
        C_im = jax.random.normal(ks[3], (NL, H, N), jnp.float32) * 0.5 ** 0.5
        D_skip = jax.random.normal(ks[4], (NL, H), jnp.float32)
        W_out = jax.random.normal(ks[5], (NL, 2 * H, H), jnp.float32) * (1.0 / np.sqrt(H))
        b_out = jnp.zeros((NL, 2 * H), jnp.float32)
        return {'x': x, 'ln_w': ln_w, 'ln_b': ln_b, 'log_dt': log_dt, 'A_re_log': A_re_log, 'A_im': A_im, 'C_re': C_re, 'C_im': C_im, 'D_skip': D_skip, 'W_out': W_out, 'b_out': b_out}
    _L1_attn_in = _L1_attn_setup()

    def _L1_ffn_setup():
        import jax, jax.numpy as jnp
        import numpy as np
        B, S, H, E = (4, 256, 128, 8)
        key = jax.random.key(seed)
        k1, k2, k3 = jax.random.split(key, 3)
        scale_w = 1.0 / np.sqrt(H)
        return {'x': jax.random.normal(k1, (B, S, H), dtype=jnp.float32), 'router_w': jax.random.normal(k2, (H, E), dtype=jnp.float32) * scale_w, 'router_b': jnp.zeros((E,), dtype=jnp.float32), 'expert_w': jax.random.normal(k3, (E, H, H), dtype=jnp.float32) * scale_w, 'expert_b': jnp.zeros((E, H), dtype=jnp.float32)}
    _L1_ffn_in = _L1_ffn_setup()
    _d = {'L0_attn_x': _L0_attn_in['x'], 'L0_attn_W_qkv': _L0_attn_in['W_qkv'], 'L0_attn_W_o': _L0_attn_in['W_o'], 'L0_ffn_W1': _L0_ffn_in['W1'], 'L0_ffn_b1': _L0_ffn_in['b1'], 'L0_ffn_W2': _L0_ffn_in['W2'], 'L0_ffn_b2': _L0_ffn_in['b2'], 'L1_attn_ln_w': _L1_attn_in['ln_w'], 'L1_attn_ln_b': _L1_attn_in['ln_b'], 'L1_attn_log_dt': _L1_attn_in['log_dt'], 'L1_attn_A_re_log': _L1_attn_in['A_re_log'], 'L1_attn_A_im': _L1_attn_in['A_im'], 'L1_attn_C_re': _L1_attn_in['C_re'], 'L1_attn_C_im': _L1_attn_in['C_im'], 'L1_attn_D_skip': _L1_attn_in['D_skip'], 'L1_attn_W_out': _L1_attn_in['W_out'], 'L1_attn_b_out': _L1_attn_in['b_out'], 'L1_ffn_router_w': _L1_ffn_in['router_w'], 'L1_ffn_router_b': _L1_ffn_in['router_b'], 'L1_ffn_expert_w': _L1_ffn_in['expert_w'], 'L1_ffn_expert_b': _L1_ffn_in['expert_b']}
    _x0 = _d['L0_attn_x']
    _d['L0_attn_x'] = jax.random.normal(jax.random.fold_in(jax.random.key(seed), 1), (16, 512, 128), dtype=_x0.dtype)
    del _x0
    return _d

def reference(L0_attn_x, L0_attn_W_qkv, L0_attn_W_o, L0_ffn_W1, L0_ffn_b1, L0_ffn_W2, L0_ffn_b2, L1_attn_ln_w, L1_attn_ln_b, L1_attn_log_dt, L1_attn_A_re_log, L1_attn_A_im, L1_attn_C_re, L1_attn_C_im, L1_attn_D_skip, L1_attn_W_out, L1_attn_b_out, L1_ffn_router_w, L1_ffn_router_b, L1_ffn_expert_w, L1_ffn_expert_b):

    def _L0_attn_ref(x, W_qkv, W_o):
        import jax, jax.numpy as jnp
        import numpy as np
        import math
        B, S, DIM, HEADS = (2, 256, 128, 16)

        def _alibi_slopes(n_heads):

            def pow2_slopes(n):
                start = 2 ** (-2 ** (-(math.log2(n) - 3)))
                return [start * start ** i for i in range(n)]
            if math.log2(n_heads).is_integer():
                slopes = pow2_slopes(n_heads)
            else:
                closest = 2 ** math.floor(math.log2(n_heads))
                slopes = pow2_slopes(closest)
                slopes += pow2_slopes(2 * closest)[0::2][:n_heads - closest]
            return np.asarray(slopes, dtype=np.float32).reshape(n_heads, 1, 1)
        b, s, d = x.shape
        h = HEADS
        hd = d // h
        scale = hd ** (-0.5)
        qkv = x @ W_qkv.T
        q, k, v = jnp.split(qkv, 3, axis=-1)
        q = q.reshape(b, s, h, hd).transpose(0, 2, 1, 3)
        k = k.reshape(b, s, h, hd).transpose(0, 2, 1, 3)
        v = v.reshape(b, s, h, hd).transpose(0, 2, 1, 3)
        scores = jnp.einsum('bhqd,bhkd->bhqk', q, k) * scale
        pos = jnp.arange(s)
        rel = (pos[None, :] - pos[:, None]).astype(scores.dtype)
        slopes = jnp.asarray(_alibi_slopes(h))
        scores = scores - slopes * rel
        causal_mask = pos[None, :] > pos[:, None]
        scores = jnp.where(causal_mask, jnp.finfo(scores.dtype).min, scores)
        weights = jax.nn.softmax(scores, axis=-1)
        out = jnp.einsum('bhqk,bhkd->bhqd', weights, v)
        out = out.transpose(0, 2, 1, 3).reshape(b, s, d)
        return out @ W_o.T

    def _L0_ffn_ref(x, W1, b1, W2, b2):
        import jax, jax.numpy as jnp
        import numpy as np
        EPS = 1e-05

        def _quantize(W):
            gamma = jnp.mean(jnp.abs(W))
            return jnp.clip(jnp.round(W / (gamma + EPS)), -1.0, 1.0)
        Wq1 = _quantize(W1)
        Wq2 = _quantize(W2)
        h = jax.nn.relu(jnp.einsum('bsd,fd->bsf', x, Wq1) + b1)
        out = jnp.einsum('bsf,df->bsd', h, Wq2) + b2
        return out

    def _L1_attn_ref(x, ln_w, ln_b, log_dt, A_re_log, A_im, C_re, C_im, D_skip, W_out, b_out):
        import jax, jax.numpy as jnp
        import numpy as np
        NL, H, N, B, L = (4, 128, 32, 8, 128)

        def _layernorm_channels(z, w, b):
            mu = jnp.mean(z, axis=1, keepdims=True)
            var = jnp.mean((z - mu) ** 2, axis=1, keepdims=True)
            zn = (z - mu) * jax.lax.rsqrt(var + 1e-05)
            return zn * w[None, :, None] + b[None, :, None]

        def _s4d_layer(z, log_dt, A_re_log, A_im, C_re, C_im, D_skip, W, bvec):
            Bz, Hh, Lz = z.shape
            dt = jnp.exp(log_dt)
            A = -jnp.exp(A_re_log) + 1j * A_im
            dtA = A * dt[:, None]
            C = (C_re + 1j * C_im) * (jnp.expm1(dtA) / A)
            l = jnp.arange(Lz, dtype=jnp.float32)
            K = 2.0 * jnp.einsum('hn,hnl->hl', C, jnp.exp(dtA[:, :, None] * l)).real
            kf = jnp.fft.rfft(K, n=2 * Lz)
            uf = jnp.fft.rfft(z, n=2 * Lz)
            y = jnp.fft.irfft(uf * kf, n=2 * Lz)[..., :Lz]
            y = y + z * D_skip[:, None]
            y = jax.nn.gelu(y)
            out = jnp.einsum('oh,bhl->bol', W, y) + bvec[None, :, None]
            return out[:, :Hh] * jax.nn.sigmoid(out[:, Hh:])
        h = jnp.transpose(x, (0, 2, 1))
        for i in range(NL):
            z = _layernorm_channels(h, ln_w[i], ln_b[i])
            z = _s4d_layer(z, log_dt[i], A_re_log[i], A_im[i], C_re[i], C_im[i], D_skip[i], W_out[i], b_out[i])
            h = z + h
        return jnp.transpose(h, (0, 2, 1))

    def _L1_ffn_ref(x, router_w, router_b, expert_w, expert_b):
        import jax, jax.numpy as jnp
        import numpy as np
        B, S, H, E = (4, 256, 128, 8)
        b, s, h = x.shape
        xt = x.reshape(b * s, h)
        logits = xt @ router_w + router_b
        probs = jax.nn.softmax(logits, axis=-1)
        gate = jnp.max(probs, axis=-1)
        idx = jnp.argmax(probs, axis=-1)
        out_all = jnp.einsum('th,ehd->ted', xt, expert_w) + expert_b[None, :, :]
        e_out = jnp.take_along_axis(out_all, idx[:, None, None], axis=1)[:, 0, :]
        y = gate[:, None] * e_out
        return y.reshape(b, s, h)
    x = L0_attn_x
    xn = _layernorm(x, axis=-1)
    x = x + _L0_attn_ref(xn, L0_attn_W_qkv, L0_attn_W_o) + _L0_ffn_ref(xn, L0_ffn_W1, L0_ffn_b1, L0_ffn_W2, L0_ffn_b2)
    xn = _layernorm(x, axis=-1)
    x = x + _L1_attn_ref(xn, L1_attn_ln_w, L1_attn_ln_b, L1_attn_log_dt, L1_attn_A_re_log, L1_attn_A_im, L1_attn_C_re, L1_attn_C_im, L1_attn_D_skip, L1_attn_W_out, L1_attn_b_out) + _L1_ffn_ref(xn, L1_ffn_router_w, L1_ffn_router_b, L1_ffn_expert_w, L1_ffn_expert_b)
    return x

_drawn_inputs = setup_inputs


def setup_inputs(seed=0):
    import zlib

    import numpy as np

    out = dict(_drawn_inputs(seed))
    spreads = {'L1_attn_ln_w': (1.0, 0.6),
     'L1_attn_ln_b': (0.0, 0.8),
     'L1_attn_A_re_log': (-0.6931471824645996, 0.6),
     'L1_attn_b_out': (0.0, 0.8),
     'L1_ffn_router_b': (0.0, 2.0),
     'L1_ffn_expert_b': (0.0, 2.0)}
    factors = {'L0_attn_W_qkv': 8.0,
     'L0_attn_W_o': 8.0,
     'L0_ffn_b1': 8.0,
     'L0_ffn_b2': 64.0,
     'L1_attn_log_dt': 64.0,
     'L1_attn_A_im': 48.0,
     'L1_attn_C_re': 57.408,
     'L1_attn_C_im': 64.0,
     'L1_attn_D_skip': 7.524,
     'L1_attn_W_out': 5.069,
     'L1_ffn_router_w': 8.0,
     'L1_ffn_expert_w': 8.0}
    for name, (base, spread) in spreads.items():
        noise = np.random.default_rng([zlib.crc32(name.encode()), seed]).standard_normal(out[name].shape)
        drawn = base * np.exp(spread * noise) if base else spread * noise
        out[name] = jnp.asarray(drawn.astype(out[name].dtype))
    for name, factor in factors.items():
        out[name] = (out[name] * factor).astype(out[name].dtype)
    return out
```

```python
import math
from contextlib import ExitStack

import numpy as np

import concourse.bass as bass
from concourse import mybir

FP32 = mybir.dt.float32
BF16 = mybir.dt.bfloat16
ALU = mybir.AluOpType
ACT = mybir.ActivationFunctionType
AX = mybir.AxisListType

B, S, D = 16, 512, 128
P = 128
C = S // P
H, HD = 16, 8
HG = 4
G = H // HG
FF = 4 * D
NF = FF // P
NL, NM = 4, 32
E = 8
EPS = 1e-5
BIG = -1e30
MAGIC = 1.5 * 2.0 ** 23

TOKENS = np.concatenate([np.arange(P) + c * P if c < C // 2 else (c + 1) * P - 1 - np.arange(P) for c in range(C)])

Q_PARTS = (0, 0, 1, 0, 2, 1)
K_PARTS = (0, 1, 0, 2, 0, 1)
N_PROD = len(Q_PARTS)
ROW_POS = N_PROD * HD
ROW_MAX = 96
FILLS = 11
TILES = 5
STACKS = 2 * N_PROD


def bf16_parts(a):
    bf = mybir.dt.np(BF16)
    out, rest = [], np.asarray(a, np.float32)
    for _ in range(3):
        part = rest.astype(bf)
        out.append(part)
        rest = rest - part.astype(np.float32)
    return out


def shape_constants():
    bf = mybir.dt.np(BF16)
    c = {}
    c["ident"] = np.eye(P, dtype=np.float32)
    c["ident_bf"] = np.eye(P, dtype=np.float32).astype(bf)
    i = np.arange(P)
    c["mask_bf"] = np.stack([np.where(i[None, :] > i[:, None], BIG, 0.0),
                             np.where(i[None, :] < i[:, None], BIG, 0.0)], 1).astype(bf)
    start = 2.0 ** (-2.0 ** (-(math.log2(H) - 3)))
    slopes = np.asarray([start * start ** h for h in range(H)], np.float32)
    parts = bf16_parts(slopes)
    pos = TOKENS
    low, high = (pos % 256).astype(np.float32), (pos - pos % 256).astype(np.float32)
    qrows, krows = np.zeros((12, H, S), np.float32), np.zeros((12, H, S), np.float32)
    for n, s in enumerate(parts):
        s = s.astype(np.float32)[:, None]
        for m, at in enumerate((low, high)):
            qrows[2 * n + m], krows[2 * n + m] = s, -at[None, :]
            qrows[6 + 2 * n + m], krows[6 + 2 * n + m] = at[None, :], s
    c["pos_q"], c["pos_k"] = qrows.astype(bf), krows.astype(bf)
    t = np.arange(S // 2) + 0.5
    even, odd = np.arange(0, S, 2), np.arange(1, S, 2)
    sin_even = even.copy()
    sin_even[0] = S
    w = np.pi / S
    cos_e, cos_o = np.cos(w * np.outer(t, even)), np.cos(w * np.outer(t, odd))
    sin_e, sin_o = np.sin(w * np.outer(t, sin_even)), np.sin(w * np.outer(t, odd))
    fwd = np.stack([np.concatenate([cos_e, sin_o], 1), np.concatenate([cos_o, sin_e], 1)])
    c["dft"] = np.ascontiguousarray(fwd.reshape(2, 2, P, S).transpose(2, 0, 1, 3)).astype(np.float32)
    inv = fwd.transpose(0, 2, 1)
    c["idft"] = np.ascontiguousarray(inv.reshape(2, 4, P, S // 2).transpose(2, 0, 1, 3)).astype(np.float32)
    l = np.arange(S)
    freq = np.concatenate([even, odd])
    weight = np.where(freq == 0, 1.0, 2.0) / (2 * S)
    first = sin_even[:P]
    first_weight = np.where(first == S, 1.0, 2.0) / (2 * S)
    a1 = np.cos(w * np.outer(l, freq)) * weight
    bb = np.sin(w * np.outer(l, freq)) * weight
    a2 = np.cos(w * np.outer(l, first)) * first_weight
    kt = np.concatenate([a1, bb, a2], 1)
    c["kdft"] = np.ascontiguousarray(kt.reshape(C, P, 9 * P).transpose(1, 0, 2)).astype(np.float32)
    dw = np.concatenate([weight, np.zeros(S), first_weight]).reshape(9, P).T
    c["dweight"] = np.ascontiguousarray(dw).astype(np.float32)
    real = (np.arange(P) // NM) % 2 == 0
    one, two = np.where(real, 0.25, 0.0), np.where(real, 0.0, 0.25)
    c["phase"] = np.stack([one, two, np.where(real, 1.0, -1.0), 2 * np.pi * one, 2 * np.pi * two, 0 * one], 1).astype(np.float32)
    c["steps"] = np.arange(NM, dtype=np.float32)
    token = np.concatenate([np.arange(S // 2), S - 1 - np.arange(S // 2)])
    c["prefix"] = np.ascontiguousarray((l[:, None] <= token[None, :]).astype(np.float32).reshape(C, P, S).transpose(1, 0, 2))
    c["rev"] = np.broadcast_to(E - np.arange(E, dtype=np.float32), (C, E)).copy()
    return c


def at(n, per, k):
    return n * per + k


def attention(nc, io, x1_dram, NB=B):
    ctx = ExitStack()

    def sb(name, shape, dt=FP32):
        return ctx.enter_context(nc.sbuf_tensor(name, shape, dt))

    def pb(name, shape, dt=FP32):
        return ctx.enter_context(nc.psum_tensor(name, shape, dt))

    def sem(name):
        return ctx.enter_context(nc.semaphore(name))

    with ctx:
        wqkv = sb("wqkv", [P, 3 * D])
        wo = sb("wo", [P, D])
        w1 = sb("w1", [P, FF])
        w2 = sb("w2", [P, NF, D])
        wtmp = sb("wtmp", [P, FF])
        b1 = sb("b1", [P, NF])
        b2f = sb("b2f", [P, D])
        ident = sb("ident", [P, P])
        ident_bf = sb("ident_bf", [P, P], BF16)
        mask_bf = sb("mask_bf", [P, 2, P], BF16)
        ones = sb("ones", [P, P])
        gsum = sb("gsum", [P, 8])
        minus_half = sb("minus_half", [P, C])
        x_sb = sb("x_sb", [P, 2, C, D])
        xr = sb("xr", [P, 2, C, D])
        stats = sb("stats", [P, C, 6])
        mv = sb("mv", [P, C, 2])
        rstd = sb("rstd", [P, C])
        xn = sb("xn", [P, C, D])
        xnT = sb("xnT", [P, S])
        parts = sb("parts", [P, 2, 3, S], BF16)
        rest = sb("rest", [P, 2, S])
        qs = sb("qs", [P, 2, H, S], BF16)
        ks = sb("ks", [P, 2, H, S], BF16)
        v_aug = sb("v_aug", [P, 2, C, H, 32])
        hT = sb("hT", [P, NF, S])
        mx = sb("mx", [P, 2, HG, C])
        mrow = sb("mrow", [HG * C, 2, 2, P], BF16)
        p_sb = sb("p_sb", [P, 2, TILES, 2 * S])
        o_sb = sb("o_sb", [P, S])
        rden = sb("rden", [P, C, HG])
        o_tok = sb("o_tok", [P, C, D])
        oT = sb("oT", [P, S])
        x1 = sb("x1", [P, C, D])

        fill_ps = [pb(f"fill_ps{i}", [P, S]) for i in range(2)]
        tile_ps = [pb(f"tile_ps{i}", [P, 2 * S]) for i in range(2)]
        o_ps = pb("o_ps", [P, S])
        misc_ps = pb("misc_ps", [P, S])

        loaded = sem("loaded")
        set_up = sem("set_up")
        stacks_zero = sem("stacks_zero")
        x_loaded = sem("x_loaded")
        pre_link = sem("pre_link")
        abs_done = sem("abs_done")
        gamma_ps = sem("gamma_ps")
        weights_ready = sem("weights_ready")
        ln_stat = sem("ln_stat")
        ln_mv = sem("ln_mv")
        ln_eps = sem("ln_eps")
        ln_rstd = sem("ln_rstd")
        ln_done = sem("ln_done")
        xT_put, xT_taken = sem("xT_put"), sem("xT_taken")
        qk_put, qk_taken = sem("qk_put"), sem("qk_taken")
        split_step = sem("split_step")
        v_put, v_taken = sem("v_put"), sem("v_taken")
        ffn1_put, ffn1_taken = sem("ffn1_put"), sem("ffn1_taken")
        ffn2_put, ffn2_taken = sem("ffn2_put"), sem("ffn2_taken")
        mrow_put, mrow_high, mrow_taken = sem("mrow_put"), sem("mrow_high"), sem("mrow_taken")
        otr_put, rden_done, otr_taken = sem("otr_put"), sem("rden_done"), sem("otr_taken")
        oT_put, oT_taken = sem("oT_put"), sem("oT_taken")
        out_put, out_taken = sem("out_put"), sem("out_taken")
        stacked = sem("stacked")
        filled, reduced = sem("filled"), sem("reduced")
        mrow_in = sem("mrow_in")
        scored, exped, masked = sem("scored"), sem("exped"), sem("masked")
        pv_done, o_copied = sem("pv_done"), sem("o_copied")
        stored = sem("stored")

        n_loads = 11
        LAST = NB - 1

        def fill_plan():
            plan = [(3, (h,)) for h in range(4)] + [(2, (h,)) for h in range(4)]
            plan += [(1, (0, 1)), (1, (2, 3)), (0, (0, 1, 2, 3))]
            return plan

        def unit_steps(g, front, back, nxt):
            own = g >= 2
            exp = front if own else back
            pv = front if g == 3 else back
            f = [("fill", i) for i in range(FILLS)] if front else []
            b = [("tile", t) for t in range(TILES)] if exp else []
            v = [("pv", kb) for kb in range(C)] if pv else []
            m = [[], [], [], [], []]
            if (front if g > 0 else back):
                m[0].append(("mrow", 0))
            if pv:
                m[3].append(("otr", 0))
            if g == 0 and front:
                m[1].append(("ffn1", 0)), m[2].append(("ffn1", 1))
            if g == 1 and front:
                m[1].append(("ffn1", 2)), m[2].append(("ffn1", 3)), m[4].append(("ffn2", 0))
            if g == 1 and nxt:
                m[4].append(("ln", 0))
            if g == 2 and nxt:
                m[1].append(("xT", 0)), m[2].append(("qk", 0)), m[4].append(("qk", 1))
            if g == 3:
                if nxt:
                    m[1].append(("v", 0))
                if back:
                    m[2].append(("oT", 0)), m[4].append(("out", 0))
            steps = []
            for i in range(5):
                steps += f[2 * i:2 * i + 2] + b[i:i + 1] + v[i:i + 1] + m[i]
            return steps + f[10:]

        TAKEN = {"mrow": (mrow_taken, G), "otr": (otr_taken, G), "ffn1": (ffn1_taken, NF), "ffn2": (ffn2_taken, 1),
                 "xT": (xT_taken, 1), "qk": (qk_taken, 2), "v": (v_taken, 1), "oT": (oT_taken, 1), "out": (out_taken, 1)}

        def misc_index(kind, i, n, g):
            if kind == "mrow":
                return (n, g - 1) if g else (n - 1, G - 1)
            if kind == "otr":
                return (n, 0) if g == 3 else (n - 1, g + 1)
            if kind in ("xT", "v", "qk"):
                return n + 1, i
            if kind in ("oT", "out"):
                return n - 1, i
            return n, i

        def exp_unit(n, g):
            return (n, g - 2) if g >= 2 else (n - 1, g + 2)

        def pv_unit(n, g):
            return (n, 0) if g == 3 else (n - 1, g + 1)

        def drive(handle, eng):
            handle.before()
            handle.pre(0)
            handle.slot(0, 0, True, False, True)
            handle.slot(1, 1, True, True, True)
            with eng.Fori(1, (NB - 2) // 2) as j:
                handle.slot(j * 2, 0, True, True, True)
                handle.slot(j * 2 + 1, 1, True, True, True)
            handle.slot(LAST - 1, 0, True, True, True)
            handle.slot(LAST, 1, True, True, False)
            handle.slot(NB, NB % 2, False, True, False)
            handle.after()

        block = ctx.enter_context(nc.Block())

        @block.sync
        def _(sp):
            class Sync:
                def before(self):
                    for dst, src in ((wqkv[:, :], io["WqkvT"]), (wo[:, :], io["WoT"]), (w1[:, :], io["W1T"]),
                                     (w2[:, :, :], io["W2T"]), (b1[:, :], io["b1"]),
                                     (b2f[:, :], io["b2"].partition_broadcast(P)), (ident[:, :], io["ident"]),
                                     (ident_bf[:, :], io["ident_bf"]), (mask_bf[:, :, :], io["mask_bf"])):
                        sp.dma_start(dst, src).then_inc(loaded, 16)
                    sp.wait_ge(stacks_zero, 3)
                    for par in range(2):
                        sp.dma_start(qs[ROW_POS:ROW_POS + 12, par], io["pos_q"]).then_inc(loaded, 16)
                        sp.dma_start(ks[ROW_POS:ROW_POS + 12, par], io["pos_k"]).then_inc(loaded, 16)

                def load_x(self, n, par):
                    sp.dma_start(x_sb[:, par], io["x"][n].rearrange("(c p) d -> p c d", p=P)).then_inc(x_loaded, 16)

                def stack(self, n, par, which):
                    sp.wait_ge(qk_taken, at(n, 2, which + 1))
                    dst, order = ((qs, Q_PARTS), (ks, K_PARTS))[which]
                    for slot, part in enumerate(order):
                        sp.dma_start(dst[slot * HD:(slot + 1) * HD, par],
                                     parts[:, which, part, :]).then_inc(stacked, 16)

                def pre(self, n):
                    self.load_x(0, 0)
                    sp.wait_ge(loaded, 16 * 13)
                    self.stack(0, 0, 0)
                    self.stack(0, 0, 1)

                def slot(self, n, par, front, back, nxt):
                    if nxt:
                        if back:
                            sp.wait_ge(ffn2_taken, at(n, 1, 0))
                        self.load_x(n + 1, 1 - par)
                    for g in range(G):
                        for kind, i in unit_steps(g, front, back, nxt):
                            if kind == "mrow":
                                m, k = misc_index(kind, i, n, g)
                                mpar = par if g else 1 - par
                                sp.wait_ge(mrow_taken, at(m, G, k + 1))
                                for r in range(2):
                                    sp.dma_start(qs[ROW_MAX + r:ROW_MAX + r + 1, mpar, k * HG:(k + 1) * HG, :],
                                                 mrow[:, k % 2, r, :]).then_inc(mrow_in, 16)
                            if kind == "qk":
                                if i == 0 and back:
                                    sp.wait_ge(scored, at(n, G * TILES, 0))
                                self.stack(n + 1, 1 - par, i)
                            if kind == "out":
                                sp.wait_ge(out_taken, at(n - 1, 1, 1))
                                sp.dma_start(x1_dram[n - 1].rearrange("(c p) d -> p c d", p=P),
                                             x1[:, :, :]).then_inc(stored, 16)

                def after(self):
                    sp.wait_ge(stored, 16 * NB)
            drive(Sync(), sp)

        @block.gpsimd
        def _(pool):
            class Pool:
                def before(self):
                    nc.gpsimd.memset(v_aug[:, :, :, :, :], 0.0).then_inc(set_up, 1)
                    nc.gpsimd.memset(minus_half[:, :], -0.5).then_inc(set_up, 1)
                    nc.gpsimd.memset(ones[:, :], 1.0).then_inc(set_up, 1)
                    pool.wait_ge(set_up, 3)
                    nc.gpsimd.memset(v_aug[:, :, :, :, HD:HD + 1], 1.0).then_inc(set_up, 1)

                def rstd(self, n):
                    pool.wait_ge(ln_eps, at(n, 1, 1))
                    nc.gpsimd.tensor_tensor(rstd[:, :], rstd[:, :], minus_half[:, :], ALU.pow).then_inc(ln_rstd, 1)

                def pre(self, n):
                    self.rstd(0)

                def slot(self, n, par, front, back, nxt):
                    for g in range(G):
                        m, k = exp_unit(n, g)
                        for kind, i in unit_steps(g, front, back, nxt):
                            if kind == "ln":
                                self.rstd(n + 1)
                            if kind == "tile":
                                pool.wait_ge(exped, at(m, G * TILES, k * TILES + i + 1))
                                t = p_sb[:, k % 2, i, :]
                                if i == HG:
                                    blocks = [(t.rearrange("p (a q) -> p a q", a=4)[:, :, 0:P], -1)]
                                else:
                                    blocks = [(t.rearrange("p (a q) -> p a q", a=2)[:, :, 0:P], 1), (t[:, 2 * S - P:2 * S], -1)]
                                pool.nop(nofuse=True)
                                for blk, way in blocks:
                                    pattern = [[way, P]] if len(blk.shape) == 2 else [[0, blk.shape[1]], [way, P]]
                                    last = nc.gpsimd.affine_select(out=blk, in_=blk, compare_op=ALU.is_ge, fill=0.0, base=0,
                                                                   pattern=pattern, channel_multiplier=-way)
                                last.then_inc(masked, 1)

                def after(self):
                    pass
            drive(Pool(), pool)

        @block.scalar
        def _(act):
            class Scalar:
                def before(self):
                    act.wait_ge(loaded, 16 * 13)
                    nc.scalar.activation(wtmp[:, :], w1[:, :], ACT.Abs, accum_out=gsum[:, 0:1]).then_inc(abs_done, 1)
                    act.wait_ge(abs_done, 1)
                    nc.scalar.activation(wtmp[:, :], w2[:, :, :].rearrange("p a b -> p (a b)"), ACT.Abs,
                                         accum_out=gsum[:, 1:2]).then_inc(abs_done, 1)

                def take_xT(self, n):
                    act.wait_ge(xT_put, at(n, 1, 1))
                    nc.scalar.activation(xnT[:, :], misc_ps[:, :], ACT.Copy).then_inc(xT_taken, 1)

                def pre(self, n):
                    self.take_xT(0)

                def slot(self, n, par, front, back, nxt):
                    for g in range(G):
                        m, k = exp_unit(n, g)
                        pm, pk = pv_unit(n, g)
                        for kind, i in unit_steps(g, front, back, nxt):
                            if kind == "tile":
                                idx = k * TILES + i
                                act.wait_ge(scored, at(m, G * TILES, idx + 1))
                                if i == 0 and (back or k >= 2):
                                    act.wait_ge(pv_done, at(m, G, k - 1))
                                nc.scalar.activation(p_sb[:, k % 2, i, :], tile_ps[idx % 2][:, :], ACT.Exp).then_inc(exped, 1)
                            if kind == "otr":
                                act.wait_ge(pv_done, at(pm, G, pk + 1))
                                if back or pk >= 1:
                                    act.wait_ge(otr_put, at(pm, G, pk))
                                nc.scalar.activation(o_sb[:, :], o_ps[:, :], ACT.Copy).then_inc(o_copied, 1)
                            if kind == "xT":
                                self.take_xT(n + 1)
                            if kind == "ffn1":
                                act.wait_ge(ffn1_put, at(n, NF, i + 1))
                                if i == 0 and back:
                                    act.wait_ge(ffn2_put, at(n, 1, 0))
                                nc.scalar.activation(hT[:, i, :], misc_ps[:, :], ACT.Relu,
                                                     bias=b1[:, i:i + 1]).then_inc(ffn1_taken, 1)
                            if kind == "oT":
                                act.wait_ge(oT_put, at(n - 1, 1, 1))
                                nc.scalar.activation(oT[:, :], misc_ps[:, :], ACT.Copy).then_inc(oT_taken, 1)

                def after(self):
                    pass
            drive(Scalar(), act)

        @block.vector
        def _(dve):
            class Vector:
                def __init__(self):
                    self.linked = 0

                def link(self, ins):
                    self.linked += 1
                    ins.then_inc(pre_link, 1)
                    dve.wait_ge(pre_link, self.linked)

                def before(self):
                    nc.vector.memset(qs[:, :, :, :].bitcast(FP32), 0.0).then_inc(stacks_zero, 1)
                    nc.vector.memset(ks[:, :, :, :].bitcast(FP32), 0.0).then_inc(stacks_zero, 1)
                    dve.wait_ge(stacks_zero, 2)
                    nc.vector.memset(ks[ROW_MAX:P, :, :, :], 1.0).then_inc(stacks_zero, 1)
                    dve.wait_ge(gamma_ps, 1)
                    self.link(nc.vector.tensor_scalar(gsum[:, 2:4], misc_ps[:, 0:2], 1.0 / (D * FF), EPS, ALU.mult, ALU.add))
                    self.link(nc.vector.reciprocal(gsum[:, 4:6], gsum[:, 2:4]))
                    for k, w in enumerate((w1[:, :], w2[:, :, :].rearrange("p a b -> p (a b)"))):
                        self.link(nc.vector.tensor_scalar(w, w, gsum[:, 4 + k:5 + k], None, ALU.mult))
                        self.link(nc.vector.tensor_scalar(w, w, 1.0, -1.0, ALU.min, ALU.max))
                        self.link(nc.vector.tensor_scalar(w, w, MAGIC, -MAGIC, ALU.add, ALU.add))
                    self.link(nc.vector.tensor_scalar(wqkv[:, 0:D], wqkv[:, 0:D], HD ** -0.5, None, ALU.mult))
                    nc.vector.tensor_scalar(wtmp[:, 0:1], wqkv[:, 0:1], 1.0, None, ALU.mult).then_inc(weights_ready, 1)

                def layer_norm(self, n, par):
                    dve.wait_ge(x_loaded, at(n, 16, 16))
                    for c in range(C):
                        nc.vector.bn_stats(stats[:, c, :], x_sb[:, par, c, :]).then_inc(ln_stat, 1)
                    dve.wait_ge(ln_stat, at(n, C, C))
                    dve.nop(nofuse=True)
                    for c in range(C):
                        nc.vector.bn_aggr(mv[:, c, :], stats[:, c, :]).then_inc(ln_mv, 1)
                    dve.wait_ge(ln_mv, at(n, C, C))
                    nc.vector.tensor_scalar(rstd[:, :], mv[:, :, 1], EPS, None, ALU.add).then_inc(ln_eps, 1)
                    dve.wait_ge(ln_rstd, at(n, 1, 1))
                    for c in range(C):
                        nc.vector.tensor_scalar(xn[:, c, :], x_sb[:, par, c, :], mv[:, c, 0:1], rstd[:, c:c + 1],
                                                ALU.subtract, ALU.mult).then_inc(ln_done, 1)

                def split(self, n, which):
                    high, mid, low = (parts[:, which, i, :] for i in range(3))
                    dve.wait_ge(qk_put, at(n, 2, which + 1))
                    if not isinstance(n, int) or n > 0:
                        dve.wait_ge(stacked, at(n, 16 * STACKS, 0))
                    nc.vector.tensor_copy(high, misc_ps[:, :]).then_inc(split_step, 1)
                    dve.wait_ge(split_step, at(n, 6, 3 * which + 1))
                    nc.vector.tensor_tensor(rest[:, which, :], misc_ps[:, :], high, ALU.subtract).then_inc(split_step, 1)
                    dve.wait_ge(split_step, at(n, 6, 3 * which + 2))
                    nc.vector.tensor_copy(mid, rest[:, which, :]).then_inc(split_step, 1)
                    dve.wait_ge(split_step, at(n, 6, 3 * which + 3))
                    nc.vector.tensor_tensor(low, rest[:, which, :], mid, ALU.subtract).then_inc(qk_taken, 1)

                def take_v(self, n, par):
                    dve.wait_ge(v_put, at(n, 1, 1))
                    nc.vector.tensor_copy(v_aug[:, par, :, :, 0:HD], misc_ps[:, :].rearrange("p (c h d) -> p c h d", c=C, d=HD)) \
                        .then_inc(v_taken, 1)

                def pre(self, n):
                    self.layer_norm(0, 0)
                    self.split(0, 0)
                    self.split(0, 1)
                    dve.wait_ge(set_up, 4)
                    self.take_v(0, 0)

                def slot(self, n, par, front, back, nxt):
                    for g in range(G):
                        pm, pk = pv_unit(n, g)
                        for kind, i in unit_steps(g, front, back, nxt):
                            if kind == "fill":
                                qb, heads = fill_plan()[i]
                                idx = g * FILLS + i
                                dve.wait_ge(filled, at(n, G * FILLS, idx + 1))
                                if i == 0 and (back or g >= 2):
                                    dve.wait_ge(mrow_put, at(n, G, g - 1))
                                width = P * (qb + 1)
                                src = fill_ps[idx % 2][:, 0:width * len(heads)].rearrange("p (h k) -> p h k", k=width)
                                nc.vector.tensor_reduce(mx[:, g % 2, heads[0]:heads[0] + len(heads), qb], src,
                                                        AX.X, ALU.max).then_inc(reduced, 1)
                            if kind == "mrow":
                                m, k = misc_index(kind, i, n, g)
                                dve.wait_ge(mrow_put, at(m, G, k + 1))
                                if back or k >= 2:
                                    dve.wait_ge(mrow_in, at(m, 32 * G, 32 * (k - 1)))
                                nc.vector.tensor_scalar(mrow[:, k % 2, 0, :], misc_ps[0:HG * C, 0:P], -1.0, None, ALU.mult) \
                                    .then_inc(mrow_high, 1)
                                dve.wait_ge(mrow_high, at(m, G, k + 1))
                                nc.vector.scalar_tensor_tensor(mrow[:, k % 2, 1, :], misc_ps[0:HG * C, 0:P], -1.0,
                                                               mrow[:, k % 2, 0, :], ALU.mult, ALU.subtract).then_inc(mrow_taken, 1)
                            if kind == "otr":
                                dve.wait_ge(otr_put, at(pm, G, pk + 1))
                                o = misc_ps[:, :].rearrange("p (c j e) -> p c j e", c=C, j=HG)
                                if back or pk >= 1:
                                    dve.wait_ge(otr_taken, at(pm, G, pk))
                                nc.vector.reciprocal(rden[:, :, :], o[:, :, :, HD]).then_inc(rden_done, 1)
                                dve.wait_ge(rden_done, at(pm, G, pk + 1))
                                if pk == 0 and back:
                                    dve.wait_ge(oT_put, at(pm, 1, 0))
                                nc.vector.tensor_tensor(
                                    o_tok[:, :, pk * HG * HD:(pk + 1) * HG * HD].rearrange("p c (j e) -> p c j e", j=HG),
                                    o[:, :, :, 0:HD], rden[:, :, :].unsqueeze(3).to_broadcast([P, C, HG, HD]),
                                    ALU.mult).then_inc(otr_taken, 1)
                            if kind == "ln":
                                dve.wait_ge(xT_put, at(n + 1, 1, 0))
                                self.layer_norm(n + 1, 1 - par)
                            if kind == "qk":
                                self.split(n + 1, i)
                            if kind == "v":
                                if back:
                                    dve.wait_ge(pv_done, at(n, G, 0))
                                self.take_v(n + 1, 1 - par)
                            if kind == "ffn2":
                                dve.wait_ge(ffn2_put, at(n, 1, 1))
                                nc.vector.tensor_tensor(xr[:, par], misc_ps[:, :].rearrange("p (c d) -> p c d", c=C),
                                                        x_sb[:, par], ALU.add).then_inc(ffn2_taken, 1)
                            if kind == "out":
                                dve.wait_ge(out_put, at(n - 1, 1, 1))
                                if not isinstance(n, int) or n >= 2:
                                    dve.wait_ge(stored, at(n - 1, 16, 0))
                                nc.vector.tensor_tensor(x1[:, :, :], misc_ps[:, :].rearrange("p (c d) -> p c d", c=C),
                                                        xr[:, 1 - par], ALU.add).then_inc(out_taken, 1)

                def after(self):
                    pass
            drive(Vector(), dve)

        @block.tensor
        def _(pe):
            mm = nc.tensor.matmul

            class Tensor:
                def __init__(self):
                    self.was = None

                def before(self):
                    pe.wait_ge(abs_done, 2)
                    pe.wait_ge(set_up, 3)
                    mm(misc_ps[:, 0:2], ones[:, :], gsum[:, 0:2], start=True, stop=True).then_inc(gamma_ps, 1)
                    pe.wait_ge(weights_ready, 1)

                def wait_taken(self, was):
                    if was:
                        kind, m, k = was
                        s, per = TAKEN[kind]
                        pe.wait_ge(s, at(m, per, k + 1))

                def misc(self, kind, i, m, k, par, last_par):
                    if kind == "xT":
                        pe.wait_ge(ln_done, at(m, C, C))
                        for c in range(C):
                            last = nc.tensor.transpose(misc_ps[:, c * P:(c + 1) * P], xn[:, c, :], ident[:, :])
                        last.then_inc(xT_put, 1)
                    if kind == "qk":
                        mm(misc_ps[:, :], wqkv[:, i * D:(i + 1) * D], xnT[:, :], start=True, stop=True).then_inc(qk_put, 1)
                    if kind == "v":
                        for c in range(C):
                            last = mm(misc_ps[:, c * P:(c + 1) * P], xnT[:, c * P:(c + 1) * P], wqkv[:, 2 * D:3 * D],
                                      start=True, stop=True)
                        last.then_inc(v_put, 1)
                    if kind == "ffn1":
                        mm(misc_ps[:, :], w1[:, i * P:(i + 1) * P], xnT[:, :], start=True, stop=True).then_inc(ffn1_put, 1)
                    if kind == "ffn2":
                        for c in range(C):
                            for f in range(NF):
                                mm(misc_ps[:, c * P:(c + 1) * P], hT[:, f, c * P:(c + 1) * P], w2[:, f, :],
                                   start=f == 0, stop=False)
                            last = mm(misc_ps[:, c * P:(c + 1) * P], ones[0:1, :], b2f[0:1, :], start=False, stop=True)
                        last.then_inc(ffn2_put, 1)
                    if kind == "mrow":
                        pe.wait_ge(reduced, at(m, G * FILLS, (k + 1) * FILLS))
                        nc.tensor.transpose(misc_ps[0:HG * C, 0:P], mx[:, k % 2].rearrange("p h c -> p (h c)"),
                                            ident[:, :]).then_inc(mrow_put, 1)
                    if kind == "otr":
                        pe.wait_ge(o_copied, at(m, G, k + 1))
                        for c in range(C):
                            last = nc.tensor.transpose(misc_ps[:, c * P:(c + 1) * P], o_sb[:, c * P:(c + 1) * P], ident[:, :])
                        last.then_inc(otr_put, 1)
                    if kind == "oT":
                        pe.wait_ge(otr_taken, at(m, G, G))
                        for c in range(C):
                            last = nc.tensor.transpose(misc_ps[:, c * P:(c + 1) * P], o_tok[:, c, :], ident[:, :])
                        last.then_inc(oT_put, 1)
                    if kind == "out":
                        pe.wait_ge(oT_taken, at(m, 1, 1))
                        for c in range(C):
                            last = mm(misc_ps[:, c * P:(c + 1) * P], oT[:, c * P:(c + 1) * P], wo[:, :], start=True, stop=True)
                        last.then_inc(out_put, 1)

                def pre(self, n):
                    for kind, i in (("xT", 0), ("qk", 0), ("qk", 1), ("v", 0)):
                        self.wait_taken(self.was)
                        self.misc(kind, i, 0, i, 0, 0)
                        self.was = (kind, 0, i)

                def slot(self, n, par, front, back, nxt):
                    first = True
                    for g in range(G):
                        em, ek = exp_unit(n, g)
                        pm, pk = pv_unit(n, g)
                        epar = par if g >= 2 else 1 - par
                        ppar = par if g == 3 else 1 - par
                        for kind, i in unit_steps(g, front, back, nxt):
                            if kind == "fill":
                                qb, heads = fill_plan()[i]
                                idx = g * FILLS + i
                                if idx == 0:
                                    pe.wait_ge(stacked, at(n, 16 * STACKS, 16 * STACKS))
                                if back or idx >= 2:
                                    pe.wait_ge(reduced, at(n, G * FILLS, idx - 1))
                                width = P * (qb + 1)
                                for j, h in enumerate(heads):
                                    h = g * HG + h
                                    mm(fill_ps[idx % 2][:, j * width:(j + 1) * width], qs[0:ROW_MAX, par, h, qb * P:(qb + 1) * P],
                                       ks[0:ROW_MAX, par, h, 0:width], start=True, stop=False)
                                    last = mm(fill_ps[idx % 2][:, (j + 1) * width - P:(j + 1) * width], ident_bf[:, :],
                                              mask_bf[:, qb // 2, :], start=False, stop=True)
                                last.then_inc(filled, 1)
                            elif kind == "tile":
                                idx = ek * TILES + i
                                if i == 0:
                                    pe.wait_ge(mrow_in, at(em, 32 * G, 32 * (ek + 1)))
                                if back or idx >= 2:
                                    pe.wait_ge(exped, at(em, G * TILES, idx - 1))
                                out = tile_ps[idx % 2]
                                if i < HG:
                                    jobs = [(i, 0, 0), (i, 1, S), (i, 3, 2 * S - P)]
                                else:
                                    jobs = [(j, 2, 2 * P * j) for j in range(HG)]
                                for j, kb, col in jobs:
                                    h = ek * HG + j
                                    last = mm(out[:, col:col + S - kb * P], ks[:, epar, h, kb * P:(kb + 1) * P],
                                              qs[:, epar, h, kb * P:S], start=True, stop=True)
                                last.then_inc(scored, 1)
                            elif kind == "pv":
                                if i == 0:
                                    pe.wait_ge(masked, at(pm, G * TILES, (pk + 1) * TILES))
                                    if back or pk >= 1:
                                        pe.wait_ge(o_copied, at(pm, G, pk))
                                    if pk == 0:
                                        pe.wait_ge(v_taken, at(pm, 1, 1))
                                for j in range(HG):
                                    t = HG if i == 2 else j
                                    col = {0: 0, 1: S, 2: 2 * P * j, 3: 2 * S - P}[i]
                                    last = mm(o_ps[32 * j:32 * j + 32, i * P:S], v_aug[:, ppar, i, pk * HG + j, :],
                                              p_sb[:, pk % 2, t, col:col + S - i * P], start=i == 0, stop=i == C - 1)
                                if i == C - 1:
                                    last.then_inc(pv_done, 1)
                            elif kind != "ln":
                                m, k = misc_index(kind, i, n, g)
                                if first and back:
                                    self.wait_taken(("otr", n - 1, 0))
                                    if not isinstance(n, int) or n >= 2:
                                        self.wait_taken(("out", n - 2, 0))
                                else:
                                    self.wait_taken(self.was)
                                first = False
                                self.misc(kind, i, m, k, par, 1 - par)
                                self.was = (kind, m, k)

                def after(self):
                    pass
            drive(Tensor(), pe)


def conv_kernels(nc, io, k_dram, kf, bias_y):
    ctx = ExitStack()

    def sb(name, shape, dt=FP32):
        return ctx.enter_context(nc.sbuf_tensor(name, shape, dt))

    def pb(name, shape, dt=FP32):
        return ctx.enter_context(nc.psum_tensor(name, shape, dt))

    def sem(name):
        return ctx.enter_context(nc.semaphore(name))

    LP = NL // 2
    NA, NB_ = 32, 16
    QUART = D // 2
    GR = QUART // 4
    with ctx:
        par = sb("par", [P, 5, LP, D])
        tmp = sb("tmp", [P, 12, LP, D])
        phase = sb("phase", [P, 6])
        steps = sb("steps", [P, NA])
        ang = sb("ang", [P, QUART * NA])
        turns = sb("turns", [P, QUART * NA])
        red = sb("red", [P, QUART * NA])
        ex = sb("ex", [P, QUART * NA])
        s1 = sb("s1", [P, QUART * NA])
        u_t = sb("u_t", [P, QUART * NA])
        v_t = sb("v_t", [P, QUART * NB_])
        k_out = sb("k_out", [P, NL, D // 4, NB_])
        k_hl = sb("k_hl", [P, NL, S])
        k_lh = sb("k_lh", [P, C, NL, D])
        kdft = sb("kdft", [P, C, 9 * P])
        dweight = sb("dweight", [P, 9])
        d_bc = sb("d_bc", [P, NL, D])
        w_bc = sb("w_bc", [P, NL, D])
        skip = sb("skip", [P, NL])
        bias = sb("bias", [P, NL])
        prefix = sb("prefix", [P, C, S])
        ident2 = sb("ident2", [P, P])
        k_ps = [pb(f"k_ps{i}", [P, 2 * S]) for i in range(2)]
        b_ps = k_ps[0][:, 0:S]
        t_ps = pb("t_ps", [P, 2 * S])
        f_ps = [pb(f"f_ps{i}", [P, S]) for i in range(2)]

        k_loaded, t_loaded = sem("k_loaded"), sem("t_loaded")
        dve_step, act_step = sem("dve_step"), sem("act_step")
        exponents, angles, tables = sem("exponents"), sem("angles"), sem("tables")
        k_put, k_taken, k_stored = sem("k_put"), sem("k_taken"), sem("k_stored")
        b_put, b_taken = sem("b_put"), sem("b_taken")
        k_back, tr_put, tr_taken, f_put, f_taken = sem("k_back"), sem("tr_put"), sem("tr_taken"), sem("f_put"), sem("f_taken")
        block = ctx.enter_context(nc.Block())
        chunks = [(lp, q) for lp in range(LP) for q in range(2)]

        @block.sync
        def _(sp):
            for i, name in enumerate(("log_dt", "A_re_log", "A_im", "C_re", "C_im")):
                for lp in range(LP):
                    src = io[name][2 * lp:2 * lp + 2]
                    if name == "log_dt":
                        src = src.unsqueeze(1).unsqueeze(2).to_broadcast([2, 2, NM, D])
                    else:
                        src = src.unsqueeze(1).to_broadcast([2, 2, NM, D])
                    for l2 in range(2):
                        for ri in range(2):
                            at_ = l2 * 2 * NM + ri * NM
                            sp.dma_start(par[at_:at_ + NM, i, lp, :], src[l2, ri]).then_inc(k_loaded, 16)
            sp.dma_start(phase[:, :], io["phase"]).then_inc(k_loaded, 16)
            sp.dma_start(steps[:, :], io["steps"].partition_broadcast(P)).then_inc(k_loaded, 16)
            sp.dma_start(kdft[:, :, :], io["kdft"]).then_inc(t_loaded, 16)
            sp.dma_start(dweight[:, :], io["dweight"]).then_inc(t_loaded, 16)
            sp.dma_start(d_bc[:, :, :], io["D_skip"].partition_broadcast(P)).then_inc(t_loaded, 16)
            sp.dma_start(ident2[:, :], io["ident"]).then_inc(t_loaded, 16)
            sp.dma_start(w_bc[:, :, :], io["ln_w"].partition_broadcast(P)).then_inc(t_loaded, 16)
            sp.dma_start(skip[:, :], io["D_skipT"]).then_inc(t_loaded, 16)
            sp.dma_start(bias[:, :], io["ln_bT"]).then_inc(t_loaded, 16)
            sp.dma_start(prefix[:, :, :], io["prefix"]).then_inc(t_loaded, 16)
            sp.wait_ge(k_taken, len(chunks))
            for lay in range(NL):
                for i in range(4):
                    dst = k_dram[lay].rearrange("(g i) (a b) -> i a g b", i=4, b=NB_)[i]
                    sp.dma_start(dst, k_out[32 * i:32 * i + 32, lay]).then_inc(k_stored, 16)
            sp.wait_ge(k_stored, 16 * 4 * NL)
            sp.dma_start(k_hl[:, :, :], k_dram.rearrange("n h l -> h n l")).then_inc(k_back, 16)

        @block.vector
        def _(dve):
            counts = {}

            def do(ins, s=None):
                s = s or dve_step
                counts[s] = counts.get(s, 0) + 1
                ins.then_inc(s, 1)
                dve.wait_ge(s, counts[s])

            def tt(out, a, b, op, s=None):
                do(nc.vector.tensor_tensor(out, a, b, op), s)

            def ts(out, a, s0, s1_, op0, op1=ALU.bypass, s=None):
                do(nc.vector.tensor_scalar(out, a, s0, s1_, op0, op1) if s1_ is not None
                   else nc.vector.tensor_scalar(out, a, s0, None, op0), s)

            TWO_PI = 2 * math.pi
            C1 = 6.28125
            C2 = float(np.float32(TWO_PI - C1))
            C2 = math.floor(C2 * 2 ** 21) / 2 ** 21
            C3 = TWO_PI - C1 - C2
            PI = 3.1415925

            def reduce_angle(out, theta, turn, sine=None):
                ts(turn, theta, 1 / TWO_PI, 0.0 if sine is None else phase[:, sine:sine + 1], ALU.mult, ALU.add)
                ts(turn, turn, MAGIC, -MAGIC, ALU.add, ALU.add)
                do(nc.vector.scalar_tensor_tensor(out, turn, -C1, theta, ALU.mult, ALU.add))
                do(nc.vector.scalar_tensor_tensor(out, turn, -C2, out, ALU.mult, ALU.add))
                do(nc.vector.scalar_tensor_tensor(out, turn, -C3, out, ALU.mult, ALU.add))
                ts(out, out, 0.0 if sine is None else phase[:, 3 + sine:4 + sine], PI, ALU.add, ALU.min)
                ts(out, out, -PI, None, ALU.max, s=angles)

            f = lambda i: tmp[:, i].rearrange("p a b -> p (a b)")
            p_ = lambda i: par[:, i].rearrange("p a b -> p (a b)")
            DT, X, Y, TH, R, SN, SH, EM, ER, EI, T1, T2 = (f(i) for i in range(12))
            dve.wait_ge(act_step, 2)
            do(nc.vector.scalar_tensor_tensor(X, p_(1), -1.0, DT, ALU.mult, ALU.mult), exponents)
            tt(Y, p_(2), DT, ALU.mult)
            reduce_angle(R, Y, T1)
            dve.wait_ge(act_step, 5)
            ts(T1, TH, -1.0, 1.0, ALU.mult, ALU.add)
            do(nc.vector.reciprocal(T1, T1))
            do(nc.vector.scalar_tensor_tensor(EM, TH, 2.0, T1, ALU.mult, ALU.mult))
            do(nc.vector.scalar_tensor_tensor(T2, SH, -2.0, SH, ALU.mult, ALU.mult))
            ts(T1, T2, 1.0, None, ALU.add)
            tt(ER, EM, T1, ALU.mult)
            tt(ER, ER, T2, ALU.add)
            do(nc.vector.scalar_tensor_tensor(EI, EM, 1.0, SN, ALU.add, ALU.mult))
            tt(T1, p_(1), p_(1), ALU.mult)
            tt(T2, p_(2), p_(2), ALU.mult)
            tt(T1, T1, T2, ALU.add)
            do(nc.vector.reciprocal(T1, T1))
            tt(T2, ER, p_(1), ALU.mult)
            tt(R, EI, p_(2), ALU.mult)
            tt(T2, R, T2, ALU.subtract)
            tt(T2, T2, T1, ALU.mult)
            tt(R, EI, p_(1), ALU.mult)
            tt(SN, ER, p_(2), ALU.mult)
            do(nc.vector.scalar_tensor_tensor(R, R, -1.0, SN, ALU.mult, ALU.subtract))
            tt(R, R, T1, ALU.mult)
            tt(SN, p_(3), T2, ALU.mult)
            tt(SH, p_(4), R, ALU.mult)
            tt(SN, SN, SH, ALU.subtract)
            ts(SN, SN, phase[:, 2:3], 2.0, ALU.mult, ALU.mult)
            tt(ER, p_(3), R, ALU.mult)
            tt(EI, p_(4), T2, ALU.mult)
            tt(ER, ER, EI, ALU.add)
            ts(ER, ER, -2.0, None, ALU.mult)
            for ci, (lp, q) in enumerate(chunks):
                hs = slice(lp * D + q * QUART, lp * D + (q + 1) * QUART)

                for kind, width, unit in (("v", NB_, 1.0), ("u", NA, float(NB_))):
                    m = QUART * width
                    w3 = lambda t: t[:, 0:m].rearrange("p (h a) -> p h a", a=width)
                    st = steps[:, 0:width].unsqueeze(1).to_broadcast([P, QUART, width])
                    bc = lambda t: t[:, hs].unsqueeze(2).to_broadcast([P, QUART, width])
                    ts(T1[:, 0:QUART], X[:, hs], unit, None, ALU.mult)
                    ts(T2[:, 0:QUART], Y[:, hs], unit, None, ALU.mult)
                    tt(w3(ex), T1[:, 0:QUART].unsqueeze(2).to_broadcast([P, QUART, width]), st, ALU.mult, exponents)
                    tt(w3(ang), T2[:, 0:QUART].unsqueeze(2).to_broadcast([P, QUART, width]), st, ALU.mult)
                    base = 5 + ci * 5 + (0 if kind == "v" else 2)
                    reduce_angle(red[:, 0:m], ang[:, 0:m], turns[:, 0:m], 0)
                    dve.wait_ge(act_step, base + 2)
                    if kind == "v":
                        if ci > 0:
                            dve.wait_ge(k_put, 2 * ci)
                        tt(v_t[:, 0:m], ex[:, 0:m], s1[:, 0:m], ALU.mult)
                    else:
                        tt(w3(u_t), w3(s1), bc(SN), ALU.mult)
                        reduce_angle(red[:, 0:m], ang[:, 0:m], turns[:, 0:m], 1)
                        dve.wait_ge(act_step, base + 3)
                        tt(w3(s1), w3(s1), bc(ER), ALU.mult)
                        tt(u_t[:, 0:m], u_t[:, 0:m], s1[:, 0:m], ALU.add)
                        tt(u_t[:, 0:m], u_t[:, 0:m], ex[:, 0:m], ALU.mult, tables)
                for l2 in range(2):
                    dve.wait_ge(k_put, 2 * ci + l2 + 1)
                    for i in range(4):
                        src = k_ps[l2][32 * i:32 * i + 32, :].rearrange("p (g e) -> p g e", e=4 * NB_)[:, :, i * NB_:(i + 1) * NB_]
                        last = nc.vector.tensor_copy(k_out[32 * i:32 * i + 32, 2 * lp + l2, q * GR:(q + 1) * GR, :], src)
                last.then_inc(k_taken, 1)
            dve.wait_ge(t_loaded, 128)
            for lay in range(NL):
                for c3 in range(3):
                    idx = 3 * lay + c3
                    dve.wait_ge(f_put, idx + 1)
                    for j in range(3):
                        ch = 3 * c3 + j
                        src = f_ps[idx % 2][:, j * P:(j + 1) * P]
                        dst = kf[:, lay, ch, :]
                        last = nc.vector.scalar_tensor_tensor(dst, d_bc[:, lay, :], dweight[:, ch:ch + 1], src, ALU.mult, ALU.add)
                        if 1 <= ch <= 3:
                            last = nc.vector.scalar_tensor_tensor(kf[:, lay, 8 + ch, :], d_bc[:, lay, :], dweight[:, ch:ch + 1], src,
                                                                  ALU.mult, ALU.add)
                    last.then_inc(f_taken, 1)
                dve.wait_ge(f_taken, 3 * lay + 3)
                w12 = w_bc[:, lay, :].unsqueeze(1).to_broadcast([P, 12, D])
                nc.vector.tensor_tensor(kf[:, lay], kf[:, lay], w12, ALU.mult)
                dve.wait_ge(b_put, lay + 1)
                nc.vector.tensor_scalar(bias_y[:, lay, :], b_ps[:, :], skip[:, lay:lay + 1], bias[:, lay:lay + 1],
                                        ALU.add, ALU.mult).then_inc(b_taken, 1)

        @block.scalar
        def _(act):
            def do(ins):
                ins.then_inc(act_step, 1)

            f = lambda i: tmp[:, i].rearrange("p a b -> p (a b)")
            act.wait_ge(k_loaded, 16 * (5 * LP * 4 + 2))
            do(nc.scalar.activation(f(0), par[:, 0].rearrange("p a b -> p (a b)"), ACT.Exp))
            do(nc.scalar.activation(par[:, 1].rearrange("p a b -> p (a b)"), par[:, 1].rearrange("p a b -> p (a b)"), ACT.Exp))
            act.wait_ge(exponents, 1)
            do(nc.scalar.activation(f(3), f(1), ACT.Tanh, scale=0.5))
            act.wait_ge(angles, 1)
            do(nc.scalar.activation(f(5), f(4), ACT.Sin))
            do(nc.scalar.activation(f(6), f(4), ACT.Sin, scale=0.5))
            r = 1
            for ci in range(len(chunks)):
                for kind, (width, sines) in enumerate(((NB_, 1), (NA, 2))):
                    m = QUART * width
                    act.wait_ge(exponents, 2 * ci + kind + 2)
                    do(nc.scalar.activation(ex[:, 0:m], ex[:, 0:m], ACT.Exp))
                    for _ in range(sines):
                        r += 1
                        act.wait_ge(angles, r)
                        do(nc.scalar.activation(s1[:, 0:m], red[:, 0:m], ACT.Sin))
            for half in range(2):
                act.wait_ge(tr_put, half + 1)
                nc.scalar.activation(k_lh[:, :, 2 * half:2 * half + 2, :].rearrange("p c l d -> p l c d"),
                                     t_ps[:, :].rearrange("p (l c d) -> p l c d", l=2, c=C), ACT.Copy).then_inc(tr_taken, 1)

        @block.tensor
        def _(pe):
            for ci, (lp, q) in enumerate(chunks):
                pe.wait_ge(tables, ci + 1)
                if ci > 0:
                    pe.wait_ge(k_taken, ci)
                for l2 in range(2):
                    rows = slice(2 * NM * l2, 2 * NM * (l2 + 1))
                    for g in range(GR):
                        last = nc.tensor.matmul(k_ps[l2][:, g * 4 * NB_:(g + 1) * 4 * NB_],
                                                u_t[rows, g * 4 * NA:(g + 1) * 4 * NA], v_t[rows, g * 4 * NB_:(g + 1) * 4 * NB_],
                                                start=True, stop=True)
                    last.then_inc(k_put, 1)
            pe.wait_ge(k_back, 16)
            pe.wait_ge(t_loaded, 128)
            for half in range(2):
                for l2 in range(2):
                    for c in range(C):
                        last = nc.tensor.transpose(t_ps[:, (l2 * C + c) * P:(l2 * C + c + 1) * P],
                                                   k_hl[:, 2 * half + l2, c * P:(c + 1) * P], ident2[:, :])
                if half == 0:
                    last.then_inc(tr_put, 1)
                    pe.wait_ge(tr_taken, 1)
                else:
                    last.then_inc(tr_put, 1)
            pe.wait_ge(tr_taken, 2)
            for lay in range(NL):
                for c3 in range(3):
                    idx = 3 * lay + c3
                    if idx >= 2:
                        pe.wait_ge(f_taken, idx - 1)
                    for j in range(3):
                        ch = 3 * c3 + j
                        for c in range(C):
                            last = nc.tensor.matmul(f_ps[idx % 2][:, j * P:(j + 1) * P], kdft[:, c, ch * P:(ch + 1) * P],
                                                    k_lh[:, c, lay, :], start=c == 0, stop=c == C - 1)
                    last.then_inc(f_put, 1)
                if lay > 0:
                    pe.wait_ge(b_taken, lay)
                for c in range(C):
                    last = nc.tensor.matmul(b_ps[:, :], k_lh[:, c, lay, :], prefix[:, c, :], start=c == 0, stop=c == C - 1)
                last.then_inc(b_put, 1)

        @block.gpsimd
        def _(pool):
            pass


def s4d_and_experts(nc, io, x1_dram, out_dram, kf, bias_y, NG=B // 4):
    ctx = ExitStack()
    NS = 4
    HALF = S // 2

    def sb(name, shape, dt=FP32):
        return ctx.enter_context(nc.sbuf_tensor(name, shape, dt))

    def pb(name, shape, dt=FP32):
        return ctx.enter_context(nc.psum_tensor(name, shape, dt))

    def sem(name):
        return ctx.enter_context(nc.semaphore(name))

    with ctx:
        dft = sb("dft", [P, 2, 2, S])
        idft = sb("idft", [P, 2, 4, HALF])
        wout = sb("wout", [P, NL, 2 * D])
        rw = sb("rw", [P, E])
        ew = sb("ew", [P, E * D])
        rb = sb("rb", [1, E])
        ident3 = sb("ident3", [P, P])
        ones3 = sb("ones3", [P, P], BF16)
        onesf = sb("onesf", [1, P])
        bias_f = sb("bias_f", [P, NL * 2 * D + E * D])
        bias_r = sb("bias_r", [P, NL * 2 * D + E * D])
        bias3 = sb("bias3", [P, NL * 2 * D + E * D], BF16)
        mhalf = sb("mhalf", [P, C])
        rev = sb("rev", [P, C, E])
        acc = sb("acc", [P, NS, C, D])
        h = sb("h", [P, NS, C, D])
        st2 = sb("st2", [P, 2, C, 6])
        mv2 = sb("mv2", [P, 2, C, 2])
        var2 = sb("var2", [P, 2, C])
        mneg = sb("mneg", [P, 2, C])
        rs2 = sb("rs2", [P, 2, C])
        mrs = sb("mrs", [P, 2, C])
        xmT = sb("xmT", [P, 2, S])
        odd = sb("odd", [P, C, D])
        lg = sb("lg", [P, 10, C, E])
        lmx = sb("lmx", [P, 4, C])
        xh = sb("xh", [P, C, D])
        zp = sb("zp", [P, 2, 2, 2, D])
        pr = sb("pr", [P, 4, S])
        yc = sb("yc", [P, S])
        ys = sb("ys", [P, S])
        q_sb = sb("q_sb", [P, HALF])
        yT = sb("yT", [P, S])
        yb = sb("yb", [P, S])
        yg = sb("yg", [P, S])
        th = sb("th", [P, C, D])
        gt = sb("gt", [P, C, D])
        res = sb("res", [P, C, D])
        z_ps = [pb(f"z_ps{i}", [P, 2 * S]) for i in range(2)]
        y_ps = [pb(f"y_ps{i}", [P, S]) for i in range(2)]
        w_ps = pb("w_ps", [P, C, 2 * D])

        s_loaded, s_setup, s_chain = sem("s_loaded"), sem("s_setup"), sem("s_chain")
        acc_in = [sem(f"acc_in{i}") for i in range(NS)]
        m_stat, m_mv, m_eps, m_pow, m_rstd, h_ready = (sem(n) for n in ("m_stat", "m_mv", "m_eps", "m_pow", "m_rstd", "h_ready"))
        xmT_put, xmT_taken, lg_put, lg_taken = sem("xmT_put"), sem("xmT_taken"), sem("lg_put"), sem("lg_taken")
        r_step, r_tanh, ex_put, sel, summed = sem("r_step"), sem("r_tanh"), sem("ex_put"), sem("sel"), sem("summed")
        l_stat, l_mv, l_eps, l_pow, l_rstd, xh_done = (sem(n) for n in ("l_stat", "l_mv", "l_eps", "l_pow", "l_rstd", "xh_done"))
        fwd_put, prod_s, prod_c, yc_done, ys_done = sem("fwd_put"), sem("prod_s"), sem("prod_c"), sem("yc_done"), sem("ys_done")
        zp_done, inv_put, q_done, pq_done, yb_done, gelu_done = (sem(n) for n in ("zp_done", "inv_put", "q_done", "pq_done",
                                                                                  "yb_done", "gelu_done"))
        w_put, th_done, g_done, gated = sem("w_put"), sem("th_done"), sem("g_done"), sem("gated")
        res_done, out_stored = sem("res_done"), sem("out_stored")
        N_K = NS * NL

        def turns_of_group(handle, eng, grp):
            base = grp * N_K
            for k in range(-1, NS - 1):
                handle.turn(base + k, k % NS, k // NS, k, N_K)
            with eng.Fori(1, NL) as lay:
                for k in range(-1, NS - 1):
                    handle.turn(base + lay * NS + k, k % NS, lay + k // NS, None, None)
            for k in range(N_K - 1, N_K + 3):
                handle.turn(base + k, k % NS, k // NS, k, N_K)

        def live(k, back):
            return k is None or 0 <= k - back < N_K

        def stream(s, back):
            return (s - back) % NS

        def layer(lay, s, back):
            return lay + (s - back) // NS

        block = ctx.enter_context(nc.Block())

        def groups(handle, eng):
            handle.before()
            handle.group(0, True)
            if NG > 1:
                with eng.Fori(1, NG) as grp:
                    handle.group(grp, False)
            handle.after()

        @block.sync
        def _(sp):
            class Sync:
                def before(self):
                    nb = NL * 2 * D
                    for dst, src in ((dft[:, :, :, :], io["dft"]), (idft[:, :, :, :], io["idft"]), (wout[:, :, :], io["WoutT"]),
                                     (rw[:, :], io["router_w"]), (ew[:, :], io["EW"]), (rb[:, :], io["router_b"].unsqueeze(0)),
                                     (ident3[:, :], io["ident"]), (rev[:, :, :], io["rev"].partition_broadcast(P)),
                                     (bias_f[:, 0:nb], io["b_out"].partition_broadcast(P)),
                                     (bias_f[:, nb:], io["expert_b"].partition_broadcast(P))):
                        sp.dma_start(dst, src).then_inc(s_loaded, 16)

                def group(self, grp, first):
                    for s in range(NS):
                        if not first:
                            sp.wait_ge(res_done, at(grp, NS, s + 1 - NS))
                        n = grp * NS + s
                        sp.dma_start(acc[:, s, 0:2], x1_dram[n, 0:HALF].rearrange("(c p) d -> p c d", p=P)).then_inc(acc_in[s], 16)
                        sp.dma_start(acc[:, s, 2], x1_dram[n, 3 * P:4 * P]).then_inc(acc_in[s], 16)
                        sp.dma_start(acc[:, s, 3], x1_dram[n, 2 * P:3 * P]).then_inc(acc_in[s], 16)
                    for s in range(NS):
                        n = grp * NS + s
                        sp.wait_ge(res_done, at(n, 1, 1))
                        sp.dma_start(out_dram[n, 0:HALF].rearrange("(c p) d -> p c d", p=P), res[:, 0:2]).then_inc(out_stored, 16)
                        sp.dma_start(out_dram[n, 3 * P:4 * P], res[:, 2]).then_inc(out_stored, 16)
                        sp.dma_start(out_dram[n, 2 * P:3 * P], res[:, 3]).then_inc(out_stored, 16)

                def after(self):
                    sp.wait_ge(out_stored, 48 * NS * NG)
            groups(Sync(), sp)

        @block.gpsimd
        def _(pool):
            class Pool:
                def before(self):
                    nc.gpsimd.memset(mhalf[:, :], -0.5).then_inc(s_setup, 1)
                    nc.gpsimd.memset(ones3[:, :], 1.0).then_inc(s_setup, 1)
                    nc.gpsimd.memset(onesf[:, :], 1.0).then_inc(s_setup, 1)
                    pool.wait_ge(s_setup, 3)
                    pool.wait_ge(s_loaded, 16 * 10)

                def rstd(self, n, par, eps, power, done):
                    pool.wait_ge(eps, at(n, 1, 1))
                    pool.nop(nofuse=True)
                    nc.gpsimd.tensor_tensor(rs2[:, par], var2[:, par], mhalf[:, :], ALU.pow).then_inc(power, 1)
                    pool.wait_ge(power, at(n, 1, 1))
                    nc.gpsimd.tensor_tensor(mrs[:, par], mneg[:, par], rs2[:, par], ALU.mult).then_inc(done, 1)

                def group(self, grp, first):
                    for s in range(NS):
                        self.rstd(grp * NS + s, s % 2, m_eps, m_pow, m_rstd)
                    turns_of_group(self, pool, grp)

                def turn(self, n, s, lay, k, end):
                    if live(k, 1):
                        pool.wait_ge(prod_s, at(n, 1, 0))
                        if not (isinstance(n, int) and n < 2):
                            pool.wait_ge(inv_put, at(n, 1, -1))
                        nc.gpsimd.tensor_tensor(ys[:, :], pr[:, 0], pr[:, 1], ALU.add).then_inc(ys_done, 1)
                    if live(k, 2):
                        pool.wait_ge(pq_done, at(n, 1, -1))
                        if not (isinstance(n, int) and n < 3):
                            pool.wait_ge(gelu_done, at(n, 1, -2))
                        pool.nop(nofuse=True)
                        nc.gpsimd.tensor_tensor(yb[:, :], yT[:, :], bias_y[:, layer(lay, s, 2), :], ALU.add).then_inc(yb_done, 1)
                    if live(k, -1):
                        self.rstd(n + 1, stream(s, -1) % 2, l_eps, l_pow, l_rstd)

                def after(self):
                    pass
            groups(Pool(), pool)

        @block.scalar
        def _(act):
            class Scalar:
                def before(self):
                    pass

                def normalise(self, src, dst, n, par, rstd, done):
                    act.wait_ge(rstd, at(n, 1, 1))
                    for c in range(C):
                        last = nc.scalar.activation(dst[:, c, :], src[:, c, :], ACT.Identity, bias=mrs[:, par, c:c + 1],
                                                    scale=rs2[:, par, c:c + 1])
                    last.then_inc(done, 1)

                def group(self, grp, first):
                    for s in range(NS + 1):
                        n = grp * NS + s
                        if s < NS:
                            act.wait_ge(acc_in[s], at(grp, 48, 48))
                            if not first:
                                act.wait_ge(res_done, at(grp, NS, s - NS + 1))
                            self.normalise(acc[:, s], h[:, s], n, s % 2, m_rstd, h_ready)
                            act.wait_ge(xmT_put, at(n, 1, 1))
                            if not (first and s < 2):
                                act.wait_ge(ex_put, at(n, C, -C))
                            nc.scalar.activation(xmT[:, s % 2], y_ps[0][:, :], ACT.Copy).then_inc(xmT_taken, 1)
                        if s > 0:
                            act.wait_ge(lg_taken, at(n, 1, 0))
                            nc.scalar.activation(lg[:, 1], lg[:, 0], ACT.Tanh, scale=0.5).then_inc(r_tanh, 1)
                    turns_of_group(self, act, grp)

                def turn(self, n, s, lay, k, end):
                    if live(k, 2):
                        act.wait_ge(inv_put, at(n, 1, -1))
                        if not (isinstance(n, int) and n < 3):
                            act.wait_ge(pq_done, at(n, 1, -2))
                        nc.scalar.activation(q_sb[:, :], y_ps[stream(s, 2) % 2][:, HALF:S], ACT.Copy).then_inc(q_done, 1)
                        act.wait_ge(yb_done, at(n, 1, -1))
                        if not (isinstance(n, int) and n < 3):
                            act.wait_ge(w_put, at(n, 1, -2))
                        nc.scalar.activation(yg[:, :], yb[:, :], ACT.Gelu_apprx_tanh).then_inc(gelu_done, 1)
                    if live(k, -1):
                        if not (isinstance(n, int) and n < 0):
                            act.wait_ge(zp_done, at(n, 1, 1))
                        s1 = stream(s, -1)
                        self.normalise(h[:, s1], xh, n + 1, s1 % 2, l_rstd, xh_done)
                    if live(k, 2):
                        act.wait_ge(w_put, at(n, 1, -1))
                        if not (isinstance(n, int) and n < 3):
                            act.wait_ge(g_done, at(n, 1, -2))
                        nc.scalar.activation(th[:, :, :], w_ps[:, :, D:2 * D], ACT.Tanh, scale=0.5).then_inc(th_done, 1)

                def after(self):
                    pass
            groups(Scalar(), act)

        @block.vector
        def _(dve):
            class Vector:
                def before(self):
                    linked = [0]

                    def link(ins):
                        linked[0] += 1
                        ins.then_inc(s_chain, 1)
                        dve.wait_ge(s_chain, linked[0])
                    dve.wait_ge(s_loaded, 16 * 10)
                    link(nc.vector.memset(bias3[:, :], 0.0))
                    hi, mid, lo = (bias3[32 * r:32 * r + 1, :] for r in range(3))
                    scratch = bias_r[:, :].bitcast(BF16)
                    link(nc.vector.tensor_copy(scratch[:, 0:bias3.shape[1]], bias_f[:, :]))
                    link(nc.vector.tensor_copy(hi, scratch[0:1, 0:bias3.shape[1]]))
                    link(nc.vector.tensor_tensor(bias_f[:, :], bias_f[:, :], scratch[:, 0:bias3.shape[1]], ALU.subtract))
                    link(nc.vector.tensor_copy(scratch[:, 0:bias3.shape[1]], bias_f[:, :]))
                    link(nc.vector.tensor_copy(mid, scratch[32:33, 0:bias3.shape[1]]))
                    link(nc.vector.tensor_tensor(bias_f[:, :], bias_f[:, :], scratch[:, 0:bias3.shape[1]], ALU.subtract))
                    nc.vector.tensor_copy(lo, bias_f[64:65, :]).then_inc(s_setup, 1)

                def stats(self, src, n, par, stat, mv, eps):
                    for c in range(C):
                        last = nc.vector.bn_stats(st2[:, par, c, :], src[:, c, :])
                    last.then_inc(stat, 1)
                    dve.wait_ge(stat, at(n, 1, 1))
                    dve.nop(nofuse=True)
                    for c in range(C):
                        last = nc.vector.bn_aggr(mv2[:, par, c, :], st2[:, par, c, :])
                    last.then_inc(mv, 1)
                    dve.wait_ge(mv, at(n, 1, 1))
                    nc.vector.tensor_scalar(mneg[:, par], mv2[:, par, :, 0], -1.0, None, ALU.mult)
                    nc.vector.tensor_scalar(var2[:, par], mv2[:, par, :, 1], EPS, None, ALU.add).then_inc(eps, 1)

                def route(self, n):
                    step = [0]
                    STEPS = 10

                    def link(ins):
                        step[0] += 1
                        ins.then_inc(r_step, 1)
                        dve.wait_ge(r_step, at(n, STEPS, step[0]))
                    bc = lambda t: t.unsqueeze(2).to_broadcast([P, C, E])
                    L = [lg[:, i] for i in range(10)]
                    dve.wait_ge(lg_put, at(n, 1, 1))
                    link(nc.vector.tensor_reduce(lmx[:, 0], y_ps[1][:, 0:C * E].rearrange("p (c e) -> p c e", c=C), AX.X, ALU.max))
                    nc.vector.tensor_tensor(L[0], y_ps[1][:, 0:C * E].rearrange("p (c e) -> p c e", c=C), bc(lmx[:, 0]),
                                            ALU.subtract).then_inc(lg_taken, 1)
                    dve.wait_ge(lg_taken, at(n, 1, 1))
                    link(nc.vector.scalar_tensor_tensor(L[2], L[0], 0.0, rev[:, :, :], ALU.is_ge, ALU.mult))
                    link(nc.vector.tensor_reduce(lmx[:, 1], L[2], AX.X, ALU.max))
                    link(nc.vector.tensor_tensor(L[3], L[2], bc(lmx[:, 1]), ALU.is_equal))
                    dve.wait_ge(r_tanh, at(n, 1, 1))
                    link(nc.vector.tensor_scalar(L[4], L[1], -1.0, 1.0, ALU.mult, ALU.add))
                    link(nc.vector.reciprocal(L[5], L[4]))
                    link(nc.vector.scalar_tensor_tensor(L[6], L[1], 1.0, L[5], ALU.add, ALU.mult))
                    link(nc.vector.tensor_reduce(lmx[:, 2], L[6], AX.X, ALU.add))
                    link(nc.vector.reciprocal(lmx[:, 3], lmx[:, 2]))
                    link(nc.vector.tensor_tensor(L[7], L[3], bc(lmx[:, 3]), ALU.mult))

                def choose(self, n, s):
                    for c in range(C):
                        dve.wait_ge(ex_put, at(n, C, c + 1))
                        for e in range(E):
                            gate = lg[:, 7, c, e:e + 1]
                            src = z_ps[c % 2][:, e * D:(e + 1) * D]
                            if e >= 2:
                                dve.wait_ge(sel, at(n, C * E, c * E + e - 1))
                            if e == 1:
                                ins = nc.vector.tensor_scalar(odd[:, c, :], src, gate, None, ALU.mult)
                            else:
                                dst = acc[:, s, c, :] if e % 2 == 0 else odd[:, c, :]
                                ins = nc.vector.scalar_tensor_tensor(dst, src, gate, dst, ALU.mult, ALU.add)
                            ins.then_inc(sel, 1)
                    dve.wait_ge(sel, at(n, C * E, C * E))
                    nc.vector.tensor_tensor(acc[:, s], acc[:, s], odd[:, :, :], ALU.add).then_inc(summed, 1)

                def group(self, grp, first):
                    self.grp = grp
                    for s in range(NS + 2):
                        n = grp * NS + s
                        if s < NS:
                            dve.wait_ge(acc_in[s], at(grp, 48, 48))
                            if s >= 2:
                                dve.wait_ge(h_ready, at(n, 1, -1))
                            self.stats(acc[:, s], n, s % 2, m_stat, m_mv, m_eps)
                        if s >= 2:
                            self.choose(n - 2, s - 2)
                        if 1 <= s <= NS:
                            self.route(n - 1)
                    dve.wait_ge(h_ready, at(grp, NS, NS))
                    turns_of_group(self, dve, grp)

                def turn(self, n, s, lay, k, end):
                    if live(k, 1):
                        ly = layer(lay, s, 1)
                        cur = stream(s, 1) % 2
                        zc, zs = z_ps[cur][:, 0:S], z_ps[cur][:, S:2 * S]
                        a1, bb, a2 = (kf[:, ly, 4 * i:4 * i + 4, :].rearrange("p c d -> p (c d)") for i in range(3))
                        dve.wait_ge(fwd_put, at(n, 1, 0))
                        if not (isinstance(n, int) and n < 2):
                            dve.wait_ge(ys_done, at(n, 1, -1))
                            dve.wait_ge(inv_put, at(n, 1, -1))
                        nc.vector.tensor_tensor(pr[:, 0], zc, bb, ALU.mult)
                        nc.vector.tensor_tensor(pr[:, 1], zs, a2, ALU.mult).then_inc(prod_s, 1)
                        nc.vector.tensor_tensor(pr[:, 2], zc, a1, ALU.mult)
                        nc.vector.tensor_tensor(pr[:, 3], zs, bb, ALU.mult).then_inc(prod_c, 1)
                        dve.wait_ge(prod_c, at(n, 1, 0))
                        nc.vector.tensor_tensor(yc[:, :], pr[:, 2], pr[:, 3], ALU.subtract).then_inc(yc_done, 1)
                    if live(k, 2):
                        dve.wait_ge(q_done, at(n, 1, -1))
                        if not (isinstance(n, int) and n < 3):
                            dve.wait_ge(yb_done, at(n, 1, -2))
                        p_ = y_ps[stream(s, 2) % 2][:, 0:HALF]
                        nc.vector.tensor_tensor(yT[:, 0:HALF], p_, q_sb[:, :], ALU.add)
                        nc.vector.tensor_tensor(yT[:, HALF:S], p_, q_sb[:, :], ALU.subtract).then_inc(pq_done, 1)
                    if live(k, 3):
                        s3 = stream(s, 3)
                        dve.wait_ge(th_done, at(n, 1, -2))
                        nc.vector.scalar_tensor_tensor(gt[:, :, :], th[:, :, :], 1.0, w_ps[:, :, 0:D], ALU.add,
                                                       ALU.mult).then_inc(g_done, 1)
                        dve.wait_ge(g_done, at(n, 1, -2))
                        nc.vector.scalar_tensor_tensor(h[:, s3], gt[:, :, :], 0.5, h[:, s3], ALU.mult, ALU.add).then_inc(gated, 1)
                        if k is not None and k - 3 >= N_K - NS:
                            dve.wait_ge(gated, at(n, 1, -2))
                            dve.wait_ge(summed, at(self.grp, NS, NS))
                            self.finish(s3, k)
                    if live(k, -1):
                        s1 = stream(s, -1)
                        if k is None or k >= 3:
                            dve.wait_ge(gated, at(n, 1, -2))
                        if not (isinstance(n, int) and n < 1):
                            dve.wait_ge(xh_done, at(n, 1, 0))
                        self.stats(h[:, s1], n + 1, s1 % 2, l_stat, l_mv, l_eps)
                        cur = s1 % 2
                        dve.wait_ge(xh_done, at(n, 1, 2))
                        if not (isinstance(n, int) and n < 1):
                            dve.wait_ge(fwd_put, at(n, 1, 0))
                        nc.vector.tensor_tensor(zp[:, cur, 0], xh[:, 0:2], xh[:, 2:4], ALU.add)
                        nc.vector.tensor_tensor(zp[:, cur, 1], xh[:, 0:2], xh[:, 2:4], ALU.subtract).then_inc(zp_done, 1)

                def finish(self, s, k):
                    m = self.grp * NS + k - 3 - (N_K - NS)
                    if not (isinstance(m, int) and m < 1):
                        dve.wait_ge(out_stored, at(m, 48, 0))
                    nc.vector.tensor_tensor(res[:, :, :], acc[:, s], h[:, s], ALU.add).then_inc(res_done, 1)

                def after(self):
                    pass
            groups(Vector(), dve)

        @block.tensor
        def _(pe):
            mm = nc.tensor.matmul

            class Tensor:
                def before(self):
                    pe.wait_ge(s_setup, 4)
                    pe.wait_ge(s_loaded, 16 * 10)

                def route(self, n, s, grp, first):
                    pe.wait_ge(h_ready, at(n, 1, 1))
                    if not (first and s == 0):
                        pe.wait_ge(xmT_taken, at(n, 1, 0))
                    if s == 0 and not first:
                        pe.wait_ge(pq_done, at(grp, N_K, 0))
                    for c in range(C):
                        last = nc.tensor.transpose(y_ps[0][:, c * P:(c + 1) * P], h[:, s, c, :], ident3[:, :])
                    last.then_inc(xmT_put, 1)
                    pe.wait_ge(xmT_taken, at(n, 1, 1))
                    if not (first and s == 0):
                        pe.wait_ge(lg_taken, at(n, 1, 0))
                    for c in range(C):
                        mm(y_ps[1][:, c * E:(c + 1) * E], xmT[:, s % 2, c * P:(c + 1) * P], rw[:, :], start=True, stop=False)
                        last = mm(y_ps[1][:, c * E:(c + 1) * E], onesf[0:1, :], rb[0:1, :], start=False, stop=True)
                    last.then_inc(lg_put, 1)

                def experts(self, n, s, grp, first):
                    for c in range(C):
                        if c >= 2 or not (first and s == 0):
                            pe.wait_ge(sel, at(n, C * E, (c - 1) * E))
                        if s == 0 and c == 0 and not first:
                            pe.wait_ge(prod_c, at(grp, N_K, 0))
                        for j in range(2):
                            o = z_ps[c % 2][:, j * S:(j + 1) * S]
                            mm(o, xmT[:, s % 2, c * P:(c + 1) * P], ew[:, j * S:(j + 1) * S], start=True, stop=False)
                            last = mm(o, ones3[0:96, :], bias3[0:96, NL * 2 * D + j * S:NL * 2 * D + (j + 1) * S],
                                      start=False, stop=True)
                        last.then_inc(ex_put, 1)

                def group(self, grp, first):
                    self.route(grp * NS, 0, grp, first)
                    for s in range(NS):
                        if s + 1 < NS:
                            self.route(grp * NS + s + 1, s + 1, grp, first)
                        self.experts(grp * NS + s, s, grp, first)
                    pe.wait_ge(sel, at(grp, NS * C * E, NS * C * E))
                    pe.wait_ge(lg_taken, at(grp, NS, NS))
                    turns_of_group(self, pe, grp)

                def turn(self, n, s, lay, k, end):
                    if live(k, 0):
                        cur = s % 2
                        pe.wait_ge(zp_done, at(n, 1, 1))
                        if not (isinstance(n, int) and n < 2):
                            pe.wait_ge(prod_c, at(n, 1, -1))
                        for col, part, f in [(0, 0, 0), (1, 0, 1), (2, 1, 0), (3, 1, 1), (4, 1, 2), (5, 1, 3), (6, 0, 2), (7, 0, 3)]:
                            for c in range(2):
                                last = mm(z_ps[cur][:, col * P:(col + 1) * P], dft[:, part, c, f * P:(f + 1) * P],
                                          zp[:, cur, part, c, :], start=c == 0, stop=c == 1)
                        last.then_inc(fwd_put, 1)
                    if live(k, 1):
                        pe.wait_ge(yc_done, at(n, 1, 0))
                        pe.wait_ge(ys_done, at(n, 1, 0))
                        if not (isinstance(n, int) and n < 3):
                            pe.wait_ge(pq_done, at(n, 1, -2))
                        for half, rows in enumerate([[(yc, 0), (yc, 1), (ys, 2), (ys, 3)], [(yc, 2), (yc, 3), (ys, 0), (ys, 1)]]):
                            for j, (src, f) in enumerate(rows):
                                last = mm(y_ps[stream(s, 1) % 2][:, half * HALF:(half + 1) * HALF], src[:, f * P:(f + 1) * P],
                                          idft[:, half, j, :], start=j == 0, stop=j == 3)
                        last.then_inc(inv_put, 1)
                    if live(k, 2):
                        ly = layer(lay, s, 2)
                        pe.wait_ge(gelu_done, at(n, 1, -1))
                        if not (isinstance(n, int) and n < 3):
                            pe.wait_ge(g_done, at(n, 1, -2))
                            pe.wait_ge(th_done, at(n, 1, -2))
                        for c in range(C):
                            mm(w_ps[:, c, :], yg[:, c * P:(c + 1) * P], wout[:, ly, :], start=True, stop=False)
                            last = mm(w_ps[:, c, :], ones3[0:96, :],
                                      bias3[0:96, 0:NL * 2 * D].rearrange("p (l o) -> p l o", l=NL)[:, ly, :], start=False, stop=True)
                        last.then_inc(w_put, 1)

                def after(self):
                    pass
            groups(Tensor(), pe)


def program(nc, io, out):
    x1_dram = nc.dram_tensor("x1_scratch", (B, S, D), FP32, kind="Internal").ap()
    k_dram = nc.dram_tensor("k_scratch", (NL, D, S), FP32, kind="Internal").ap()
    with nc.sbuf_tensor("kf", [P, NL, 12, D], FP32) as kf, nc.sbuf_tensor("bias_y", [P, NL, S], FP32) as bias_y:
        conv_kernels(nc, io, k_dram, kf, bias_y)
        attention(nc, io, x1_dram)
        s4d_and_experts(nc, io, x1_dram, out, kf, bias_y)


def kernel(**inputs):
    import numpy as _np
    import concourse.bacc as _bacc
    from concourse import mybir as _mybir
    from concourse.bass_utils import run_bass_kernel_spmd as _run

    nc = _bacc.Bacc("TRN2", target_bir_lowering=False, num_devices=1)
    g = {k: _np.asarray(v) for k, v in inputs.items()}
    arrays = dict(shape_constants())
    arrays["x"] = g["L0_attn_x"][:, TOKENS]
    wqk = g["L0_attn_W_qkv"][:2 * D].reshape(2, H, HD, D).transpose(0, 2, 1, 3).reshape(2 * D, D)
    arrays["WqkvT"] = _np.concatenate([wqk, g["L0_attn_W_qkv"][2 * D:]]).T
    arrays["WoT"] = g["L0_attn_W_o"].T
    arrays["W1T"] = g["L0_ffn_W1"].T
    arrays["W2T"] = g["L0_ffn_W2"].T.reshape(NF, P, D).transpose(1, 0, 2)
    arrays["b1"] = g["L0_ffn_b1"].reshape(NF, P).T
    arrays["b2"] = g["L0_ffn_b2"]
    arrays["ln_w"] = g["L1_attn_ln_w"]
    arrays["log_dt"] = g["L1_attn_log_dt"]
    for k in ("A_re_log", "A_im", "C_re", "C_im"):
        arrays[k] = g["L1_attn_" + k].transpose(0, 2, 1)
    arrays["D_skip"] = g["L1_attn_D_skip"]
    arrays["D_skipT"], arrays["ln_bT"] = g["L1_attn_D_skip"].T, g["L1_attn_ln_b"].T
    arrays["WoutT"] = g["L1_attn_W_out"].transpose(2, 0, 1)
    arrays["b_out"] = g["L1_attn_b_out"].reshape(-1)
    arrays["router_w"], arrays["router_b"] = g["L1_ffn_router_w"], g["L1_ffn_router_b"]
    arrays["EW"] = g["L1_ffn_expert_w"].transpose(1, 0, 2).reshape(D, E * D)
    arrays["expert_b"] = g["L1_ffn_expert_b"].reshape(-1)
    arrays = {"in_" + k: _np.ascontiguousarray(v) for k, v in arrays.items()}
    io = {k[3:]: nc.dram_tensor(k, v.shape, _mybir.dt.from_np(v.dtype), kind="ExternalInput").ap() for k, v in arrays.items()}
    out = nc.dram_tensor("out", (B, S, D), _mybir.dt.float32, kind="ExternalOutput").ap()
    program(nc, io, out)
    r = _run(nc, [arrays], core_ids=[0])
    got = r.results[0]["out"]
    back = _np.argsort(TOKENS)
    return _np.ascontiguousarray(_np.asarray(got)[:, back])
```

```python
import math
from contextlib import ExitStack

import numpy as np

import concourse.bass as bass
from concourse import mybir

FP32 = mybir.dt.float32
BF16 = mybir.dt.bfloat16
ALU = mybir.AluOpType
ACT = mybir.ActivationFunctionType
AX = mybir.AxisListType

B, S, D = 16, 512, 128
P = 128
C = S // P
H, HD = 16, 8
HG = 4
G = H // HG
FF = 4 * D
NF = FF // P
NL, NM = 4, 32
E = 8
EPS = 1e-5
BIG = -1e30
TWO_BF16_ONES = float(np.array([0x3F803F80], np.uint32).view(np.float32)[0])
MAGIC = 1.5 * 2.0 ** 23

TOKENS = np.concatenate([np.arange(P) + c * P if c < C // 2 else (c + 1) * P - 1 - np.arange(P) for c in range(C)])

Q_PARTS = (0, 0, 1, 0, 2, 1)
K_PARTS = (0, 1, 0, 2, 0, 1)
N_PROD = len(Q_PARTS)
ROW_POS = N_PROD * HD
ROW_MAX = 96
FILLS = 11
TILES = 5
STACKS = 2 * N_PROD


def bf16_parts(a):
    bf = mybir.dt.np(BF16)
    out, rest = [], np.asarray(a, np.float32)
    for _ in range(3):
        part = rest.astype(bf)
        out.append(part)
        rest = rest - part.astype(np.float32)
    return out


def shape_constants():
    bf = mybir.dt.np(BF16)
    c = {}
    c["ident"] = np.eye(P, dtype=np.float32)
    c["ident_bf"] = np.eye(P, dtype=np.float32).astype(bf)
    i = np.arange(P)
    c["mask_bf"] = np.stack([np.where(i[None, :] > i[:, None], BIG, 0.0),
                             np.where(i[None, :] < i[:, None], BIG, 0.0)], 1).astype(bf)
    start = 2.0 ** (-2.0 ** (-(math.log2(H) - 3)))
    slopes = np.asarray([start * start ** h for h in range(H)], np.float32)
    parts = bf16_parts(slopes)
    pos = TOKENS
    low, high = (pos % 256).astype(np.float32), (pos - pos % 256).astype(np.float32)
    qrows, krows = np.zeros((12, H, S), np.float32), np.zeros((12, H, S), np.float32)
    for n, s in enumerate(parts):
        s = s.astype(np.float32)[:, None]
        for m, at in enumerate((low, high)):
            qrows[2 * n + m], krows[2 * n + m] = s, -at[None, :]
            qrows[6 + 2 * n + m], krows[6 + 2 * n + m] = at[None, :], s
    c["pos_q"], c["pos_k"] = qrows.astype(bf), krows.astype(bf)
    t = np.arange(S // 2) + 0.5
    even, odd = np.arange(0, S, 2), np.arange(1, S, 2)
    sin_even = even.copy()
    sin_even[0] = S
    w = np.pi / S
    cos_e, cos_o = np.cos(w * np.outer(t, even)), np.cos(w * np.outer(t, odd))
    sin_e, sin_o = np.sin(w * np.outer(t, sin_even)), np.sin(w * np.outer(t, odd))
    fwd = np.stack([np.concatenate([cos_e, sin_o], 1), np.concatenate([cos_o, sin_e], 1)])
    c["dft"] = np.ascontiguousarray(fwd.reshape(2, 2, P, S).transpose(2, 0, 1, 3)).astype(np.float32)
    inv = fwd.transpose(0, 2, 1)
    c["idft"] = np.ascontiguousarray(inv.reshape(2, 4, P, S // 2).transpose(2, 0, 1, 3)).astype(np.float32)
    l = np.arange(S)
    freq = np.concatenate([even, odd])
    weight = np.where(freq == 0, 1.0, 2.0) / (2 * S)
    first = sin_even[:P]
    first_weight = np.where(first == S, 1.0, 2.0) / (2 * S)
    a1 = np.cos(w * np.outer(l, freq)) * weight
    bb = np.sin(w * np.outer(l, freq)) * weight
    a2 = np.cos(w * np.outer(l, first)) * first_weight
    kt = np.concatenate([a1, bb, a2], 1)
    c["kdft"] = np.ascontiguousarray(kt.reshape(C, P, 9 * P).transpose(1, 0, 2)).astype(np.float32)
    real = ((np.arange(P) // NM) % 2 == 0).astype(np.float32)
    c["phase"] = np.stack([0.25 * real, 2 * real - 1, -2 * real, -2 * (1 - real), real, 1 - real], 1).astype(np.float32)
    c["steps"] = np.arange(NM, dtype=np.float32)
    token = np.concatenate([np.arange(S // 2), S - 1 - np.arange(S // 2)])
    c["prefix"] = np.ascontiguousarray((l[:, None] <= token[None, :]).astype(np.float32).reshape(C, P, S).transpose(1, 0, 2))
    c["rev"] = np.broadcast_to(E - np.arange(E, dtype=np.float32), (C, E)).copy()
    return c


def at(n, per, k):
    return n * per + k


def attention(nc, io, x1_dram, NB=B):
    ctx = ExitStack()

    def sb(name, shape, dt=FP32):
        return ctx.enter_context(nc.sbuf_tensor(name, shape, dt))

    def pb(name, shape, dt=FP32):
        return ctx.enter_context(nc.psum_tensor(name, shape, dt))

    def sem(name):
        return ctx.enter_context(nc.semaphore(name))

    with ctx:
        wqkv = sb("wqkv", [P, 3 * D])
        wo = sb("wo", [P, D])
        w1 = sb("w1", [P, FF])
        w2 = sb("w2", [P, NF, D])
        wtmp = sb("wtmp", [P, FF])
        b1 = sb("b1", [P, NF])
        b2f = sb("b2f", [P, D])
        ident = sb("ident", [P, P])
        ident_bf = sb("ident_bf", [P, P], BF16)
        mask_bf = sb("mask_bf", [P, 2, P], BF16)
        ones = sb("ones", [P, P])
        gsum = sb("gsum", [P, 8])
        minus_half = sb("minus_half", [P, C])
        x_sb = sb("x_sb", [P, 2, C, D])
        xr = sb("xr", [P, 2, C, D])
        stats = sb("stats", [P, C, 6])
        mv = sb("mv", [P, C, 2])
        rstd = sb("rstd", [P, C])
        xn = sb("xn", [P, C, D])
        xnT = sb("xnT", [P, S])
        parts = sb("parts", [P, 2, 3, S], BF16)
        rest = sb("rest", [P, 2, S])
        qs = sb("qs", [P, 2, H, S], BF16)
        ks = sb("ks", [P, 2, H, S], BF16)
        v_aug = sb("v_aug", [P, 2, C, H, 32])
        hT = sb("hT", [P, NF, S])
        mx = sb("mx", [P, 2, HG, C])
        mrow = sb("mrow", [HG * C, 2, 2, P], BF16)
        p_sb = sb("p_sb", [P, 2, TILES, 2 * S])
        o_sb = sb("o_sb", [P, S])
        rden = sb("rden", [P, C, HG])
        o_tok = sb("o_tok", [P, C, D])
        oT = sb("oT", [P, S])
        x1 = sb("x1", [P, C, D])

        fill_ps = [pb(f"fill_ps{i}", [P, S]) for i in range(2)]
        tile_ps = [pb(f"tile_ps{i}", [P, 2 * S]) for i in range(2)]
        o_ps = pb("o_ps", [P, S])
        misc_ps = pb("misc_ps", [P, S])

        loaded = sem("loaded")
        set_up = sem("set_up")
        stacks_zero = sem("stacks_zero")
        odd_zero = sem("odd_zero")
        even_pos, odd_pos = sem("even_pos"), sem("odd_pos")
        x_loaded = sem("x_loaded")
        pre_link = sem("pre_link")
        abs_done = sem("abs_done")
        gamma_ps = sem("gamma_ps")
        weights_ready = sem("weights_ready")
        ln_stat = sem("ln_stat")
        ln_mv = sem("ln_mv")
        ln_eps = sem("ln_eps")
        ln_rstd = sem("ln_rstd")
        ln_done = sem("ln_done")
        xT_put, xT_taken = sem("xT_put"), sem("xT_taken")
        qk_put = sem("qk_put")
        qk_high, qk_rest, qk_mid, qk_split = sem("qk_high"), sem("qk_rest"), sem("qk_mid"), sem("qk_split")
        v_put, v_taken = sem("v_put"), sem("v_taken")
        ffn1_put, ffn1_taken = sem("ffn1_put"), sem("ffn1_taken")
        ffn2_put, ffn2_taken = sem("ffn2_put"), sem("ffn2_taken")
        mrow_put, mrow_high, mrow_taken = sem("mrow_put"), sem("mrow_high"), sem("mrow_taken")
        otr_put, rden_done, otr_taken = sem("otr_put"), sem("rden_done"), sem("otr_taken")
        oT_put, oT_taken = sem("oT_put"), sem("oT_taken")
        out_put, out_taken = sem("out_put"), sem("out_taken")
        stacked = sem("stacked")
        filled, reduced = sem("filled"), sem("reduced")
        mrow_in = sem("mrow_in")
        scored, exped, masked = sem("scored"), sem("exped"), sem("masked")
        pv_done, o_copied = sem("pv_done"), sem("o_copied")
        stored = sem("stored")

        N_LOADS = 9
        LAST = NB - 1

        def fill_plan():
            plan = [(3, (h,)) for h in range(4)] + [(2, (h,)) for h in range(4)]
            plan += [(1, (0, 1)), (1, (2, 3)), (0, (0, 1, 2, 3))]
            return plan

        def unit_steps(g, front, back, nxt):
            own = g >= 2
            exp = front if own else back
            pv = front if g == 3 else back
            f = [("fill", i) for i in range(FILLS)] if front else []
            b = [("tile", t) for t in range(TILES)] if exp else []
            v = [("pv", kb) for kb in range(C)] if pv else []
            m = [[], [], [], [], []]
            if (front if g > 0 else back):
                m[0].append(("mrow", 0))
            if g == 2 and nxt:
                m[0].append(("xT", 0))
                m[1].append(("qk", 0))
                m[2] += [("rest", 0), ("qk", 1)]
                m[3] += [("mid", 0), ("rest", 1)]
            if pv:
                m[3].append(("o_copy", 0))
                m[4].append(("otr", 0))
            if g == 2 and nxt:
                m[4].append(("mid", 1))
            if g == 0 and front:
                m[1].append(("ffn1", 0)), m[2].append(("ffn1", 1))
            if g == 1 and front:
                m[1].append(("ffn1", 2)), m[2].append(("ffn1", 3)), m[3].append(("ffn2", 0))
            if g == 1 and nxt:
                m[2].append(("ln", 0)), m[4].append(("lnx", 0))
            if g == 3:
                if nxt:
                    m[1].append(("v", 0))
                if back:
                    m[2].append(("oT", 0)), m[3].append(("out", 0))
            steps = []
            for i in range(5):
                steps += f[2 * i:2 * i + 1] + b[i:i + 1] + f[2 * i + 1:2 * i + 2] + v[i:i + 1] + m[i]
            return steps + f[10:]

        TAKEN = {"mrow": (mrow_taken, G), "otr": (otr_taken, G), "ffn1": (ffn1_taken, NF), "ffn2": (ffn2_taken, 1),
                 "xT": (xT_taken, 1), "qk": (qk_rest, 2), "v": (v_taken, 1), "oT": (oT_taken, 1), "out": (out_taken, 1)}

        def misc_index(kind, i, n, g):
            if kind == "mrow":
                return (n, g - 1) if g else (n - 1, G - 1)
            if kind == "otr":
                return (n, 0) if g == 3 else (n - 1, g + 1)
            if kind in ("xT", "v", "qk"):
                return n + 1, i
            if kind in ("oT", "out"):
                return n - 1, i
            return n, i

        def exp_unit(n, g):
            return (n, g - 2) if g >= 2 else (n - 1, g + 2)

        def pv_unit(n, g):
            return (n, 0) if g == 3 else (n - 1, g + 1)

        def drive(handle, eng):
            handle.before()
            handle.pre(0)
            handle.slot(0, 0, True, False, True)
            handle.slot(1, 1, True, True, True)
            with eng.Fori(1, (NB - 2) // 2) as j:
                handle.slot(j * 2, 0, True, True, True)
                handle.slot(j * 2 + 1, 1, True, True, True)
            handle.slot(LAST - 1, 0, True, True, True)
            handle.slot(LAST, 1, True, True, False)
            handle.slot(NB, NB % 2, False, True, False)
            handle.after()

        block = ctx.enter_context(nc.Block())

        @block.sync
        def _(sp):
            class Sync:
                def before(self):
                    self.load_x(0, 0)
                    for dst, src in ((wqkv[:, :], io["WqkvT"]), (wo[:, :], io["WoT"]), (w1[:, :], io["W1T"]),
                                     (w2[:, :, :], io["W2T"]), (b1[:, :], io["b1"]),
                                     (b2f[:, :], io["b2"].partition_broadcast(P)), (ident[:, :], io["ident"]),
                                     (ident_bf[:, :], io["ident_bf"]), (mask_bf[:, :, :], io["mask_bf"])):
                        sp.dma_start(dst, src).then_inc(loaded, 16)
                    sp.wait_ge(stacks_zero, 3)
                    sp.dma_start(qs[ROW_POS:ROW_POS + 12, 0], io["pos_q"]).then_inc(even_pos, 16)
                    sp.dma_start(ks[ROW_POS:ROW_POS + 12, 0], io["pos_k"]).then_inc(even_pos, 16)

                def load_x(self, n, par):
                    sp.dma_start(x_sb[:, par], io["x"][n].rearrange("(c p) d -> p c d", p=P)).then_inc(x_loaded, 16)

                def stack(self, n, par, which):
                    sp.wait_ge(qk_split, at(n, 2, which + 1))
                    dst, order = ((qs, Q_PARTS), (ks, K_PARTS))[which]
                    for slot, part in enumerate(order):
                        sp.dma_start(dst[slot * HD:(slot + 1) * HD, par],
                                     parts[:, which, part, :]).then_inc(stacked, 16)

                def pre(self, n):
                    self.stack(0, 0, 0)
                    self.stack(0, 0, 1)
                    sp.wait_ge(odd_zero, 3)
                    sp.dma_start(qs[ROW_POS:ROW_POS + 12, 1], io["pos_q"]).then_inc(odd_pos, 16)
                    sp.dma_start(ks[ROW_POS:ROW_POS + 12, 1], io["pos_k"]).then_inc(odd_pos, 16)

                def slot(self, n, par, front, back, nxt):
                    if nxt:
                        if back:
                            sp.wait_ge(ffn2_taken, at(n, 1, 0))
                        self.load_x(n + 1, 1 - par)
                    for g in range(G):
                        for kind, i in unit_steps(g, front, back, nxt):
                            if kind == "mrow":
                                m, k = misc_index(kind, i, n, g)
                                mpar = par if g else 1 - par
                                sp.wait_ge(mrow_taken, at(m, G, k + 1))
                                for r in range(2):
                                    sp.dma_start(qs[ROW_MAX + r:ROW_MAX + r + 1, mpar, k * HG:(k + 1) * HG, :],
                                                 mrow[:, k % 2, r, :]).then_inc(mrow_in, 16)
                            if kind == "mid":
                                if i == 0 and back:
                                    sp.wait_ge(scored, at(n, G * TILES, 0))
                                self.stack(n + 1, 1 - par, i)
                            if kind == "out":
                                sp.wait_ge(out_taken, at(n - 1, 1, 1))
                                sp.dma_start(x1_dram[n - 1].rearrange("(c p) d -> p c d", p=P),
                                             x1[:, :, :]).then_inc(stored, 16)

                def after(self):
                    sp.wait_ge(stored, 16 * NB)
            drive(Sync(), sp)

        @block.gpsimd
        def _(pool):
            class Pool:
                def before(self):
                    nc.gpsimd.memset(v_aug[:, :, :, :, :], 0.0).then_inc(set_up, 1)
                    nc.gpsimd.memset(minus_half[:, :], -0.5).then_inc(set_up, 1)
                    nc.gpsimd.memset(ones[:, :], 1.0).then_inc(set_up, 1)
                    pool.wait_ge(set_up, 3)
                    nc.gpsimd.memset(v_aug[:, :, :, :, HD:HD + 1], 1.0).then_inc(set_up, 1)

                def low(self, n, which):
                    pool.wait_ge(qk_mid, at(n, 2, which + 1))
                    nc.gpsimd.tensor_tensor(parts[:, which, 2, :], rest[:, which, :], parts[:, which, 1, :],
                                            ALU.subtract).then_inc(qk_split, 1)

                def rstd(self, n):
                    pool.wait_ge(ln_eps, at(n, 1, 1))
                    nc.gpsimd.tensor_tensor(rstd[:, :], rstd[:, :], minus_half[:, :], ALU.pow).then_inc(ln_rstd, 1)

                def pre(self, n):
                    self.rstd(0)
                    self.low(0, 0)
                    self.low(0, 1)
                    nc.gpsimd.memset(qs[:, 1].bitcast(FP32), 0.0).then_inc(odd_zero, 1)
                    nc.gpsimd.memset(ks[0:ROW_MAX, 1].bitcast(FP32), 0.0).then_inc(odd_zero, 1)
                    pool.wait_ge(odd_zero, 2)
                    nc.gpsimd.memset(ks[ROW_MAX:P, 1].bitcast(FP32), TWO_BF16_ONES).then_inc(odd_zero, 1)

                def slot(self, n, par, front, back, nxt):
                    for g in range(G):
                        m, k = exp_unit(n, g)
                        for kind, i in unit_steps(g, front, back, nxt):
                            if kind == "ln":
                                self.rstd(n + 1)
                            if kind == "mid":
                                self.low(n + 1, i)
                            if kind == "tile":
                                pool.wait_ge(exped, at(m, G * TILES, k * TILES + i + 1))
                                t = p_sb[:, k % 2, i, :]
                                if i == HG:
                                    blocks = [(t.rearrange("p (a q) -> p a q", a=4)[:, :, 0:P], -1)]
                                else:
                                    blocks = [(t.rearrange("p (a q) -> p a q", a=2)[:, :, 0:P], 1), (t[:, 2 * S - P:2 * S], -1)]
                                pool.nop(nofuse=True)
                                for blk, way in blocks:
                                    pattern = [[way, P]] if len(blk.shape) == 2 else [[0, blk.shape[1]], [way, P]]
                                    last = nc.gpsimd.affine_select(out=blk, in_=blk, compare_op=ALU.is_ge, fill=0.0, base=0,
                                                                   pattern=pattern, channel_multiplier=-way)
                                last.then_inc(masked, 1)

                def after(self):
                    pass
            drive(Pool(), pool)

        @block.scalar
        def _(act):
            class Scalar:
                def before(self):
                    act.wait_ge(loaded, 16 * N_LOADS)
                    nc.scalar.activation(wtmp[:, :], w1[:, :], ACT.Abs, accum_out=gsum[:, 0:1]).then_inc(abs_done, 1)
                    act.wait_ge(abs_done, 1)
                    nc.scalar.activation(wtmp[:, :], w2[:, :, :].rearrange("p a b -> p (a b)"), ACT.Abs,
                                         accum_out=gsum[:, 1:2]).then_inc(abs_done, 1)

                def take_xT(self, n):
                    act.wait_ge(xT_put, at(n, 1, 1))
                    nc.scalar.activation(xnT[:, :], misc_ps[:, :], ACT.Copy).then_inc(xT_taken, 1)

                def high(self, n, which):
                    act.wait_ge(qk_put, at(n, 2, which + 1))
                    if not isinstance(n, int) or n > 0:
                        act.wait_ge(stacked, at(n, 16 * STACKS, 0))
                    nc.scalar.activation(parts[:, which, 0, :], misc_ps[:, :], ACT.Copy).then_inc(qk_high, 1)

                def mid(self, n, which):
                    act.wait_ge(qk_rest, at(n, 2, which + 1))
                    nc.scalar.activation(parts[:, which, 1, :], rest[:, which, :], ACT.Copy).then_inc(qk_mid, 1)

                def pre(self, n):
                    self.take_xT(0)
                    for which in range(2):
                        self.high(0, which)
                        self.mid(0, which)

                def slot(self, n, par, front, back, nxt):
                    for g in range(G):
                        m, k = exp_unit(n, g)
                        pm, pk = pv_unit(n, g)
                        for kind, i in unit_steps(g, front, back, nxt):
                            if kind == "tile":
                                idx = k * TILES + i
                                act.wait_ge(scored, at(m, G * TILES, idx + 1))
                                if i == 0 and (back or k >= 2):
                                    act.wait_ge(pv_done, at(m, G, k - 1))
                                nc.scalar.activation(p_sb[:, k % 2, i, :], tile_ps[idx % 2][:, :], ACT.Exp).then_inc(exped, 1)
                            if kind == "o_copy":
                                act.wait_ge(pv_done, at(pm, G, pk + 1))
                                if back or pk >= 1:
                                    act.wait_ge(otr_put, at(pm, G, pk))
                                nc.scalar.activation(o_sb[:, :], o_ps[:, :], ACT.Copy).then_inc(o_copied, 1)
                            if kind == "xT":
                                self.take_xT(n + 1)
                            if kind == "qk":
                                self.high(n + 1, i)
                            if kind == "mid":
                                self.mid(n + 1, i)
                            if kind == "ffn1":
                                act.wait_ge(ffn1_put, at(n, NF, i + 1))
                                if i == 0 and back:
                                    act.wait_ge(ffn2_put, at(n, 1, 0))
                                nc.scalar.activation(hT[:, i, :], misc_ps[:, :], ACT.Relu,
                                                     bias=b1[:, i:i + 1]).then_inc(ffn1_taken, 1)
                            if kind == "oT":
                                act.wait_ge(oT_put, at(n - 1, 1, 1))
                                nc.scalar.activation(oT[:, :], misc_ps[:, :], ACT.Copy).then_inc(oT_taken, 1)

                def after(self):
                    pass
            drive(Scalar(), act)

        @block.vector
        def _(dve):
            class Vector:
                def __init__(self):
                    self.linked = 0

                def link(self, ins):
                    self.linked += 1
                    ins.then_inc(pre_link, 1)
                    dve.wait_ge(pre_link, self.linked)

                def before(self):
                    dve.wait_ge(set_up, 3)
                    self.layer_norm(0, 0)
                    self.apply_norm(0, 0)
                    nc.vector.memset(qs[:, 0].bitcast(FP32), 0.0).then_inc(stacks_zero, 1)
                    nc.vector.memset(ks[0:ROW_MAX, 0].bitcast(FP32), 0.0).then_inc(stacks_zero, 1)
                    nc.vector.memset(ks[ROW_MAX:P, 0].bitcast(FP32), TWO_BF16_ONES).then_inc(stacks_zero, 1)
                    dve.wait_ge(gamma_ps, 1)
                    self.link(nc.vector.tensor_scalar(gsum[:, 2:4], misc_ps[:, 0:2], 1.0 / (D * FF), EPS, ALU.mult, ALU.add))
                    self.link(nc.vector.reciprocal(gsum[:, 4:6], gsum[:, 2:4]))
                    for k, w in enumerate((w1[:, :], w2[:, :, :].rearrange("p a b -> p (a b)"))):
                        self.link(nc.vector.tensor_scalar(w, w, gsum[:, 4 + k:5 + k], None, ALU.mult))
                        self.link(nc.vector.tensor_scalar(w, w, 1.0, -1.0, ALU.min, ALU.max))
                        self.link(nc.vector.tensor_scalar(w, w, MAGIC, -MAGIC, ALU.add, ALU.add))
                    self.link(nc.vector.tensor_scalar(wqkv[:, 0:D], wqkv[:, 0:D], HD ** -0.5, None, ALU.mult))
                    nc.vector.tensor_scalar(wtmp[:, 0:1], wqkv[:, 0:1], 1.0, None, ALU.mult).then_inc(weights_ready, 1)

                def layer_norm(self, n, par):
                    dve.wait_ge(x_loaded, at(n, 16, 16))
                    for c in range(C):
                        nc.vector.bn_stats(stats[:, c, :], x_sb[:, par, c, :]).then_inc(ln_stat, 1)
                    dve.wait_ge(ln_stat, at(n, C, C))
                    dve.nop(nofuse=True)
                    for c in range(C):
                        nc.vector.bn_aggr(mv[:, c, :], stats[:, c, :]).then_inc(ln_mv, 1)
                    dve.wait_ge(ln_mv, at(n, C, C))
                    nc.vector.tensor_scalar(rstd[:, :], mv[:, :, 1], EPS, None, ALU.add).then_inc(ln_eps, 1)

                def apply_norm(self, n, par):
                    dve.wait_ge(ln_rstd, at(n, 1, 1))
                    for c in range(C):
                        nc.vector.tensor_scalar(xn[:, c, :], x_sb[:, par, c, :], mv[:, c, 0:1], rstd[:, c:c + 1],
                                                ALU.subtract, ALU.mult).then_inc(ln_done, 1)

                def rest(self, n, which):
                    dve.wait_ge(qk_high, at(n, 2, which + 1))
                    nc.vector.tensor_tensor(rest[:, which, :], misc_ps[:, :], parts[:, which, 0, :], ALU.subtract).then_inc(qk_rest, 1)

                def take_v(self, n, par):
                    dve.wait_ge(v_put, at(n, 1, 1))
                    nc.vector.tensor_copy(v_aug[:, par, :, :, 0:HD], misc_ps[:, :].rearrange("p (c h d) -> p c h d", c=C, d=HD)) \
                        .then_inc(v_taken, 1)

                def pre(self, n):
                    self.rest(0, 0)
                    self.rest(0, 1)
                    dve.wait_ge(set_up, 4)
                    self.take_v(0, 0)

                def slot(self, n, par, front, back, nxt):
                    for g in range(G):
                        pm, pk = pv_unit(n, g)
                        for kind, i in unit_steps(g, front, back, nxt):
                            if kind == "fill":
                                qb, heads = fill_plan()[i]
                                idx = g * FILLS + i
                                dve.wait_ge(filled, at(n, G * FILLS, idx + 1))
                                if i == 0 and (back or g >= 2):
                                    dve.wait_ge(mrow_put, at(n, G, g - 1))
                                width = P * (qb + 1)
                                src = fill_ps[idx % 2][:, 0:width * len(heads)].rearrange("p (h k) -> p h k", k=width)
                                nc.vector.tensor_reduce(mx[:, g % 2, heads[0]:heads[0] + len(heads), qb], src,
                                                        AX.X, ALU.max).then_inc(reduced, 1)
                            if kind == "mrow":
                                m, k = misc_index(kind, i, n, g)
                                dve.wait_ge(mrow_put, at(m, G, k + 1))
                                if back or k >= 2:
                                    dve.wait_ge(mrow_in, at(m, 32 * G, 32 * (k - 1)))
                                nc.vector.tensor_scalar(mrow[:, k % 2, 0, :], misc_ps[0:HG * C, 0:P], -1.0, None, ALU.mult) \
                                    .then_inc(mrow_high, 1)
                                dve.wait_ge(mrow_high, at(m, G, k + 1))
                                nc.vector.scalar_tensor_tensor(mrow[:, k % 2, 1, :], misc_ps[0:HG * C, 0:P], -1.0,
                                                               mrow[:, k % 2, 0, :], ALU.mult, ALU.subtract).then_inc(mrow_taken, 1)
                            if kind == "otr":
                                dve.wait_ge(otr_put, at(pm, G, pk + 1))
                                o = misc_ps[:, :].rearrange("p (c j e) -> p c j e", c=C, j=HG)
                                if back or pk >= 1:
                                    dve.wait_ge(otr_taken, at(pm, G, pk))
                                nc.vector.reciprocal(rden[:, :, :], o[:, :, :, HD]).then_inc(rden_done, 1)
                                dve.wait_ge(rden_done, at(pm, G, pk + 1))
                                if pk == 0 and back:
                                    dve.wait_ge(oT_put, at(pm, 1, 0))
                                nc.vector.tensor_tensor(
                                    o_tok[:, :, pk * HG * HD:(pk + 1) * HG * HD].rearrange("p c (j e) -> p c j e", j=HG),
                                    o[:, :, :, 0:HD], rden[:, :, :].unsqueeze(3).to_broadcast([P, C, HG, HD]),
                                    ALU.mult).then_inc(otr_taken, 1)
                            if kind == "ln":
                                self.layer_norm(n + 1, 1 - par)
                            if kind == "lnx":
                                dve.wait_ge(xT_put, at(n + 1, 1, 0))
                                self.apply_norm(n + 1, 1 - par)
                            if kind == "rest":
                                self.rest(n + 1, i)
                            if kind == "v":
                                if back:
                                    dve.wait_ge(pv_done, at(n, G, 0))
                                self.take_v(n + 1, 1 - par)
                            if kind == "ffn2":
                                dve.wait_ge(ffn2_put, at(n, 1, 1))
                                nc.vector.tensor_tensor(xr[:, par], misc_ps[:, :].rearrange("p (c d) -> p c d", c=C),
                                                        x_sb[:, par], ALU.add).then_inc(ffn2_taken, 1)
                            if kind == "out":
                                dve.wait_ge(out_put, at(n - 1, 1, 1))
                                if not isinstance(n, int) or n >= 2:
                                    dve.wait_ge(stored, at(n - 1, 16, 0))
                                nc.vector.tensor_tensor(x1[:, :, :], misc_ps[:, :].rearrange("p (c d) -> p c d", c=C),
                                                        xr[:, 1 - par], ALU.add).then_inc(out_taken, 1)

                def after(self):
                    pass
            drive(Vector(), dve)

        @block.tensor
        def _(pe):
            mm = nc.tensor.matmul

            class Tensor:
                def __init__(self):
                    self.was = None

                def before(self):
                    pe.wait_ge(loaded, 16 * N_LOADS)
                    self.misc("xT", 0, 0, 0, 0, 0)
                    pe.wait_ge(xT_taken, 1)
                    pe.wait_ge(abs_done, 2)
                    pe.wait_ge(set_up, 3)
                    mm(misc_ps[:, 0:2], ones[:, :], gsum[:, 0:2], start=True, stop=True).then_inc(gamma_ps, 1)
                    pe.wait_ge(weights_ready, 1)

                def wait_taken(self, was):
                    if was:
                        kind, m, k = was
                        s, per = TAKEN[kind]
                        pe.wait_ge(s, at(m, per, k + 1))

                def misc(self, kind, i, m, k, par, last_par):
                    if kind == "xT":
                        pe.wait_ge(ln_done, at(m, C, C))
                        for c in range(C):
                            last = nc.tensor.transpose(misc_ps[:, c * P:(c + 1) * P], xn[:, c, :], ident[:, :])
                        last.then_inc(xT_put, 1)
                    if kind == "qk":
                        mm(misc_ps[:, :], wqkv[:, i * D:(i + 1) * D], xnT[:, :], start=True, stop=True).then_inc(qk_put, 1)
                    if kind == "v":
                        for c in range(C):
                            last = mm(misc_ps[:, c * P:(c + 1) * P], xnT[:, c * P:(c + 1) * P], wqkv[:, 2 * D:3 * D],
                                      start=True, stop=True)
                        last.then_inc(v_put, 1)
                    if kind == "ffn1":
                        mm(misc_ps[:, :], w1[:, i * P:(i + 1) * P], xnT[:, :], start=True, stop=True).then_inc(ffn1_put, 1)
                    if kind == "ffn2":
                        for c in range(C):
                            for f in range(NF):
                                mm(misc_ps[:, c * P:(c + 1) * P], hT[:, f, c * P:(c + 1) * P], w2[:, f, :],
                                   start=f == 0, stop=False)
                            last = mm(misc_ps[:, c * P:(c + 1) * P], ones[0:1, :], b2f[0:1, :], start=False, stop=True)
                        last.then_inc(ffn2_put, 1)
                    if kind == "mrow":
                        pe.wait_ge(reduced, at(m, G * FILLS, (k + 1) * FILLS))
                        nc.tensor.transpose(misc_ps[0:HG * C, 0:P], mx[:, k % 2].rearrange("p h c -> p (h c)"),
                                            ident[:, :]).then_inc(mrow_put, 1)
                    if kind == "otr":
                        pe.wait_ge(o_copied, at(m, G, k + 1))
                        for c in range(C):
                            last = nc.tensor.transpose(misc_ps[:, c * P:(c + 1) * P], o_sb[:, c * P:(c + 1) * P], ident[:, :])
                        last.then_inc(otr_put, 1)
                    if kind == "oT":
                        pe.wait_ge(otr_taken, at(m, G, G))
                        for c in range(C):
                            last = nc.tensor.transpose(misc_ps[:, c * P:(c + 1) * P], o_tok[:, c, :], ident[:, :])
                        last.then_inc(oT_put, 1)
                    if kind == "out":
                        pe.wait_ge(oT_taken, at(m, 1, 1))
                        for c in range(C):
                            last = mm(misc_ps[:, c * P:(c + 1) * P], oT[:, c * P:(c + 1) * P], wo[:, :], start=True, stop=True)
                        last.then_inc(out_put, 1)

                def pre(self, n):
                    for kind, i in (("qk", 0), ("qk", 1), ("v", 0)):
                        self.wait_taken(self.was)
                        self.misc(kind, i, 0, i, 0, 0)
                        self.was = (kind, 0, i)

                def slot(self, n, par, front, back, nxt):
                    first = True
                    for g in range(G):
                        em, ek = exp_unit(n, g)
                        pm, pk = pv_unit(n, g)
                        epar = par if g >= 2 else 1 - par
                        ppar = par if g == 3 else 1 - par
                        for kind, i in unit_steps(g, front, back, nxt):
                            if kind == "fill":
                                qb, heads = fill_plan()[i]
                                idx = g * FILLS + i
                                if idx == 0:
                                    pe.wait_ge(stacked, at(n, 16 * STACKS, 16 * STACKS))
                                    if isinstance(n, int) and n < 2:
                                        pe.wait_ge((even_pos, odd_pos)[par], 32)
                                if back or idx >= 2:
                                    pe.wait_ge(reduced, at(n, G * FILLS, idx - 1))
                                width = P * (qb + 1)
                                for j, h in enumerate(heads):
                                    h = g * HG + h
                                    mm(fill_ps[idx % 2][:, j * width:(j + 1) * width], qs[0:ROW_MAX, par, h, qb * P:(qb + 1) * P],
                                       ks[0:ROW_MAX, par, h, 0:width], start=True, stop=False)
                                    last = mm(fill_ps[idx % 2][:, (j + 1) * width - P:(j + 1) * width], ident_bf[:, :],
                                              mask_bf[:, qb // 2, :], start=False, stop=True)
                                last.then_inc(filled, 1)
                            elif kind == "tile":
                                idx = ek * TILES + i
                                if i == 0:
                                    pe.wait_ge(mrow_in, at(em, 32 * G, 32 * (ek + 1)))
                                if back or idx >= 2:
                                    pe.wait_ge(exped, at(em, G * TILES, idx - 1))
                                out = tile_ps[idx % 2]
                                if i < HG:
                                    jobs = [(i, 0, 0), (i, 1, S), (i, 3, 2 * S - P)]
                                else:
                                    jobs = [(j, 2, 2 * P * j) for j in range(HG)]
                                for j, kb, col in jobs:
                                    h = ek * HG + j
                                    last = mm(out[:, col:col + S - kb * P], ks[:, epar, h, kb * P:(kb + 1) * P],
                                              qs[:, epar, h, kb * P:S], start=True, stop=True)
                                last.then_inc(scored, 1)
                            elif kind == "pv":
                                if i == 0:
                                    pe.wait_ge(masked, at(pm, G * TILES, (pk + 1) * TILES))
                                    if back or pk >= 1:
                                        pe.wait_ge(o_copied, at(pm, G, pk))
                                    if pk == 0:
                                        pe.wait_ge(v_taken, at(pm, 1, 1))
                                for j in range(HG):
                                    t = HG if i == 2 else j
                                    col = {0: 0, 1: S, 2: 2 * P * j, 3: 2 * S - P}[i]
                                    last = mm(o_ps[32 * j:32 * j + 32, i * P:S], v_aug[:, ppar, i, pk * HG + j, :],
                                              p_sb[:, pk % 2, t, col:col + S - i * P], start=i == 0, stop=i == C - 1)
                                if i == C - 1:
                                    last.then_inc(pv_done, 1)
                            elif kind in TAKEN:
                                m, k = misc_index(kind, i, n, g)
                                if first and back:
                                    self.wait_taken(("otr", n - 1, 0))
                                    if not isinstance(n, int) or n >= 2:
                                        self.wait_taken(("out", n - 2, 0))
                                else:
                                    self.wait_taken(self.was)
                                first = False
                                self.misc(kind, i, m, k, par, 1 - par)
                                self.was = (kind, m, k)

                def after(self):
                    pass
            drive(Tensor(), pe)


def conv_kernels(nc, io, k_dram, kf, bias_y):
    ctx = ExitStack()

    def sb(name, shape, dt=FP32):
        return ctx.enter_context(nc.sbuf_tensor(name, shape, dt))

    def pb(name, shape, dt=FP32):
        return ctx.enter_context(nc.psum_tensor(name, shape, dt))

    def sem(name):
        return ctx.enter_context(nc.semaphore(name))

    LP = NL // 2
    NA, NB_ = 32, 16
    QN = 4
    QW = D // QN
    GR = QW // 4
    TWO_PI = 2 * math.pi
    PI = 3.1415925
    with ctx:
        par = sb("par", [P, 5, LP, D])
        tmp = sb("tmp", [P, 13, LP, D])
        phase = sb("phase", [P, 6])
        steps = sb("steps", [P, NA])
        ex_u = sb("ex_u", [P, LP * D, NA])
        ex_v = sb("ex_v", [P, LP * D, NB_])
        ang = sb("ang", [P, QW * NA])
        near = sb("near", [P, QW * NA])
        r_u = sb("r_u", [P, 2, QW * NA])
        s_u = sb("s_u", [P, 2, QW * NA])
        r_v = sb("r_v", [P, 2, QW * NB_])
        u_t = sb("u_t", [P, 2, QW * NA])
        v_t = sb("v_t", [P, 2, QW * NB_])
        k_out = sb("k_out", [P, NL, D // 4, NB_])
        k_hl = sb("k_hl", [P, 2, S])
        k_lh = sb("k_lh", [P, C, 2, D])
        kdft = sb("kdft", [P, C, 9 * P])
        w_bc = sb("w_bc", [P, NL, D])
        skip = sb("skip", [P, NL])
        bias = sb("bias", [P, NL])
        prefix = sb("prefix", [P, C, S])
        ident2 = sb("ident2", [P, P])
        k_ps = [[pb(f"k_ps{i}{j}", [P, S]) for j in range(2)] for i in range(2)]
        t_ps = pb("t_ps", [P, 2, S])
        f_ps = [pb(f"f_ps{i}", [P, S]) for i in range(2)]

        k_loaded, t_loaded = sem("k_loaded"), sem("t_loaded")
        dve_step = sem("dve_step")
        dt_done, x_ready, act_small = sem("dt_done"), sem("x_ready"), sem("act_small")
        angle_ready = sem("angle_ready")
        ex_ready = sem("ex_ready")
        coef_ready = sem("coef_ready")
        v_angles, u_angles = sem("v_angles"), sem("u_angles")
        v_sine, u_sine, half_sine, squared = sem("v_sine"), sem("u_sine"), sem("half_sine"), sem("squared")
        sine_part, v_ready, tables = sem("sine_part"), sem("v_ready"), sem("tables")
        k_put, k_taken, k_stored = sem("k_put"), sem("k_taken"), sem("k_stored")
        k_back, skip_in, tr_put, tr_taken = sem("k_back"), sem("skip_in"), sem("tr_put"), sem("tr_taken")
        f_put, f_taken, b_put, b_taken = sem("f_put"), sem("f_taken"), sem("b_put"), sem("b_taken")
        weighted = sem("weighted")
        block = ctx.enter_context(nc.Block())
        chunks = [(lp, q) for lp in range(LP) for q in range(QN)]
        LAST = len(chunks) - 1
        F_BANKS = 5

        @block.sync
        def _(sp):
            for i in range(5):
                sp.dma_start(par[:, i], io["s4d_par"][:, i]).then_inc(k_loaded, 16)
            sp.dma_start(phase[:, :], io["phase"]).then_inc(k_loaded, 16)
            sp.dma_start(steps[:, :], io["steps"].partition_broadcast(P)).then_inc(k_loaded, 16)
            sp.dma_start(ident2[:, :], io["ident"]).then_inc(t_loaded, 16)
            sp.dma_start(skip[:, :], io["D_skipT"]).then_inc(t_loaded, 16)
            sp.dma_start(bias[:, :], io["ln_bT"]).then_inc(t_loaded, 16)
            sp.dma_start(kdft[:, :, :], io["kdft"]).then_inc(t_loaded, 16)
            sp.dma_start(prefix[:, :, :], io["prefix"]).then_inc(t_loaded, 16)
            sp.dma_start(w_bc[:, :, :], io["ln_w"].partition_broadcast(P)).then_inc(t_loaded, 16)
            for lp in range(LP):
                sp.wait_ge(k_taken, (lp + 1) * QN)
                for lay in (2 * lp, 2 * lp + 1):
                    for i in range(4):
                        dst = k_dram[lay].rearrange("(g i) (a b) -> i a g b", i=4, b=NB_)[i]
                        sp.dma_start(dst, k_out[32 * i:32 * i + 32, lay]).then_inc(k_stored, 16)
                sp.wait_ge(k_stored, 16 * 8 * (lp + 1))
                if lp > 0:
                    sp.wait_ge(tr_put, lp)
                sp.dma_start(k_hl[:, :, :], k_dram[2 * lp:2 * lp + 2].rearrange("n h l -> h n l")).then_inc(k_back, 16)

        @block.vector
        def _(dve):
            counts = {}

            def do(ins, s=None):
                s = s or dve_step
                counts[s] = counts.get(s, 0) + 1
                ins.then_inc(s, 1)
                dve.wait_ge(s, counts[s])

            def tt(out, a, b, op, s=None):
                do(nc.vector.tensor_tensor(out, a, b, op), s)

            def ts(out, a, s0, s1_, op0, op1=ALU.bypass, s=None):
                do(nc.vector.tensor_scalar(out, a, s0, s1_, op0, op1) if s1_ is not None
                   else nc.vector.tensor_scalar(out, a, s0, None, op0), s)

            C1 = 6.28125
            C2 = float(np.float32(TWO_PI - C1))
            C2 = math.floor(C2 * 2 ** 21) / 2 ** 21
            C3 = TWO_PI - C1 - C2

            f = lambda i: tmp[:, i].rearrange("p a b -> p (a b)")
            p_ = lambda i: par[:, i].rearrange("p a b -> p (a b)")
            DT, X, Y, TH, R, SN, SH, EM, ER, EI, T1, T2, T3 = (f(i) for i in range(13))

            def angles(ci):
                lp, q = chunks[ci]
                hs = slice(lp * D + q * QW, lp * D + (q + 1) * QW)
                for kind, width, unit, out, done in (("v", NB_, 1.0, r_v, v_angles), ("u", NA, float(NB_), r_u, u_angles)):
                    m = QW * width
                    a, t, r = ang[:, 0:m], near[:, 0:m], out[:, ci % 2, 0:m]
                    w3 = a.rearrange("p (h a) -> p h a", a=width)
                    st = steps[:, 0:width].unsqueeze(1).to_broadcast([P, QW, width])
                    src = Y if kind == "v" else T3
                    tt(w3, src[:, hs].unsqueeze(2).to_broadcast([P, QW, width]), st, ALU.mult)
                    if kind == "v":
                        ts(a, a, phase[:, 0:1], None, ALU.add)
                        if ci >= 2:
                            dve.wait_ge(v_ready, ci - 1)
                    ts(t, a, MAGIC, None, ALU.add)
                    do(nc.vector.scalar_tensor_tensor(r, t, -MAGIC, a, ALU.add, ALU.subtract), done)

            def u_table(ci):
                lp, q = chunks[ci]
                hs = slice(lp * D + q * QW, lp * D + (q + 1) * QW)
                w3 = lambda t: t[:, ci % 2].rearrange("p (h a) -> p h a", a=NA)
                dve.wait_ge(squared, ci + 1)
                do(nc.vector.scalar_tensor_tensor(w3(r_u), w3(r_u), -0.5, EM[:, hs].unsqueeze(2).to_broadcast([P, QW, NA]),
                                                  ALU.add, ALU.mult))
                dve.wait_ge(sine_part, ci + 1)
                tt(r_u[:, ci % 2], r_u[:, ci % 2], s_u[:, ci % 2], ALU.add)
                if ci == 0:
                    dve.wait_ge(ex_ready, 2)
                if ci >= 2:
                    dve.wait_ge(k_put, 2 * (ci - 1))
                tt(w3(u_t), w3(r_u), ex_u[:, hs, :], ALU.mult, tables)

            dve.wait_ge(k_loaded, 16 * 7)
            dve.wait_ge(dt_done, 2)
            tt(Y, p_(2), DT, ALU.mult)
            do(nc.vector.scalar_tensor_tensor(X, p_(1), -1.0, DT, ALU.mult, ALU.mult), x_ready)
            ts(T1, Y, 1 / TWO_PI, None, ALU.mult)
            ts(T1, T1, MAGIC, -MAGIC, ALU.add, ALU.add)
            do(nc.vector.scalar_tensor_tensor(R, T1, -C1, Y, ALU.mult, ALU.add))
            do(nc.vector.scalar_tensor_tensor(R, T1, -C2, R, ALU.mult, ALU.add))
            do(nc.vector.scalar_tensor_tensor(R, T1, -C3, R, ALU.mult, ALU.add))
            ts(R, R, PI, -PI, ALU.min, ALU.max, s=angle_ready)
            ts(Y, R, 1 / TWO_PI, None, ALU.mult)
            ts(T3, Y, float(NB_), None, ALU.mult)
            angles(0)
            dve.wait_ge(act_small, 3)
            ts(T1, TH, -1.0, 1.0, ALU.mult, ALU.add)
            do(nc.vector.reciprocal(T1, T1))
            do(nc.vector.scalar_tensor_tensor(EM, TH, 2.0, T1, ALU.mult, ALU.mult))
            do(nc.vector.scalar_tensor_tensor(T2, SH, -2.0, SH, ALU.mult, ALU.mult))
            ts(T1, T2, 1.0, None, ALU.add)
            tt(ER, EM, T1, ALU.mult)
            tt(ER, ER, T2, ALU.add)
            do(nc.vector.scalar_tensor_tensor(EI, EM, 1.0, SN, ALU.add, ALU.mult))
            tt(T1, p_(1), p_(1), ALU.mult)
            tt(T2, p_(2), p_(2), ALU.mult)
            tt(T1, T1, T2, ALU.add)
            do(nc.vector.reciprocal(T1, T1))
            tt(T2, ER, p_(1), ALU.mult)
            tt(R, EI, p_(2), ALU.mult)
            tt(T2, R, T2, ALU.subtract)
            tt(T2, T2, T1, ALU.mult)
            tt(R, EI, p_(1), ALU.mult)
            tt(SN, ER, p_(2), ALU.mult)
            do(nc.vector.scalar_tensor_tensor(R, R, -1.0, SN, ALU.mult, ALU.subtract))
            tt(R, R, T1, ALU.mult)
            tt(SN, p_(3), T2, ALU.mult)
            tt(SH, p_(4), R, ALU.mult)
            tt(SN, SN, SH, ALU.subtract)
            ts(SN, SN, phase[:, 1:2], 2.0, ALU.mult, ALU.mult)
            tt(ER, p_(3), R, ALU.mult)
            tt(EI, p_(4), T2, ALU.mult)
            tt(ER, ER, EI, ALU.add)
            ts(ER, ER, -2.0, None, ALU.mult)
            ts(T1, ER, phase[:, 3:4], None, ALU.mult)
            do(nc.vector.scalar_tensor_tensor(EM, SN, phase[:, 2:3], T1, ALU.mult, ALU.add))
            ts(T1, ER, phase[:, 4:5], None, ALU.mult)
            do(nc.vector.scalar_tensor_tensor(TH, SN, phase[:, 5:6], T1, ALU.mult, ALU.add), coef_ready)
            for ci in range(len(chunks)):
                if ci < LAST:
                    angles(ci + 1)
                u_table(ci)
            dve.wait_ge(t_loaded, 16 * 6)
            for lay in range(NL):
                dve.wait_ge(f_taken, F_BANKS * (lay // 2 + 1))
                w12 = w_bc[:, lay, :].unsqueeze(1).to_broadcast([P, 12, D])
                nc.vector.tensor_tensor(kf[:, lay], kf[:, lay], w12, ALU.mult).then_inc(weighted, 1)

        @block.gpsimd
        def _(pool):
            pool.wait_ge(coef_ready, 1)
            for ci, (lp, q) in enumerate(chunks):
                hs = slice(lp * D + q * QW, lp * D + (q + 1) * QW)
                w3 = s_u[:, ci % 2].rearrange("p (h a) -> p h a", a=NA)
                coef = tmp[:, 3].rearrange("p a b -> p (a b)")[:, hs]
                pool.wait_ge(u_sine, ci + 1)
                nc.gpsimd.tensor_tensor(w3, w3, coef.unsqueeze(2).to_broadcast([P, QW, NA]), ALU.mult).then_inc(sine_part, 1)
                pool.wait_ge(v_sine, ci + 1)
                if ci == 0:
                    pool.wait_ge(ex_ready, 1)
                if ci >= 2:
                    pool.wait_ge(k_put, 2 * (ci - 1))
                nc.gpsimd.tensor_tensor(v_t[:, ci % 2].rearrange("p (h b) -> p h b", b=NB_),
                                        r_v[:, ci % 2].rearrange("p (h b) -> p h b", b=NB_), ex_v[:, hs, :],
                                        ALU.mult).then_inc(v_ready, 1)

        @block.scalar
        def _(act):
            f = lambda i: tmp[:, i].rearrange("p a b -> p (a b)")
            act.wait_ge(k_loaded, 16 * 7)
            nc.scalar.activation(f(0), par[:, 0].rearrange("p a b -> p (a b)"), ACT.Exp).then_inc(dt_done, 1)
            nc.scalar.activation(par[:, 1].rearrange("p a b -> p (a b)"), par[:, 1].rearrange("p a b -> p (a b)"),
                                 ACT.Exp).then_inc(dt_done, 1)
            act.wait_ge(x_ready, 1)
            nc.scalar.activation(f(3), f(1), ACT.Tanh, scale=0.5).then_inc(act_small, 1)
            act.wait_ge(angle_ready, 1)
            nc.scalar.activation(f(5), f(4), ACT.Sin).then_inc(act_small, 1)
            nc.scalar.activation(f(6), f(4), ACT.Sin, scale=0.5).then_inc(act_small, 1)
            for b in range(NB_):
                last = nc.scalar.activation(ex_v[:, :, b], f(1), ACT.Exp, scale=float(b))
            last.then_inc(ex_ready, 1)
            for a in range(NA):
                last = nc.scalar.activation(ex_u[:, :, a], f(1), ACT.Exp, scale=float(NB_ * a))
            last.then_inc(ex_ready, 1)

            def sines(ci):
                act.wait_ge(v_angles, ci + 1)
                nc.scalar.activation(r_v[:, ci % 2], r_v[:, ci % 2], ACT.Sin, scale=-2 * PI).then_inc(v_sine, 1)
                act.wait_ge(u_angles, ci + 1)
                if ci >= 2:
                    act.wait_ge(tables, ci - 1)
                nc.scalar.activation(s_u[:, ci % 2], r_u[:, ci % 2], ACT.Sin, scale=-2 * PI).then_inc(u_sine, 1)
                nc.scalar.activation(r_u[:, ci % 2], r_u[:, ci % 2], ACT.Sin, scale=PI).then_inc(half_sine, 1)
                act.wait_ge(half_sine, ci + 1)
                nc.scalar.activation(r_u[:, ci % 2], r_u[:, ci % 2], ACT.Square).then_inc(squared, 1)

            def take(ci):
                lp, q = chunks[ci]
                for l2 in range(2):
                    act.wait_ge(k_put, 2 * ci + l2 + 1)
                    for i in range(4):
                        src = k_ps[ci % 2][l2][32 * i:32 * i + 32, :].rearrange("p (g e) -> p g e", e=4 * NB_)
                        last = nc.scalar.activation(k_out[32 * i:32 * i + 32, 2 * lp + l2, q * GR:(q + 1) * GR, :],
                                                    src[:, :, i * NB_:(i + 1) * NB_], ACT.Copy)
                last.then_inc(k_taken, 1)

            def finish(lp):
                act.wait_ge(t_loaded, 16 * 6)
                act.wait_ge(k_back, 16 * (lp + 1))
                for l2 in range(2):
                    last = nc.scalar.activation(k_hl[:, l2, 0:1], k_hl[:, l2, 0:1], ACT.Identity, bias=skip[:, 2 * lp + l2:2 * lp + l2 + 1])
                last.then_inc(skip_in, 1)
                act.wait_ge(tr_put, lp + 1)
                nc.scalar.activation(k_lh[:, :, :, :].rearrange("p c l d -> p l c d"),
                                     t_ps[:, :, :].rearrange("p l (c d) -> p l c d", c=C), ACT.Copy).then_inc(tr_taken, 1)

            def take_transform(lp, banks):
                pair = slice(2 * lp, 2 * lp + 2)
                for j in banks:
                    act.wait_ge(f_put, F_BANKS * lp + j + 1)
                    n = min(2, 9 - 2 * j)
                    src = f_ps[j % 2][:, 0:n * 2 * D].rearrange("p (c l d) -> p l c d", c=n, l=2)
                    last = nc.scalar.activation(kf[:, pair, 2 * j:2 * j + n, :], src, ACT.Copy)
                    if j < 2:
                        last = nc.scalar.activation(kf[:, pair, 8 + max(1, 2 * j):10 + 2 * j, :], src[:, :, 1 - j:2, :], ACT.Copy)
                    last.then_inc(f_taken, 1)

            def take_bias(lp):
                for l2 in range(2):
                    act.wait_ge(b_put, 2 * lp + l2 + 1)
                    nc.scalar.activation(bias_y[:, 2 * lp + l2, :], t_ps[:, l2, :], ACT.Copy,
                                         scale=bias[:, 2 * lp + l2:2 * lp + l2 + 1]).then_inc(b_taken, 1)

            sines(0)
            for ci in range(1, LAST):
                sines(ci)
                take(ci - 1)
            sines(LAST)
            finish(0)
            take_transform(0, (0,))
            take(LAST - 1)
            take_transform(0, (1,))
            take(LAST)
            take_transform(0, (2, 3, 4))
            take_bias(0)
            for lp in range(1, LP):
                finish(lp)
                take_transform(lp, range(F_BANKS))
                take_bias(lp)

        @block.tensor
        def _(pe):
            def products(ci):
                pe.wait_ge(tables, ci + 1)
                pe.wait_ge(v_ready, ci + 1)
                if ci >= 2:
                    pe.wait_ge(k_taken, ci - 1)
                for l2 in range(2):
                    rows = slice(2 * NM * l2, 2 * NM * (l2 + 1))
                    for g in range(GR):
                        last = nc.tensor.matmul(k_ps[ci % 2][l2][:, g * 4 * NB_:(g + 1) * 4 * NB_],
                                                u_t[rows, ci % 2, g * 4 * NA:(g + 1) * 4 * NA],
                                                v_t[rows, ci % 2, g * 4 * NB_:(g + 1) * 4 * NB_], start=True, stop=True)
                    last.then_inc(k_put, 1)

            def transpose(lp):
                pe.wait_ge(skip_in, lp + 1)
                if lp > 0:
                    pe.wait_ge(b_taken, 2 * lp)
                for l2 in range(2):
                    for c in range(C):
                        last = nc.tensor.transpose(t_ps[:, l2, c * P:(c + 1) * P], k_hl[:, l2, c * P:(c + 1) * P], ident2[:, :])
                last.then_inc(tr_put, 1)
                pe.wait_ge(tr_taken, lp + 1)

            def transform(lp, banks):
                for j in banks:
                    idx = F_BANKS * lp + j
                    if idx >= 2:
                        pe.wait_ge(f_taken, idx - 1)
                    for i in range(min(2, 9 - 2 * j)):
                        ch = 2 * j + i
                        for c in range(C):
                            last = nc.tensor.matmul(f_ps[j % 2][:, i * 2 * D:(i + 1) * 2 * D], kdft[:, c, ch * P:(ch + 1) * P],
                                                    k_lh[:, c, :, :], start=c == 0, stop=c == C - 1)
                    last.then_inc(f_put, 1)

            def bias_sums(lp):
                for l2 in range(2):
                    for c in range(C):
                        last = nc.tensor.matmul(t_ps[:, l2, :], k_lh[:, c, l2, :], prefix[:, c, :], start=c == 0, stop=c == C - 1)
                    last.then_inc(b_put, 1)

            pe.wait_ge(t_loaded, 16 * 6)
            for ci in range(LAST - 1):
                products(ci)
            transpose(0)
            transform(0, (0,))
            products(LAST - 1)
            transform(0, (1,))
            products(LAST)
            transform(0, (2, 3, 4))
            bias_sums(0)
            for lp in range(1, LP):
                transpose(lp)
                transform(lp, range(F_BANKS))
                bias_sums(lp)


def s4d_and_experts(nc, io, x1_dram, out_dram, kf, bias_y, NG=B // 4):
    ctx = ExitStack()
    NS = 4
    HALF = S // 2

    def sb(name, shape, dt=FP32):
        return ctx.enter_context(nc.sbuf_tensor(name, shape, dt))

    def pb(name, shape, dt=FP32):
        return ctx.enter_context(nc.psum_tensor(name, shape, dt))

    def sem(name):
        return ctx.enter_context(nc.semaphore(name))

    with ctx:
        dft = sb("dft", [P, 2, 2, S])
        idft = sb("idft", [P, 2, 4, HALF])
        wout = sb("wout", [P, NL, 2 * D])
        rw = sb("rw", [P, E])
        ew = sb("ew", [P, E * D])
        rb = sb("rb", [1, E])
        ident3 = sb("ident3", [P, P])
        ones3 = sb("ones3", [P, P], BF16)
        onesf = sb("onesf", [1, P])
        NBIAS = NL * 2 * D + E * D
        bias_f = sb("bias_f", [P, NBIAS // P])
        bias_rest = sb("bias_rest", [P, 2, NBIAS // P])
        bias_parts = sb("bias_parts", [P, 3, NBIAS // P], BF16)
        bias3 = sb("bias3", [P, NBIAS], BF16)
        mhalf = sb("mhalf", [P, C])
        rev = sb("rev", [P, C, E])
        acc = sb("acc", [P, NS, C, D])
        h = sb("h", [P, NS, C, D])
        st2 = sb("st2", [P, NS, C, 6])
        mv2 = sb("mv2", [P, NS, C, 2])
        var2 = sb("var2", [P, NS, C])
        mneg = sb("mneg", [P, NS, C])
        rs2 = sb("rs2", [P, NS, C])
        mrs = sb("mrs", [P, NS, C])
        xmT = sb("xmT", [P, 2, S])
        odd = sb("odd", [P, C, D])
        lg = sb("lg", [P, 10, C, E])
        lmx = sb("lmx", [P, 4, C])
        xh = sb("xh", [P, C, D])
        zp = sb("zp", [P, 2, 2, 2, D])
        pr = sb("pr", [P, 4, S])
        yc = sb("yc", [P, S])
        ys = sb("ys", [P, S])
        q_sb = sb("q_sb", [P, HALF])
        yT = sb("yT", [P, S])
        yb = sb("yb", [P, S])
        yg = sb("yg", [P, S])
        th = sb("th", [P, C, D])
        gt = sb("gt", [P, C, D])
        res = sb("res", [P, 2, C, D])
        xin = sb("xin", [P, NS, C, D])
        gates = sb("gates", [P, 2, C, E])
        scaled_z = sb("scaled_z", [P, 2, E // 2, D])
        part = sb("part", [P, C, D])
        z_ps = [pb(f"z_ps{i}", [P, 2 * S]) for i in range(2)]
        y_ps = [pb(f"y_ps{i}", [P, S]) for i in range(2)]
        w_ps = pb("w_ps", [P, C, 2 * D])

        s_loaded, s_setup, s_chain = sem("s_loaded"), sem("s_setup"), sem("s_chain")
        bias_setup = sem("bias_setup")
        bias_loaded, bias_rows, ew_loaded, dft_loaded = sem("bias_loaded"), sem("bias_rows"), sem("ew_loaded"), sem("dft_loaded")
        acc_in = [sem(f"acc_in{i}") for i in range(NS)]
        m_stat, m_mv, m_eps, m_pow, m_rstd, h_ready = (sem(n) for n in ("m_stat", "m_mv", "m_eps", "m_pow", "m_rstd", "h_ready"))
        xmT_put, xmT_taken, lg_put, lg_taken = sem("xmT_put"), sem("xmT_taken"), sem("lg_put"), sem("lg_taken")
        r_step, r_tanh, ex_put, sel, summed = sem("r_step"), sem("r_tanh"), sem("ex_put"), sem("sel"), sem("summed")
        l_stat, l_mv, l_eps, l_pow, l_rstd, xh_done = (sem(n) for n in ("l_stat", "l_mv", "l_eps", "l_pow", "l_rstd", "xh_done"))
        fwd_put, prod_s, prod_c, yc_done, ys_done = sem("fwd_put"), sem("prod_s"), sem("prod_c"), sem("yc_done"), sem("ys_done")
        zp_done, inv_put, q_done, pq_done, yb_done, gelu_done = (sem(n) for n in ("zp_done", "inv_put", "q_done", "pq_done",
                                                                                  "yb_done", "gelu_done"))
        w_put, th_done, g_done, gated = sem("w_put"), sem("th_done"), sem("g_done"), sem("gated")
        gates_ready = sem("gates_ready")
        scaled, part_step, part_done, mixed = sem("scaled"), sem("part_step"), sem("part_done"), sem("mixed")
        res_done, out_stored = sem("res_done"), [sem(f"out_stored{i}") for i in range(2)]
        N_K = NS * NL
        E_DVE = E // 2

        def turn(handle, grp, k):
            handle.grp = grp
            handle.turn(grp * N_K + k, k % NS, k // NS, k)

        def group(handle, eng, grp, first):
            handle.start(grp, first)
            if not first:
                turn(handle, grp - 1, N_K)
            handle.step(grp, 0, first, range(C))
            if not first:
                turn(handle, grp - 1, N_K + 1)
            for s in range(1, NS):
                handle.step(grp, s, first, range(C))
            turn(handle, grp, -2)
            handle.step(grp, NS, first, range(C))
            handle.step(grp, NS + 1, first, range(C // 2))
            turn(handle, grp, -1)
            handle.step(grp, NS + 1, first, range(C // 2, C))
            for k in range(NS - 2):
                turn(handle, grp, k)
            with eng.Fori(1, NL) as lay:
                for k in range(-2, NS - 2):
                    handle.turn(grp * N_K + lay * NS + k, k % NS, lay + k // NS, None)
            for k in range(N_K - 2, N_K):
                turn(handle, grp, k)

        def live(k, back):
            return k is None or 0 <= k - back < N_K

        def stream(s, back):
            return (s - back) % NS

        def layer(lay, s, back):
            return lay + (s - back) // NS

        block = ctx.enter_context(nc.Block())

        def groups(handle, eng):
            handle.before()
            group(handle, eng, 0, True)
            if NG > 1:
                with eng.Fori(1, NG) as grp:
                    group(handle, eng, grp, False)
            for k in (N_K, N_K + 1):
                turn(handle, NG - 1, k)

        @block.sync
        def _(sp):
            class Sync:
                def before(self):
                    self.load_batch(0, 0)
                    sp.dma_start(bias_f[:, :], io["biases"]).then_inc(bias_loaded, 16)
                    for dst, src in ((ident3[:, :], io["ident"]), (rw[:, :], io["router_w"]), (rb[:, :], io["router_b"].unsqueeze(0)),
                                     (rev[:, :, :], io["rev"].partition_broadcast(P))):
                        sp.dma_start(dst, src).then_inc(s_loaded, 16)
                    sp.dma_start(ew[:, :], io["EW"]).then_inc(ew_loaded, 16)
                    for s in range(1, NS):
                        self.load_batch(s, s)
                    sp.wait_ge(bias_setup, 2)
                    for r in range(3):
                        sp.dma_start(bias3[32 * r:32 * r + 1, :], bias_parts[:, r, :]).then_inc(bias_rows, 16)
                    for dst, src in ((wout[:, :, :], io["WoutT"]), (dft[:, :, :, :], io["dft"]), (idft[:, :, :, :], io["idft"])):
                        sp.dma_start(dst, src).then_inc(dft_loaded, 16)

                def load_batch(self, n, s):
                    sp.dma_start(xin[:, s, 0:2], x1_dram[n, 0:HALF].rearrange("(c p) d -> p c d", p=P)).then_inc(acc_in[s], 16)
                    sp.dma_start(xin[:, s, 2], x1_dram[n, 3 * P:4 * P]).then_inc(acc_in[s], 16)
                    sp.dma_start(xin[:, s, 3], x1_dram[n, 2 * P:3 * P]).then_inc(acc_in[s], 16)

                def load(self, grp):
                    for s in range(NS):
                        self.load_batch(grp * NS + s, s)

                def store(self, grp):
                    for s in range(NS):
                        n = grp * NS + s
                        sp.wait_ge(res_done, at(n, 1, 1))
                        sp.dma_start(out_dram[n, 0:HALF].rearrange("(c p) d -> p c d", p=P), res[:, s % 2, 0:2]).then_inc(out_stored[s % 2], 16)
                        sp.dma_start(out_dram[n, 3 * P:4 * P], res[:, s % 2, 2]).then_inc(out_stored[s % 2], 16)
                        sp.dma_start(out_dram[n, 2 * P:3 * P], res[:, s % 2, 3]).then_inc(out_stored[s % 2], 16)
            sync = Sync()
            sync.before()
            if NG > 1:
                with sp.Fori(0, NG - 1) as grp:
                    sp.wait_ge(summed, at(grp, NS, NS))
                    sync.load(grp + 1)
                    sync.store(grp)
            sync.store(NG - 1)
            for s in range(2):
                sp.wait_ge(out_stored[s], 48 * NS * NG // 2)

        @block.gpsimd
        def _(pool):
            class Pool:
                def before(self):
                    nc.gpsimd.memset(mhalf[:, :], -0.5).then_inc(s_setup, 1)
                    nc.gpsimd.memset(ones3[:, :], 1.0).then_inc(s_setup, 1)
                    nc.gpsimd.memset(onesf[:, :], 1.0).then_inc(s_setup, 1)
                    pool.wait_ge(s_setup, 3)

                def rstd(self, n, par, eps, power, done):
                    pool.wait_ge(eps, at(n, 1, 1))
                    pool.nop(nofuse=True)
                    nc.gpsimd.tensor_tensor(rs2[:, par], var2[:, par], mhalf[:, :], ALU.pow).then_inc(power, 1)
                    pool.wait_ge(power, at(n, 1, 1))
                    nc.gpsimd.tensor_tensor(mrs[:, par], mneg[:, par], rs2[:, par], ALU.mult).then_inc(done, 1)

                def sum_scaled(self, n, s, chunks):
                    for c in chunks:
                        pool.wait_ge(scaled, at(n, C, c + 1))
                        z = scaled_z[:, c % 2]
                        nc.gpsimd.tensor_tensor(z[:, 0:2], z[:, 0:2], z[:, 2:4], ALU.add).then_inc(part_step, 1)
                        pool.wait_ge(part_step, at(n, C, c + 1))
                        nc.gpsimd.tensor_tensor(part[:, c], z[:, 0], z[:, 1], ALU.add).then_inc(part_done, 1)
                    if C - 1 in chunks:
                        pool.wait_ge(part_done, at(n, C, C))
                        pool.wait_ge(summed, at(n, 1, 1))
                        nc.gpsimd.tensor_tensor(acc[:, s], acc[:, s], part[:, :, :], ALU.add).then_inc(mixed, 1)

                def start(self, grp, first):
                    for i in (0, 1):
                        self.rstd(grp * NS + i, i, m_eps, m_pow, m_rstd)

                def step(self, grp, s, first, chunks):
                    if s == 1:
                        for i in (2, 3):
                            self.rstd(grp * NS + i, i, m_eps, m_pow, m_rstd)
                    if s >= 2:
                        self.sum_scaled(grp * NS + s - 2, s - 2, chunks)

                def turn(self, n, s, lay, k):
                    if live(k, 2):
                        pool.wait_ge(pq_done, at(n, 1, -1))
                        if not (isinstance(n, int) and n < 3):
                            pool.wait_ge(gelu_done, at(n, 1, -2))
                        pool.nop(nofuse=True)
                        nc.gpsimd.tensor_tensor(yb[:, :], yT[:, :], bias_y[:, layer(lay, s, 2), :], ALU.add).then_inc(yb_done, 1)
                    if live(k, 1):
                        pool.wait_ge(prod_s, at(n, 1, 0))
                        if not (isinstance(n, int) and n < 2):
                            pool.wait_ge(inv_put, at(n, 1, -1))
                        nc.gpsimd.tensor_tensor(ys[:, :], pr[:, 0], pr[:, 1], ALU.add).then_inc(ys_done, 1)
                    if live(k, -2):
                        self.rstd(n + 2, stream(s, -2), l_eps, l_pow, l_rstd)

            groups(Pool(), pool)

        @block.scalar
        def _(act):
            class Scalar:
                def before(self):
                    pass

                def normalise(self, src, dst, n, par, rstd, done):
                    act.wait_ge(rstd, at(n, 1, 1))
                    for c in range(C):
                        last = nc.scalar.activation(dst[:, c, :], src[:, c, :], ACT.Identity, bias=mrs[:, par, c:c + 1],
                                                    scale=rs2[:, par, c:c + 1])
                    last.then_inc(done, 1)

                def scale(self, n, par, first, chunks):
                    for c in chunks:
                        act.wait_ge(gates_ready, at(n, 1, 1))
                        act.wait_ge(ex_put, at(n, C, c + 1))
                        if not (first and c < 2):
                            act.wait_ge(part_done, at(n, C, c - 1))
                        for e in range(E_DVE, E):
                            last = nc.scalar.activation(scaled_z[:, c % 2, e - E_DVE], z_ps[c % 2][:, e * D:(e + 1) * D], ACT.Copy,
                                                        scale=gates[:, par, c, e:e + 1])
                        last.then_inc(scaled, 1)

                def normalised(self, grp, s, first):
                    act.wait_ge(acc_in[s], at(grp, 48, 48))
                    if not first:
                        act.wait_ge(res_done, at(grp, NS, s - NS + 1))
                    self.normalise(xin[:, s], h[:, s], grp * NS + s, s, m_rstd, h_ready)

                def start(self, grp, first):
                    pass

                def step(self, grp, s, first, chunks):
                    n = grp * NS + s
                    if s == 0:
                        self.normalised(grp, 0, first)
                    if s >= 2:
                        self.scale(n - 2, s % 2, first and s == 2, chunks)
                    if 1 <= s <= NS:
                        act.wait_ge(lg_taken, at(n, 1, 0))
                        nc.scalar.activation(lg[:, 1], lg[:, 0], ACT.Tanh, scale=0.5).then_inc(r_tanh, 1)
                    if s < NS:
                        act.wait_ge(xmT_put, at(n, 1, 1))
                        if not (first and s < 2):
                            act.wait_ge(ex_put, at(n, C, -C))
                        nc.scalar.activation(xmT[:, s % 2], y_ps[0][:, :], ACT.Copy).then_inc(xmT_taken, 1)
                    if s == 0:
                        self.normalised(grp, 1, first)
                    if s == 1:
                        self.normalised(grp, 2, first)
                        self.normalised(grp, 3, first)

                def turn(self, n, s, lay, k):
                    if live(k, 2):
                        act.wait_ge(inv_put, at(n, 1, -1))
                        if not (isinstance(n, int) and n < 3):
                            act.wait_ge(pq_done, at(n, 1, -2))
                        nc.scalar.activation(q_sb[:, :], y_ps[stream(s, 2) % 2][:, HALF:S], ACT.Copy).then_inc(q_done, 1)
                        act.wait_ge(yb_done, at(n, 1, -1))
                        if not (isinstance(n, int) and n < 3):
                            act.wait_ge(w_put, at(n, 1, -2))
                        nc.scalar.activation(yg[:, :], yb[:, :], ACT.Gelu_apprx_tanh).then_inc(gelu_done, 1)
                    if live(k, -1):
                        if not (isinstance(n, int) and n < 0):
                            act.wait_ge(zp_done, at(n, 1, 1))
                        s1 = stream(s, -1)
                        self.normalise(h[:, s1], xh, n + 1, s1, l_rstd, xh_done)
                    if live(k, 2):
                        act.wait_ge(w_put, at(n, 1, -1))
                        if not (isinstance(n, int) and n < 3):
                            act.wait_ge(g_done, at(n, 1, -2))
                        nc.scalar.activation(th[:, :, :], w_ps[:, :, D:2 * D], ACT.Tanh, scale=0.5).then_inc(th_done, 1)

            groups(Scalar(), act)

        @block.vector
        def _(dve):
            class Vector:
                def before(self):
                    linked = [0]

                    def link(ins):
                        linked[0] += 1
                        ins.then_inc(s_chain, 1)
                        dve.wait_ge(s_chain, linked[0])
                    nc.vector.memset(bias3[:, :].bitcast(FP32), 0.0).then_inc(bias_setup, 1)
                    dve.wait_ge(bias_loaded, 16)
                    link(nc.vector.tensor_copy(bias_parts[:, 0], bias_f[:, :]))
                    link(nc.vector.tensor_tensor(bias_rest[:, 0], bias_f[:, :], bias_parts[:, 0], ALU.subtract))
                    link(nc.vector.tensor_copy(bias_parts[:, 1], bias_rest[:, 0]))
                    link(nc.vector.tensor_tensor(bias_rest[:, 1], bias_rest[:, 0], bias_parts[:, 1], ALU.subtract))
                    nc.vector.tensor_copy(bias_parts[:, 2], bias_rest[:, 1]).then_inc(bias_setup, 1)
                    dve.wait_ge(s_loaded, 16 * 4)

                def stats(self, src, n, par, stat, mv, eps):
                    for c in range(C):
                        last = nc.vector.bn_stats(st2[:, par, c, :], src[:, c, :])
                    last.then_inc(stat, 1)
                    dve.wait_ge(stat, at(n, 1, 1))
                    dve.nop(nofuse=True)
                    for c in range(C):
                        last = nc.vector.bn_aggr(mv2[:, par, c, :], st2[:, par, c, :])
                    last.then_inc(mv, 1)
                    dve.wait_ge(mv, at(n, 1, 1))
                    nc.vector.tensor_scalar(mneg[:, par], mv2[:, par, :, 0], -1.0, None, ALU.mult)
                    nc.vector.tensor_scalar(var2[:, par], mv2[:, par, :, 1], EPS, None, ALU.add).then_inc(eps, 1)

                def route(self, n, par):
                    step = [0]
                    STEPS = 9

                    def link(ins):
                        step[0] += 1
                        ins.then_inc(r_step, 1)
                        dve.wait_ge(r_step, at(n, STEPS, step[0]))
                    bc = lambda t: t.unsqueeze(2).to_broadcast([P, C, E])
                    L = [lg[:, i] for i in range(10)]
                    dve.wait_ge(lg_put, at(n, 1, 1))
                    link(nc.vector.tensor_reduce(lmx[:, 0], y_ps[1][:, 0:C * E].rearrange("p (c e) -> p c e", c=C), AX.X, ALU.max))
                    nc.vector.tensor_tensor(L[0], y_ps[1][:, 0:C * E].rearrange("p (c e) -> p c e", c=C), bc(lmx[:, 0]),
                                            ALU.subtract).then_inc(lg_taken, 1)
                    dve.wait_ge(lg_taken, at(n, 1, 1))
                    link(nc.vector.scalar_tensor_tensor(L[2], L[0], 0.0, rev[:, :, :], ALU.is_ge, ALU.mult))
                    link(nc.vector.tensor_reduce(lmx[:, 1], L[2], AX.X, ALU.max))
                    link(nc.vector.tensor_tensor(L[3], L[2], bc(lmx[:, 1]), ALU.is_equal))
                    dve.wait_ge(r_tanh, at(n, 1, 1))
                    link(nc.vector.tensor_scalar(L[4], L[1], -1.0, 1.0, ALU.mult, ALU.add))
                    link(nc.vector.reciprocal(L[5], L[4]))
                    link(nc.vector.scalar_tensor_tensor(L[6], L[1], 1.0, L[5], ALU.add, ALU.mult))
                    link(nc.vector.tensor_reduce(lmx[:, 2], L[6], AX.X, ALU.add))
                    link(nc.vector.reciprocal(lmx[:, 3], lmx[:, 2]))
                    nc.vector.tensor_tensor(gates[:, par], L[3], bc(lmx[:, 3]), ALU.mult).then_inc(gates_ready, 1)

                def choose(self, n, s, chunks):
                    dve.wait_ge(gates_ready, at(n, 1, 1))
                    for c in chunks:
                        dve.wait_ge(ex_put, at(n, C, c + 1))
                        for e in range(E_DVE):
                            gate = gates[:, s % 2, c, e:e + 1]
                            src = z_ps[c % 2][:, e * D:(e + 1) * D]
                            if e >= 2:
                                dve.wait_ge(sel, at(n, C * E_DVE, c * E_DVE + e - 1))
                            if e == 1:
                                ins = nc.vector.tensor_scalar(odd[:, c, :], src, gate, None, ALU.mult)
                            else:
                                dst = acc[:, s, c, :] if e % 2 == 0 else odd[:, c, :]
                                ins = nc.vector.scalar_tensor_tensor(dst, src, gate, xin[:, s, c, :] if e == 0 else dst, ALU.mult, ALU.add)
                            ins.then_inc(sel, 1)
                    if C - 1 in chunks:
                        dve.wait_ge(sel, at(n, C * E_DVE, C * E_DVE))
                        nc.vector.tensor_tensor(acc[:, s], acc[:, s], odd[:, :, :], ALU.add).then_inc(summed, 1)

                def statistics(self, grp, s):
                    n = grp * NS + s
                    dve.wait_ge(acc_in[s], at(grp, 48, 48))
                    self.stats(xin[:, s], n, s, m_stat, m_mv, m_eps)

                def start(self, grp, first):
                    self.statistics(grp, 0)
                    self.statistics(grp, 1)

                def step(self, grp, s, first, chunks):
                    n = grp * NS + s
                    if s == 1:
                        self.statistics(grp, 2)
                        self.statistics(grp, 3)
                    if s >= 2:
                        self.choose(n - 2, s - 2, chunks)
                    if 1 <= s <= NS:
                        self.route(n - 1, (s - 1) % 2)

                def turn(self, n, s, lay, k):
                    if live(k, 2):
                        dve.wait_ge(q_done, at(n, 1, -1))
                        if not (isinstance(n, int) and n < 3):
                            dve.wait_ge(yb_done, at(n, 1, -2))
                        p_ = y_ps[stream(s, 2) % 2][:, 0:HALF]
                        nc.vector.tensor_tensor(yT[:, 0:HALF], p_, q_sb[:, :], ALU.add)
                        nc.vector.tensor_tensor(yT[:, HALF:S], p_, q_sb[:, :], ALU.subtract).then_inc(pq_done, 1)
                    if live(k, 1):
                        ly = layer(lay, s, 1)
                        cur = stream(s, 1) % 2
                        zc, zs = z_ps[cur][:, 0:S], z_ps[cur][:, S:2 * S]
                        a1, bb, a2 = (kf[:, ly, 4 * i:4 * i + 4, :].rearrange("p c d -> p (c d)") for i in range(3))
                        dve.wait_ge(fwd_put, at(n, 1, 0))
                        if not (isinstance(n, int) and n < 2):
                            dve.wait_ge(ys_done, at(n, 1, -1))
                            dve.wait_ge(inv_put, at(n, 1, -1))
                        nc.vector.tensor_tensor(pr[:, 0], zc, bb, ALU.mult)
                        nc.vector.tensor_tensor(pr[:, 1], zs, a2, ALU.mult).then_inc(prod_s, 1)
                        nc.vector.tensor_tensor(pr[:, 2], zc, a1, ALU.mult)
                        nc.vector.tensor_tensor(pr[:, 3], zs, bb, ALU.mult).then_inc(prod_c, 1)
                        dve.wait_ge(prod_c, at(n, 1, 0))
                        nc.vector.tensor_tensor(yc[:, :], pr[:, 2], pr[:, 3], ALU.subtract).then_inc(yc_done, 1)
                    if live(k, -1):
                        cur = stream(s, -1) % 2
                        dve.wait_ge(xh_done, at(n, 1, 2))
                        if not (isinstance(n, int) and n < 1):
                            dve.wait_ge(fwd_put, at(n, 1, 0))
                        nc.vector.tensor_tensor(zp[:, cur, 0], xh[:, 0:2], xh[:, 2:4], ALU.add)
                        nc.vector.tensor_tensor(zp[:, cur, 1], xh[:, 0:2], xh[:, 2:4], ALU.subtract).then_inc(zp_done, 1)
                    if live(k, 2):
                        s2 = stream(s, 2)
                        dve.wait_ge(th_done, at(n, 1, -1))
                        nc.vector.scalar_tensor_tensor(gt[:, :, :], th[:, :, :], 1.0, w_ps[:, :, 0:D], ALU.add,
                                                       ALU.mult).then_inc(g_done, 1)
                        dve.wait_ge(g_done, at(n, 1, -1))
                        nc.vector.scalar_tensor_tensor(h[:, s2], gt[:, :, :], 0.5, h[:, s2], ALU.mult, ALU.add).then_inc(gated, 1)
                        if k is not None and k - 2 >= N_K - NS:
                            dve.wait_ge(gated, at(n, 1, -1))
                            dve.wait_ge(mixed, at(self.grp, NS, NS))
                            self.finish(s2, k - 2 - (N_K - NS))
                    if live(k, -2):
                        s2 = stream(s, -2)
                        if k == -2:
                            dve.wait_ge(h_ready, at(self.grp, NS, NS))
                        if k is None or k >= 2:
                            dve.wait_ge(gated, at(n, 1, -1))
                        self.stats(h[:, s2], n + 2, s2, l_stat, l_mv, l_eps)

                def finish(self, s, i):
                    m = self.grp * NS + i
                    if not (isinstance(m, int) and m < 2):
                        dve.wait_ge(out_stored[s % 2], at(self.grp, 48 * NS // 2, 48 * (i // 2)))
                    nc.vector.tensor_tensor(res[:, s % 2], acc[:, s], h[:, s], ALU.add).then_inc(res_done, 1)

            groups(Vector(), dve)

        @block.tensor
        def _(pe):
            mm = nc.tensor.matmul

            class Tensor:
                def before(self):
                    pe.wait_ge(s_setup, 3)
                    pe.wait_ge(s_loaded, 16 * 4)

                def transpose(self, n, s, grp, first):
                    pe.wait_ge(h_ready, at(n, 1, 1))
                    if not (first and s == 0):
                        pe.wait_ge(xmT_taken, at(n, 1, 0))
                    if s == 0 and not first:
                        pe.wait_ge(pq_done, at(grp, N_K, -1))
                    for c in range(C):
                        last = nc.tensor.transpose(y_ps[0][:, c * P:(c + 1) * P], h[:, s, c, :], ident3[:, :])
                    last.then_inc(xmT_put, 1)

                def logits(self, n, s, grp, first):
                    pe.wait_ge(xmT_taken, at(n, 1, 1))
                    if not (first and s == 0):
                        pe.wait_ge(lg_taken, at(n, 1, 0))
                    if s == 0 and not first:
                        pe.wait_ge(pq_done, at(grp, N_K, 0))
                    for c in range(C):
                        mm(y_ps[1][:, c * E:(c + 1) * E], xmT[:, s % 2, c * P:(c + 1) * P], rw[:, :], start=True, stop=False)
                        last = mm(y_ps[1][:, c * E:(c + 1) * E], onesf[0:1, :], rb[0:1, :], start=False, stop=True)
                    last.then_inc(lg_put, 1)

                def experts(self, n, s, c, grp, first):
                    if c >= 2 or not (first and s == 0):
                        pe.wait_ge(sel, at(n, C * E_DVE, (c - 1) * E_DVE))
                        pe.wait_ge(scaled, at(n, C, c - 1))
                    if s == 0 and c == 0 and first:
                        pe.wait_ge(ew_loaded, 16)
                        pe.wait_ge(bias_rows, 48)
                    if s == 0 and c < 2 and not first:
                        pe.wait_ge(prod_c, at(grp, N_K, c - 1))
                    for j in range(2):
                        o = z_ps[c % 2][:, j * S:(j + 1) * S]
                        mm(o, xmT[:, s % 2, c * P:(c + 1) * P], ew[:, j * S:(j + 1) * S], start=True, stop=False)
                        last = mm(o, ones3[0:96, :], bias3[0:96, NL * 2 * D + j * S:NL * 2 * D + (j + 1) * S],
                                  start=False, stop=True)
                    last.then_inc(ex_put, 1)

                def start(self, grp, first):
                    pass

                def step(self, grp, s, first, chunks):
                    n = grp * NS + s
                    if s == 1:
                        self.logits(n - 1, 0, grp, first)
                    if s < NS:
                        self.transpose(n, s, grp, first)
                    if 1 <= s <= NS:
                        for c in range(C):
                            self.experts(n - 1, s - 1, c, grp, first)
                            if c == 1 and s < NS:
                                self.logits(n, s, grp, first)
                    if s == NS and first:
                        pe.wait_ge(dft_loaded, 48)

                def turn(self, n, s, lay, k):
                    if live(k, 0):
                        cur = s % 2
                        pe.wait_ge(zp_done, at(n, 1, 1))
                        if k is not None and k < 2:
                            pe.wait_ge(sel, at(self.grp, NS * C * E_DVE, (NS * C + k - 1) * E_DVE))
                            pe.wait_ge(scaled, at(self.grp, NS * C, NS * C + k - 1))
                            pe.wait_ge(lg_taken, at(self.grp, NS, NS))
                        if not (isinstance(n, int) and n < 2):
                            pe.wait_ge(prod_c, at(n, 1, -1))
                        for col, part_, f in [(0, 0, 0), (1, 0, 1), (2, 1, 0), (3, 1, 1), (4, 1, 2), (5, 1, 3), (6, 0, 2), (7, 0, 3)]:
                            for c in range(2):
                                last = mm(z_ps[cur][:, col * P:(col + 1) * P], dft[:, part_, c, f * P:(f + 1) * P],
                                          zp[:, cur, part_, c, :], start=c == 0, stop=c == 1)
                        last.then_inc(fwd_put, 1)
                    if live(k, 2):
                        ly = layer(lay, s, 2)
                        pe.wait_ge(gelu_done, at(n, 1, -1))
                        if not (isinstance(n, int) and n < 3):
                            pe.wait_ge(g_done, at(n, 1, -2))
                            pe.wait_ge(th_done, at(n, 1, -2))
                        for c in range(C):
                            mm(w_ps[:, c, :], yg[:, c * P:(c + 1) * P], wout[:, ly, :], start=True, stop=False)
                            last = mm(w_ps[:, c, :], ones3[0:96, :],
                                      bias3[0:96, 0:NL * 2 * D].rearrange("p (l o) -> p l o", l=NL)[:, ly, :], start=False, stop=True)
                        last.then_inc(w_put, 1)
                    if live(k, 1):
                        pe.wait_ge(yc_done, at(n, 1, 0))
                        pe.wait_ge(ys_done, at(n, 1, 0))
                        if not (isinstance(n, int) and n < 3):
                            pe.wait_ge(pq_done, at(n, 1, -2))
                        for half, rows in enumerate([[(yc, 0), (yc, 1), (ys, 2), (ys, 3)], [(yc, 2), (yc, 3), (ys, 0), (ys, 1)]]):
                            for j, (src, f) in enumerate(rows):
                                last = mm(y_ps[stream(s, 1) % 2][:, half * HALF:(half + 1) * HALF], src[:, f * P:(f + 1) * P],
                                          idft[:, half, j, :], start=j == 0, stop=j == 3)
                        last.then_inc(inv_put, 1)

            groups(Tensor(), pe)


def program(nc, io, out):
    x1_dram = nc.dram_tensor("x1_scratch", (B, S, D), FP32, kind="Internal").ap()
    k_dram = nc.dram_tensor("k_scratch", (NL, D, S), FP32, kind="Internal").ap()
    with nc.sbuf_tensor("kf", [P, NL, 12, D], FP32) as kf, nc.sbuf_tensor("bias_y", [P, NL, S], FP32) as bias_y:
        conv_kernels(nc, io, k_dram, kf, bias_y)
        attention(nc, io, x1_dram)
        s4d_and_experts(nc, io, x1_dram, out, kf, bias_y)


def kernel(**inputs):
    import numpy as _np
    import concourse.bacc as _bacc
    from concourse import mybir as _mybir
    from concourse.bass_utils import run_bass_kernel_spmd as _run

    nc = _bacc.Bacc("TRN2", target_bir_lowering=False, num_devices=1)
    g = {k: _np.asarray(v) for k, v in inputs.items()}
    arrays = dict(shape_constants())
    arrays["x"] = g["L0_attn_x"][:, TOKENS]
    wqk = g["L0_attn_W_qkv"][:2 * D].reshape(2, H, HD, D).transpose(0, 2, 1, 3).reshape(2 * D, D)
    arrays["WqkvT"] = _np.concatenate([wqk, g["L0_attn_W_qkv"][2 * D:]]).T
    arrays["WoT"] = g["L0_attn_W_o"].T
    arrays["W1T"] = g["L0_ffn_W1"].T
    arrays["W2T"] = g["L0_ffn_W2"].T.reshape(NF, P, D).transpose(1, 0, 2)
    arrays["b1"] = g["L0_ffn_b1"].reshape(NF, P).T
    arrays["b2"] = g["L0_ffn_b2"]
    arrays["ln_w"] = g["L1_attn_ln_w"]
    modes = [_np.broadcast_to(g["L1_attn_log_dt"][:, None, :], (NL, NM, D))]
    modes += [g["L1_attn_" + k].transpose(0, 2, 1) for k in ("A_re_log", "A_im", "C_re", "C_im")]
    modes = _np.stack(modes).reshape(5, NL // 2, 2, 1, NM, D)
    arrays["s4d_par"] = _np.broadcast_to(modes, (5, NL // 2, 2, 2, NM, D)).transpose(2, 3, 4, 0, 1, 5).reshape(P, 5, NL // 2, D)
    arrays["D_skipT"], arrays["ln_bT"] = g["L1_attn_D_skip"].T, g["L1_attn_ln_b"].T
    arrays["WoutT"] = g["L1_attn_W_out"].transpose(2, 0, 1)
    arrays["biases"] = _np.concatenate([g["L1_attn_b_out"].reshape(-1), g["L1_ffn_expert_b"].reshape(-1)]).reshape(P, -1)
    arrays["router_w"], arrays["router_b"] = g["L1_ffn_router_w"], g["L1_ffn_router_b"]
    arrays["EW"] = g["L1_ffn_expert_w"].transpose(1, 0, 2).reshape(D, E * D)
    arrays = {"in_" + k: _np.ascontiguousarray(v) for k, v in arrays.items()}
    io = {k[3:]: nc.dram_tensor(k, v.shape, _mybir.dt.from_np(v.dtype), kind="ExternalInput").ap() for k, v in arrays.items()}
    out = nc.dram_tensor("out", (B, S, D), _mybir.dt.float32, kind="ExternalOutput").ap()
    program(nc, io, out)
    r = _run(nc, [arrays], core_ids=[0])
    got = r.results[0]["out"]
    back = _np.argsort(TOKENS)
    return _np.ascontiguousarray(_np.asarray(got)[:, back])
```

```python
import math
from contextlib import ExitStack

import numpy as np

import concourse.bass as bass
from concourse import mybir

FP32 = mybir.dt.float32
BF16 = mybir.dt.bfloat16
ALU = mybir.AluOpType
ACT = mybir.ActivationFunctionType
AX = mybir.AxisListType

B, S, D = 16, 512, 128
P = 128
C = S // P
H, HD = 16, 8
HG = 4
G = H // HG
FF = 4 * D
NF = FF // P
NL, NM = 4, 32
E = 8
EPS = 1e-5
BIG = -1e30
TWO_BF16_ONES = float(np.array([0x3F803F80], np.uint32).view(np.float32)[0])
MAGIC = 1.5 * 2.0 ** 23

TOKENS = np.concatenate([np.arange(P) + c * P if c % 2 == 0 else (c + 1) * P - 1 - np.arange(P) for c in range(C)])

Q_PARTS = (0, 0, 1, 0, 2, 1)
K_PARTS = (0, 1, 0, 2, 0, 1)
N_PROD = len(Q_PARTS)
ROW_POS = N_PROD * HD
ROW_MAX = 96
FILLS = 11
TILES = 5
STACKS = 2 * N_PROD


def bf16_parts(a):
    bf = mybir.dt.np(BF16)
    out, rest = [], np.asarray(a, np.float32)
    for _ in range(3):
        part = rest.astype(bf)
        out.append(part)
        rest = rest - part.astype(np.float32)
    return out


def shape_constants():
    bf = mybir.dt.np(BF16)
    c = {}
    c["ident"] = np.eye(P, dtype=np.float32)
    c["ident_bf"] = np.eye(P, dtype=np.float32).astype(bf)
    i = np.arange(P)
    c["mask_bf"] = np.stack([np.where(i[None, :] > i[:, None], BIG, 0.0),
                             np.where(i[None, :] < i[:, None], BIG, 0.0)], 1).astype(bf)
    start = 2.0 ** (-2.0 ** (-(math.log2(H) - 3)))
    slopes = np.asarray([start * start ** h for h in range(H)], np.float32)
    parts = bf16_parts(slopes)
    pos = TOKENS
    low, high = (pos % 256).astype(np.float32), (pos - pos % 256).astype(np.float32)
    qrows, krows = np.zeros((12, H, S), np.float32), np.zeros((12, H, S), np.float32)
    for n, s in enumerate(parts):
        s = s.astype(np.float32)[:, None]
        for m, at in enumerate((low, high)):
            qrows[2 * n + m], krows[2 * n + m] = s, -at[None, :]
            qrows[6 + 2 * n + m], krows[6 + 2 * n + m] = at[None, :], s
    c["pos_q"], c["pos_k"] = qrows.astype(bf), krows.astype(bf)
    by4, even, odd = np.arange(0, S, 4), np.arange(2, S, 4), np.arange(1, S, 2)
    by4_sin = by4.copy()
    by4_sin[0] = S
    w = np.pi / S
    t = np.arange(P) + 0.5
    row = lambda f, freqs: f(w * np.outer(t, freqs))
    mirror = lambda f, freqs: f(w * np.outer(S / 2 - t, freqs))
    blocks = [row(np.cos, by4), row(np.cos, even)]
    blocks += [(row(np.cos, odd) + mirror(np.cos, odd)) / 2, (row(np.cos, odd) - mirror(np.cos, odd)) / 2]
    blocks += [row(np.sin, by4_sin), row(np.sin, even)]
    blocks += [(row(np.sin, odd) + mirror(np.sin, odd)) / 2, (row(np.sin, odd) - mirror(np.sin, odd)) / 2]
    blocks = np.concatenate(blocks, 1).reshape(P, 12, P)
    c["dft"] = np.ascontiguousarray(blocks).astype(np.float32)
    c["idft"] = np.ascontiguousarray(blocks.transpose(2, 1, 0)).astype(np.float32)
    l = np.arange(S)
    freq = np.concatenate([by4, even, odd])
    weight = np.where(freq == 0, 1.0, 2.0) / (2 * S)
    first = by4_sin
    first_weight = np.where(first == S, 1.0, 2.0) / (2 * S)
    a1 = np.cos(w * np.outer(l, freq)) * weight
    bb = np.sin(w * np.outer(l, freq)) * weight
    a2 = np.cos(w * np.outer(l, first)) * first_weight
    kt = np.concatenate([a1, bb, a2], 1)
    c["kdft"] = np.ascontiguousarray(kt.reshape(C, P, 9 * P).transpose(1, 0, 2)).astype(np.float32)
    real = ((np.arange(P) // NM) % 2 == 0).astype(np.float32)
    c["phase"] = np.stack([0.25 * real, 2 * real - 1, -2 * real, -2 * (1 - real), real, 1 - real], 1).astype(np.float32)
    c["steps"] = np.arange(NM, dtype=np.float32)
    p = np.arange(P)
    token = np.concatenate([p, S // 2 - 1 - p, S - 1 - p, S // 2 + p])
    c["prefix"] = np.ascontiguousarray((l[:, None] <= token[None, :]).astype(np.float32).reshape(C, P, S).transpose(1, 0, 2))
    c["rev"] = np.broadcast_to(E - np.arange(E, dtype=np.float32), (C, E)).copy()
    return c


def at(n, per, k):
    return n * per + k


def attention(nc, io, x1_dram, NB=B):
    ctx = ExitStack()

    def sb(name, shape, dt=FP32):
        return ctx.enter_context(nc.sbuf_tensor(name, shape, dt))

    def pb(name, shape, dt=FP32):
        return ctx.enter_context(nc.psum_tensor(name, shape, dt))

    def sem(name):
        return ctx.enter_context(nc.semaphore(name))

    with ctx:
        wqkv = sb("wqkv", [P, 3 * D])
        wo = sb("wo", [P, D])
        w1 = sb("w1", [P, FF])
        w2 = sb("w2", [P, NF, D])
        wtmp = sb("wtmp", [P, FF])
        b1 = sb("b1", [P, NF])
        b2f = sb("b2f", [P, D])
        ident = sb("ident", [P, P])
        ident_bf = sb("ident_bf", [P, P], BF16)
        mask_bf = sb("mask_bf", [P, 2, P], BF16)
        ones = sb("ones", [P, P])
        gsum = sb("gsum", [P, 6])
        minus_half = sb("minus_half", [P, C])
        x_sb = sb("x_sb", [P, 2, C, D])
        xr = sb("xr", [P, 2, C, D])
        xb = sb("xb", [P, C, D])
        stats = sb("stats", [P, C, 6])
        mv = sb("mv", [P, C, 2])
        rstd = sb("rstd", [P, C])
        xn = sb("xn", [P, C, D])
        xnT = sb("xnT", [P, S])
        parts = sb("parts", [P, 2, 3, S], BF16)
        rest = sb("rest", [P, 2, S])
        qs = sb("qs", [P, 2, H, S], BF16)
        ks = sb("ks", [P, 2, H, S], BF16)
        v_aug = sb("v_aug", [P, 2, C, H, 32])
        hT = sb("hT", [P, NF, S])
        mx = sb("mx", [P, 2, HG, C])
        mrow = sb("mrow", [HG * C, 2, 2, P], BF16)
        p_sb = sb("p_sb", [P, 2, TILES, 2 * S])
        o_sb = sb("o_sb", [P, S])
        rden = sb("rden", [P, C, HG])
        o_tok = sb("o_tok", [P, C, D])
        oT = sb("oT", [P, S])
        x1 = sb("x1", [P, C, D])

        fill_ps = [pb(f"fill_ps{i}", [P, S]) for i in range(2)]
        tile_ps = [pb(f"tile_ps{i}", [P, 2 * S]) for i in range(2)]
        o_ps = pb("o_ps", [P, S])
        misc_ps = pb("misc_ps", [P, S])

        loaded = sem("loaded")
        set_up = sem("set_up")
        stacks_zero, even_zero = sem("stacks_zero"), sem("even_zero")
        v_zero = sem("v_zero")
        odd_zero = sem("odd_zero")
        even_pos, odd_pos = sem("even_pos"), sem("odd_pos")
        x_loaded = sem("x_loaded")
        pre_link = sem("pre_link")
        abs_done = sem("abs_done")
        gamma_ps = sem("gamma_ps")
        weights_ready = sem("weights_ready")
        ln_stat = sem("ln_stat")
        ln_mv = sem("ln_mv")
        ln_eps = sem("ln_eps")
        ln_rstd = sem("ln_rstd")
        ln_done = sem("ln_done")
        xT_put, xT_taken = sem("xT_put"), sem("xT_taken")
        qk_put = sem("qk_put")
        qk_high, qk_rest, qk_mid, qk_split = sem("qk_high"), sem("qk_rest"), sem("qk_mid"), sem("qk_split")
        v_put, v_taken = sem("v_put"), sem("v_taken")
        ffn1_put, ffn1_taken = sem("ffn1_put"), sem("ffn1_taken")
        x_biased = sem("x_biased")
        ffn2_put, ffn2_taken = sem("ffn2_put"), sem("ffn2_taken")
        mrow_put, mrow_high, mrow_taken = sem("mrow_put"), sem("mrow_high"), sem("mrow_taken")
        otr_put, rden_done, otr_taken = sem("otr_put"), sem("rden_done"), sem("otr_taken")
        oT_put, oT_taken = sem("oT_put"), sem("oT_taken")
        out_put, out_taken = sem("out_put"), sem("out_taken")
        stacked = sem("stacked")
        filled, reduced = sem("filled"), sem("reduced")
        mrow_in = sem("mrow_in")
        scored, exped, masked = sem("scored"), sem("exped"), sem("masked")
        pv_done, o_copied = sem("pv_done"), sem("o_copied")
        stored = sem("stored")

        N_LOADS = 9
        LAST = NB - 1

        def fill_plan():
            plan = [(3, (h,)) for h in range(4)] + [(2, (h,)) for h in range(4)]
            plan += [(1, (0, 1)), (1, (2, 3)), (0, (0, 1, 2, 3))]
            return plan

        def unit_steps(g, front, back, nxt):
            own = g >= 2
            exp = front if own else back
            pv = front if g == 3 else back
            f = [("fill", i) for i in range(FILLS)] if front else []
            b = [("tile", t) for t in range(TILES)] if exp else []
            v = [("pv", kb) for kb in range(C)] if pv else []
            m = [[], [], [], [], []]
            if (front if g > 0 else back):
                m[0].append(("mrow", 0))
            if g == 2 and nxt:
                m[0].append(("xT", 0))
                m[1].append(("qk", 0))
                m[2].append(("rest", 0))
                m[3] += [("mid", 0), ("qk", 1)]
                m[4].append(("rest", 1))
            if pv:
                m[3].append(("o_copy", 0))
                m[4].append(("otr", 0))
            if g == 3 and nxt:
                m[0].append(("mid", 1))
            if g == 0 and front:
                m[1].append(("ffn1", 0)), m[2].append(("ffn1", 1))
            if g == 1 and front:
                m[1].append(("ffn1", 2)), m[2].append(("ffn1", 3)), m[3].append(("ffn2", 0))
            if g == 1 and nxt:
                m[1].append(("ln", 0)), m[3].append(("lnx", 0))
            if g == 3:
                if nxt:
                    m[1].append(("v", 0))
                if back:
                    m[2].append(("oT", 0)), m[3].append(("out", 0))
            steps = []
            for i in range(5):
                steps += b[i:i + 1] + f[2 * i:2 * i + 1] + v[i:i + 1] + f[2 * i + 1:2 * i + 2] + m[i]
            return steps + f[10:]

        TAKEN = {"mrow": (mrow_taken, G), "otr": (otr_taken, G), "ffn1": (ffn1_taken, NF), "ffn2": (ffn2_taken, 1),
                 "xT": (xT_taken, 1), "qk": (qk_rest, 2), "v": (v_taken, 1), "oT": (oT_taken, 1), "out": (out_taken, 1)}

        def misc_index(kind, i, n, g):
            if kind == "mrow":
                return (n, g - 1) if g else (n - 1, G - 1)
            if kind == "otr":
                return (n, 0) if g == 3 else (n - 1, g + 1)
            if kind in ("xT", "v", "qk"):
                return n + 1, i
            if kind in ("oT", "out"):
                return n - 1, i
            return n, i

        def exp_unit(n, g):
            return (n, g - 2) if g >= 2 else (n - 1, g + 2)

        def pv_unit(n, g):
            return (n, 0) if g == 3 else (n - 1, g + 1)

        def drive(handle, eng):
            handle.before()
            handle.pre(0)
            handle.slot(0, 0, True, False, True)
            handle.slot(1, 1, True, True, True)
            with eng.Fori(1, (NB - 2) // 2) as j:
                handle.slot(j * 2, 0, True, True, True)
                handle.slot(j * 2 + 1, 1, True, True, True)
            handle.slot(LAST - 1, 0, True, True, True)
            handle.slot(LAST, 1, True, True, False)
            handle.slot(NB, NB % 2, False, True, False)
            handle.after()

        block = ctx.enter_context(nc.Block())

        @block.sync
        def _(sp):
            class Sync:
                def before(self):
                    self.load_x(0, 0)
                    for dst, src in ((wqkv[:, :], io["WqkvT"]), (wo[:, :], io["WoT"]), (w1[:, :], io["W1T"]),
                                     (w2[:, :, :], io["W2T"]), (b1[:, :], io["b1"]),
                                     (b2f[:, :], io["b2"].partition_broadcast(P)), (ident[:, :], io["ident"]),
                                     (ident_bf[:, :], io["ident_bf"]), (mask_bf[:, :, :], io["mask_bf"])):
                        sp.dma_start(dst, src).then_inc(loaded, 16)
                    sp.wait_ge(stacks_zero, 1)
                    sp.wait_ge(even_zero, 2)
                    sp.dma_start(qs[ROW_POS:ROW_POS + 12, 0], io["pos_q"]).then_inc(even_pos, 16)
                    sp.dma_start(ks[ROW_POS:ROW_POS + 12, 0], io["pos_k"]).then_inc(even_pos, 16)

                def load_x(self, n, par):
                    sp.dma_start(x_sb[:, par], io["x"][n].rearrange("(c p) d -> p c d", p=P)).then_inc(x_loaded, 16)

                def stack(self, n, par, which):
                    sp.wait_ge(qk_split, at(n, 2, which + 1))
                    dst, order = ((qs, Q_PARTS), (ks, K_PARTS))[which]
                    for slot, part in enumerate(order):
                        sp.dma_start(dst[slot * HD:(slot + 1) * HD, par],
                                     parts[:, which, part, :]).then_inc(stacked, 16)

                def pre(self, n):
                    self.stack(0, 0, 0)
                    self.stack(0, 0, 1)
                    sp.wait_ge(odd_zero, 3)
                    sp.dma_start(qs[ROW_POS:ROW_POS + 12, 1], io["pos_q"]).then_inc(odd_pos, 16)
                    sp.dma_start(ks[ROW_POS:ROW_POS + 12, 1], io["pos_k"]).then_inc(odd_pos, 16)

                def slot(self, n, par, front, back, nxt):
                    if nxt:
                        if back:
                            sp.wait_ge(ffn2_taken, at(n, 1, 0))
                        self.load_x(n + 1, 1 - par)
                    for g in range(G):
                        for kind, i in unit_steps(g, front, back, nxt):
                            if kind == "mrow":
                                m, k = misc_index(kind, i, n, g)
                                mpar = par if g else 1 - par
                                sp.wait_ge(mrow_taken, at(m, G, k + 1))
                                for r in range(2):
                                    sp.dma_start(qs[ROW_MAX + r:ROW_MAX + r + 1, mpar, k * HG:(k + 1) * HG, :],
                                                 mrow[:, k % 2, r, :]).then_inc(mrow_in, 16)
                            if kind == "mid":
                                if i == 0 and back:
                                    sp.wait_ge(scored, at(n, G * TILES, 0))
                                self.stack(n + 1, 1 - par, i)
                            if kind == "out":
                                sp.wait_ge(out_taken, at(n - 1, 1, 1))
                                sp.dma_start(x1_dram[n - 1].rearrange("(c p) d -> p c d", p=P),
                                             x1[:, :, :]).then_inc(stored, 16)

                def after(self):
                    sp.wait_ge(stored, 16 * NB)
            drive(Sync(), sp)

        @block.gpsimd
        def _(pool):
            class Pool:
                def before(self):
                    nc.gpsimd.memset(minus_half[:, :], -0.5).then_inc(set_up, 1)
                    nc.gpsimd.memset(ones[:, :], 1.0).then_inc(set_up, 1)
                    nc.gpsimd.memset(ks[0:ROW_MAX, 0].bitcast(FP32), 0.0).then_inc(even_zero, 1)
                    pool.wait_ge(even_zero, 1)
                    nc.gpsimd.memset(ks[ROW_MAX:P, 0].bitcast(FP32), TWO_BF16_ONES).then_inc(even_zero, 1)
                    pool.wait_ge(set_up, 2)
                    pool.wait_ge(even_zero, 2)

                def low(self, n, which):
                    pool.wait_ge(qk_mid, at(n, 2, which + 1))
                    nc.gpsimd.tensor_tensor(parts[:, which, 2, :], rest[:, which, :], parts[:, which, 1, :],
                                            ALU.subtract).then_inc(qk_split, 1)

                def rstd(self, n):
                    pool.wait_ge(ln_eps, at(n, 1, 1))
                    nc.gpsimd.tensor_tensor(rstd[:, :], rstd[:, :], minus_half[:, :], ALU.pow).then_inc(ln_rstd, 1)

                def pre(self, n):
                    self.rstd(0)
                    nc.gpsimd.memset(v_aug[:, :, :, :, :], 0.0).then_inc(v_zero, 1)
                    pool.wait_ge(v_zero, 1)
                    nc.gpsimd.memset(v_aug[:, :, :, :, HD:HD + 1], 1.0).then_inc(v_zero, 1)
                    self.low(0, 0)
                    self.low(0, 1)
                    nc.gpsimd.memset(qs[:, 1].bitcast(FP32), 0.0).then_inc(odd_zero, 1)
                    nc.gpsimd.memset(ks[0:ROW_MAX, 1].bitcast(FP32), 0.0).then_inc(odd_zero, 1)
                    pool.wait_ge(odd_zero, 2)
                    nc.gpsimd.memset(ks[ROW_MAX:P, 1].bitcast(FP32), TWO_BF16_ONES).then_inc(odd_zero, 1)
                    pool.wait_ge(odd_zero, 3)
                    pool.wait_ge(loaded, 16 * N_LOADS)

                def slot(self, n, par, front, back, nxt):
                    for g in range(G):
                        m, k = exp_unit(n, g)
                        for kind, i in unit_steps(g, front, back, nxt):
                            if kind == "ln":
                                self.rstd(n + 1)
                            if kind == "mid":
                                self.low(n + 1, i)
                            if kind == "ffn1" and i == 0:
                                pool.wait_ge(x_loaded, at(n, 16, 16))
                                if back:
                                    pool.wait_ge(ffn2_taken, at(n, 1, 0))
                                pool.nop(nofuse=True)
                                nc.gpsimd.tensor_tensor(xb[:, :, :], x_sb[:, par], b2f[:, :].unsqueeze(1).to_broadcast([P, C, D]),
                                                        ALU.add).then_inc(x_biased, 1)
                            if kind == "tile":
                                pool.wait_ge(exped, at(m, G * TILES, k * TILES + i + 1))
                                t = p_sb[:, k % 2, i, :]
                                if i == HG:
                                    blocks = [(t.rearrange("p (a q) -> p a q", a=4)[:, :, 0:P], 1)]
                                else:
                                    odd_chunks = t[:, S:2 * S].rearrange("p (a q) -> p a q", a=C)[:, 0:C:C - 1, :]
                                    blocks = [(t[:, 0:P], 1), (odd_chunks, -1)]
                                pool.nop(nofuse=True)
                                for blk, way in blocks:
                                    pattern = [[way, P]] if len(blk.shape) == 2 else [[0, blk.shape[1]], [way, P]]
                                    last = nc.gpsimd.affine_select(out=blk, in_=blk, compare_op=ALU.is_ge, fill=0.0, base=0,
                                                                   pattern=pattern, channel_multiplier=-way)
                                last.then_inc(masked, 1)

                def after(self):
                    pass
            drive(Pool(), pool)

        @block.scalar
        def _(act):
            class Scalar:
                def before(self):
                    act.wait_ge(loaded, 16 * N_LOADS)
                    nc.scalar.activation(wtmp[:, :], w1[:, :], ACT.Abs, accum_out=gsum[:, 0:1]).then_inc(abs_done, 1)
                    act.wait_ge(abs_done, 1)
                    nc.scalar.activation(wtmp[:, :], w2[:, :, :].rearrange("p a b -> p (a b)"), ACT.Abs,
                                         accum_out=gsum[:, 1:2]).then_inc(abs_done, 1)

                def take_xT(self, n):
                    act.wait_ge(xT_put, at(n, 1, 1))
                    nc.scalar.activation(xnT[:, :], misc_ps[:, :], ACT.Copy).then_inc(xT_taken, 1)

                def high(self, n, which):
                    act.wait_ge(qk_put, at(n, 2, which + 1))
                    if not isinstance(n, int) or n > 0:
                        act.wait_ge(stacked, at(n, 16 * STACKS, 0))
                    nc.scalar.activation(parts[:, which, 0, :], misc_ps[:, :], ACT.Copy).then_inc(qk_high, 1)

                def mid(self, n, which):
                    act.wait_ge(qk_rest, at(n, 2, which + 1))
                    nc.scalar.activation(parts[:, which, 1, :], rest[:, which, :], ACT.Copy).then_inc(qk_mid, 1)

                def pre(self, n):
                    self.take_xT(0)
                    for which in range(2):
                        self.high(0, which)
                        self.mid(0, which)

                def slot(self, n, par, front, back, nxt):
                    for g in range(G):
                        m, k = exp_unit(n, g)
                        pm, pk = pv_unit(n, g)
                        for kind, i in unit_steps(g, front, back, nxt):
                            if kind == "tile":
                                idx = k * TILES + i
                                act.wait_ge(scored, at(m, G * TILES, idx + 1))
                                if i == 0 and (back or k >= 2):
                                    act.wait_ge(pv_done, at(m, G, k - 1))
                                nc.scalar.activation(p_sb[:, k % 2, i, :], tile_ps[idx % 2][:, :], ACT.Exp).then_inc(exped, 1)
                            if kind == "o_copy":
                                act.wait_ge(pv_done, at(pm, G, pk + 1))
                                if back or pk >= 1:
                                    act.wait_ge(otr_put, at(pm, G, pk))
                                nc.scalar.activation(o_sb[:, :], o_ps[:, :], ACT.Copy).then_inc(o_copied, 1)
                            if kind == "xT":
                                self.take_xT(n + 1)
                            if kind == "qk":
                                self.high(n + 1, i)
                            if kind == "mid":
                                self.mid(n + 1, i)
                            if kind == "ffn1":
                                act.wait_ge(ffn1_put, at(n, NF, i + 1))
                                if i == 0 and back:
                                    act.wait_ge(ffn2_put, at(n, 1, 0))
                                nc.scalar.activation(hT[:, i, :], misc_ps[:, :], ACT.Relu,
                                                     bias=b1[:, i:i + 1]).then_inc(ffn1_taken, 1)
                            if kind == "oT":
                                act.wait_ge(oT_put, at(n - 1, 1, 1))
                                nc.scalar.activation(oT[:, :], misc_ps[:, :], ACT.Copy).then_inc(oT_taken, 1)

                def after(self):
                    pass
            drive(Scalar(), act)

        @block.vector
        def _(dve):
            class Vector:
                def __init__(self):
                    self.linked = 0

                def link(self, ins):
                    self.linked += 1
                    ins.then_inc(pre_link, 1)
                    dve.wait_ge(pre_link, self.linked)

                def before(self):
                    nc.vector.memset(qs[:, 0].bitcast(FP32), 0.0).then_inc(stacks_zero, 1)
                    self.layer_norm(0, 0)
                    self.apply_norm(0, 0)
                    dve.wait_ge(gamma_ps, 1)
                    self.link(nc.vector.tensor_scalar(gsum[:, 2:4], misc_ps[:, 0:2], 1.0 / (D * FF), EPS, ALU.mult, ALU.add))
                    self.link(nc.vector.reciprocal(gsum[:, 4:6], gsum[:, 2:4]))
                    for k, w in enumerate((w1[:, :], w2[:, :, :].rearrange("p a b -> p (a b)"))):
                        self.link(nc.vector.tensor_scalar(w, w, gsum[:, 4 + k:5 + k], None, ALU.mult))
                        self.link(nc.vector.tensor_scalar(w, w, 1.0, -1.0, ALU.min, ALU.max))
                        self.link(nc.vector.tensor_scalar(w, w, MAGIC, -MAGIC, ALU.add, ALU.add))
                    self.link(nc.vector.tensor_scalar(wqkv[:, 0:D], wqkv[:, 0:D], HD ** -0.5, None, ALU.mult))
                    nc.vector.tensor_scalar(wtmp[:, 0:1], wqkv[:, 0:1], 1.0, None, ALU.mult).then_inc(weights_ready, 1)

                def layer_norm(self, n, par):
                    dve.wait_ge(x_loaded, at(n, 16, 16))
                    for c in range(C):
                        nc.vector.bn_stats(stats[:, c, :], x_sb[:, par, c, :]).then_inc(ln_stat, 1)
                    dve.wait_ge(ln_stat, at(n, C, C))
                    dve.nop(nofuse=True)
                    for c in range(C):
                        nc.vector.bn_aggr(mv[:, c, :], stats[:, c, :]).then_inc(ln_mv, 1)
                    dve.wait_ge(ln_mv, at(n, C, C))
                    nc.vector.tensor_scalar(rstd[:, :], mv[:, :, 1], EPS, None, ALU.add).then_inc(ln_eps, 1)

                def apply_norm(self, n, par):
                    dve.wait_ge(ln_rstd, at(n, 1, 1))
                    for c in range(C):
                        nc.vector.tensor_scalar(xn[:, c, :], x_sb[:, par, c, :], mv[:, c, 0:1], rstd[:, c:c + 1],
                                                ALU.subtract, ALU.mult).then_inc(ln_done, 1)

                def rest(self, n, which):
                    dve.wait_ge(qk_high, at(n, 2, which + 1))
                    nc.vector.tensor_tensor(rest[:, which, :], misc_ps[:, :], parts[:, which, 0, :], ALU.subtract).then_inc(qk_rest, 1)

                def take_v(self, n, par):
                    dve.wait_ge(v_put, at(n, 1, 1))
                    nc.vector.tensor_copy(v_aug[:, par, :, :, 0:HD], misc_ps[:, :].rearrange("p (c h d) -> p c h d", c=C, d=HD)) \
                        .then_inc(v_taken, 1)

                def pre(self, n):
                    self.rest(0, 0)
                    self.rest(0, 1)
                    dve.wait_ge(v_zero, 2)
                    self.take_v(0, 0)

                def slot(self, n, par, front, back, nxt):
                    for g in range(G):
                        pm, pk = pv_unit(n, g)
                        for kind, i in unit_steps(g, front, back, nxt):
                            if kind == "fill":
                                qb, heads = fill_plan()[i]
                                idx = g * FILLS + i
                                dve.wait_ge(filled, at(n, G * FILLS, idx + 1))
                                if i == 0 and (back or g >= 2):
                                    dve.wait_ge(mrow_put, at(n, G, g - 1))
                                width = P * (qb + 1)
                                src = fill_ps[idx % 2][:, 0:width * len(heads)].rearrange("p (h k) -> p h k", k=width)
                                nc.vector.tensor_reduce(mx[:, g % 2, heads[0]:heads[0] + len(heads), qb], src,
                                                        AX.X, ALU.max).then_inc(reduced, 1)
                            if kind == "mrow":
                                m, k = misc_index(kind, i, n, g)
                                dve.wait_ge(mrow_put, at(m, G, k + 1))
                                if back or k >= 2:
                                    dve.wait_ge(mrow_in, at(m, 32 * G, 32 * (k - 1)))
                                nc.vector.tensor_scalar(mrow[:, k % 2, 0, :], misc_ps[0:HG * C, 0:P], -1.0, None, ALU.mult) \
                                    .then_inc(mrow_high, 1)
                                dve.wait_ge(mrow_high, at(m, G, k + 1))
                                nc.vector.scalar_tensor_tensor(mrow[:, k % 2, 1, :], misc_ps[0:HG * C, 0:P], -1.0,
                                                               mrow[:, k % 2, 0, :], ALU.mult, ALU.subtract).then_inc(mrow_taken, 1)
                            if kind == "otr":
                                dve.wait_ge(otr_put, at(pm, G, pk + 1))
                                o = misc_ps[:, :].rearrange("p (c j e) -> p c j e", c=C, j=HG)
                                if back or pk >= 1:
                                    dve.wait_ge(otr_taken, at(pm, G, pk))
                                nc.vector.reciprocal(rden[:, :, :], o[:, :, :, HD]).then_inc(rden_done, 1)
                                dve.wait_ge(rden_done, at(pm, G, pk + 1))
                                if pk == 0 and back:
                                    dve.wait_ge(oT_put, at(pm, 1, 0))
                                nc.vector.tensor_tensor(
                                    o_tok[:, :, pk * HG * HD:(pk + 1) * HG * HD].rearrange("p c (j e) -> p c j e", j=HG),
                                    o[:, :, :, 0:HD], rden[:, :, :].unsqueeze(3).to_broadcast([P, C, HG, HD]),
                                    ALU.mult).then_inc(otr_taken, 1)
                            if kind == "ln":
                                self.layer_norm(n + 1, 1 - par)
                            if kind == "lnx":
                                dve.wait_ge(xT_put, at(n + 1, 1, 0))
                                self.apply_norm(n + 1, 1 - par)
                            if kind == "rest":
                                self.rest(n + 1, i)
                            if kind == "v":
                                if back:
                                    dve.wait_ge(pv_done, at(n, G, 0))
                                self.take_v(n + 1, 1 - par)
                            if kind == "ffn2":
                                dve.wait_ge(ffn2_put, at(n, 1, 1))
                                dve.wait_ge(x_biased, at(n, 1, 1))
                                nc.vector.tensor_tensor(xr[:, par], misc_ps[:, :].rearrange("p (c d) -> p c d", c=C),
                                                        xb[:, :, :], ALU.add).then_inc(ffn2_taken, 1)
                            if kind == "out":
                                dve.wait_ge(out_put, at(n - 1, 1, 1))
                                if not isinstance(n, int) or n >= 2:
                                    dve.wait_ge(stored, at(n - 1, 16, 0))
                                nc.vector.tensor_tensor(x1[:, :, :], misc_ps[:, :].rearrange("p (c d) -> p c d", c=C),
                                                        xr[:, 1 - par], ALU.add).then_inc(out_taken, 1)

                def after(self):
                    pass
            drive(Vector(), dve)

        @block.tensor
        def _(pe):
            mm = nc.tensor.matmul

            class Tensor:
                def __init__(self):
                    self.was = None

                def before(self):
                    pe.wait_ge(loaded, 16 * N_LOADS)
                    self.misc("xT", 0, 0, 0, 0, 0)
                    pe.wait_ge(xT_taken, 1)
                    pe.wait_ge(abs_done, 2)
                    pe.wait_ge(set_up, 2)
                    mm(misc_ps[:, 0:2], ones[:, :], gsum[:, 0:2], start=True, stop=True).then_inc(gamma_ps, 1)
                    pe.wait_ge(weights_ready, 1)

                def wait_taken(self, was):
                    if was:
                        kind, m, k = was
                        s, per = TAKEN[kind]
                        pe.wait_ge(s, at(m, per, k + 1))

                def misc(self, kind, i, m, k, par, last_par):
                    if kind == "xT":
                        pe.wait_ge(ln_done, at(m, C, C))
                        for c in range(C):
                            last = nc.tensor.transpose(misc_ps[:, c * P:(c + 1) * P], xn[:, c, :], ident[:, :])
                        last.then_inc(xT_put, 1)
                    if kind == "qk":
                        mm(misc_ps[:, :], wqkv[:, i * D:(i + 1) * D], xnT[:, :], start=True, stop=True).then_inc(qk_put, 1)
                    if kind == "v":
                        for c in range(C):
                            last = mm(misc_ps[:, c * P:(c + 1) * P], xnT[:, c * P:(c + 1) * P], wqkv[:, 2 * D:3 * D],
                                      start=True, stop=True)
                        last.then_inc(v_put, 1)
                    if kind == "ffn1":
                        mm(misc_ps[:, :], w1[:, i * P:(i + 1) * P], xnT[:, :], start=True, stop=True).then_inc(ffn1_put, 1)
                    if kind == "ffn2":
                        for c in range(C):
                            for f in range(NF):
                                last = mm(misc_ps[:, c * P:(c + 1) * P], hT[:, f, c * P:(c + 1) * P], w2[:, f, :],
                                          start=f == 0, stop=f == NF - 1)
                        last.then_inc(ffn2_put, 1)
                    if kind == "mrow":
                        pe.wait_ge(reduced, at(m, G * FILLS, (k + 1) * FILLS))
                        nc.tensor.transpose(misc_ps[0:HG * C, 0:P], mx[:, k % 2].rearrange("p h c -> p (h c)"),
                                            ident[:, :]).then_inc(mrow_put, 1)
                    if kind == "otr":
                        pe.wait_ge(o_copied, at(m, G, k + 1))
                        for c in range(C):
                            last = nc.tensor.transpose(misc_ps[:, c * P:(c + 1) * P], o_sb[:, c * P:(c + 1) * P], ident[:, :])
                        last.then_inc(otr_put, 1)
                    if kind == "oT":
                        pe.wait_ge(otr_taken, at(m, G, G))
                        for c in range(C):
                            last = nc.tensor.transpose(misc_ps[:, c * P:(c + 1) * P], o_tok[:, c, :], ident[:, :])
                        last.then_inc(oT_put, 1)
                    if kind == "out":
                        pe.wait_ge(oT_taken, at(m, 1, 1))
                        for c in range(C):
                            last = mm(misc_ps[:, c * P:(c + 1) * P], oT[:, c * P:(c + 1) * P], wo[:, :], start=True, stop=True)
                        last.then_inc(out_put, 1)

                def pre(self, n):
                    for kind, i in (("qk", 0), ("qk", 1), ("v", 0)):
                        self.wait_taken(self.was)
                        self.misc(kind, i, 0, i, 0, 0)
                        self.was = (kind, 0, i)

                def slot(self, n, par, front, back, nxt):
                    first = True
                    for g in range(G):
                        em, ek = exp_unit(n, g)
                        pm, pk = pv_unit(n, g)
                        epar = par if g >= 2 else 1 - par
                        ppar = par if g == 3 else 1 - par
                        for kind, i in unit_steps(g, front, back, nxt):
                            if kind == "fill":
                                qb, heads = fill_plan()[i]
                                idx = g * FILLS + i
                                if idx == 0:
                                    pe.wait_ge(stacked, at(n, 16 * STACKS, 16 * STACKS))
                                    if isinstance(n, int) and n < 2:
                                        pe.wait_ge((even_pos, odd_pos)[par], 32)
                                if back or idx >= 2:
                                    pe.wait_ge(reduced, at(n, G * FILLS, idx - 1))
                                width = P * (qb + 1)
                                for j, h in enumerate(heads):
                                    h = g * HG + h
                                    mm(fill_ps[idx % 2][:, j * width:(j + 1) * width], qs[0:ROW_MAX, par, h, qb * P:(qb + 1) * P],
                                       ks[0:ROW_MAX, par, h, 0:width], start=True, stop=False)
                                    last = mm(fill_ps[idx % 2][:, (j + 1) * width - P:(j + 1) * width], ident_bf[:, :],
                                              mask_bf[:, qb % 2, :], start=False, stop=True)
                                last.then_inc(filled, 1)
                            elif kind == "tile":
                                idx = ek * TILES + i
                                if i == 0:
                                    pe.wait_ge(mrow_in, at(em, 32 * G, 32 * (ek + 1)))
                                if back or idx >= 2:
                                    pe.wait_ge(exped, at(em, G * TILES, idx - 1))
                                out = tile_ps[idx % 2]
                                if i < HG:
                                    jobs = [(i, 0, 0), (i, 1, S), (i, 3, 2 * S - P)]
                                else:
                                    jobs = [(j, 2, 2 * P * j) for j in range(HG)]
                                for j, kb, col in jobs:
                                    h = ek * HG + j
                                    last = mm(out[:, col:col + S - kb * P], ks[:, epar, h, kb * P:(kb + 1) * P],
                                              qs[:, epar, h, kb * P:S], start=True, stop=True)
                                last.then_inc(scored, 1)
                            elif kind == "pv":
                                if i == 0:
                                    pe.wait_ge(masked, at(pm, G * TILES, (pk + 1) * TILES))
                                    if back or pk >= 1:
                                        pe.wait_ge(o_copied, at(pm, G, pk))
                                    if pk == 0:
                                        pe.wait_ge(v_taken, at(pm, 1, 1))
                                for j in range(HG):
                                    t = HG if i == 2 else j
                                    col = {0: 0, 1: S, 2: 2 * P * j, 3: 2 * S - P}[i]
                                    last = mm(o_ps[32 * j:32 * j + 32, i * P:S], v_aug[:, ppar, i, pk * HG + j, :],
                                              p_sb[:, pk % 2, t, col:col + S - i * P], start=i == 0, stop=i == C - 1)
                                if i == C - 1:
                                    last.then_inc(pv_done, 1)
                            elif kind in TAKEN:
                                m, k = misc_index(kind, i, n, g)
                                if first and back:
                                    self.wait_taken(("otr", n - 1, 0))
                                    if not isinstance(n, int) or n >= 2:
                                        self.wait_taken(("out", n - 2, 0))
                                else:
                                    self.wait_taken(self.was)
                                first = False
                                self.misc(kind, i, m, k, par, 1 - par)
                                self.was = (kind, m, k)

                def after(self):
                    pass
            drive(Tensor(), pe)


def conv_kernels(nc, io, k_dram, kf, bias_y):
    ctx = ExitStack()

    def sb(name, shape, dt=FP32):
        return ctx.enter_context(nc.sbuf_tensor(name, shape, dt))

    def pb(name, shape, dt=FP32):
        return ctx.enter_context(nc.psum_tensor(name, shape, dt))

    def sem(name):
        return ctx.enter_context(nc.semaphore(name))

    LP = NL // 2
    NA, NB_ = 32, 16
    QN = 4
    QW = D // QN
    GR = QW // 4
    TWO_PI = 2 * math.pi
    PI = 3.1415925
    with ctx:
        par = sb("par", [P, 5, LP, D])
        tmp = sb("tmp", [P, 13, LP, D])
        phase = sb("phase", [P, 6])
        steps = sb("steps", [P, NA])
        ex_u = sb("ex_u", [P, LP * D, NA])
        ex_v = sb("ex_v", [P, LP * D, NB_])
        ang = sb("ang", [P, QW * NA])
        near = sb("near", [P, QW * NA])
        r_u = sb("r_u", [P, 2, QW * NA])
        s_u = sb("s_u", [P, 2, QW * NA])
        r_v = sb("r_v", [P, 2, QW * NB_])
        u_t = sb("u_t", [P, 2, QW * NA])
        v_t = sb("v_t", [P, 2, QW * NB_])
        k_out = sb("k_out", [P, NL, D // 4, NB_])
        k_hl = sb("k_hl", [P, 2, S])
        k_lh = sb("k_lh", [P, C, 2, D])
        kdft = sb("kdft", [P, C, 9 * P])
        w_bc = sb("w_bc", [P, NL, D])
        skip = sb("skip", [P, NL])
        bias = sb("bias", [P, NL])
        prefix = sb("prefix", [P, C, S])
        ident2 = sb("ident2", [P, P])
        k_ps = [[pb(f"k_ps{i}{j}", [P, S]) for j in range(2)] for i in range(2)]
        t_ps = pb("t_ps", [P, 2, S])
        f_ps = [pb(f"f_ps{i}", [P, S]) for i in range(2)]

        k_loaded, t_loaded = sem("k_loaded"), sem("t_loaded")
        dve_step = sem("dve_step")
        dt_done, x_ready, act_small = sem("dt_done"), sem("x_ready"), sem("act_small")
        angle_ready = sem("angle_ready")
        ex_ready = sem("ex_ready")
        coef_ready = sem("coef_ready")
        v_angles, u_angles = sem("v_angles"), sem("u_angles")
        v_sine, u_sine, half_sine, squared = sem("v_sine"), sem("u_sine"), sem("half_sine"), sem("squared")
        waves = sem("waves")
        sine_part, v_ready, tables = sem("sine_part"), sem("v_ready"), sem("tables")
        k_put, k_taken, k_stored = sem("k_put"), sem("k_taken"), sem("k_stored")
        k_back, skip_in, tr_put, tr_taken = sem("k_back"), sem("skip_in"), sem("tr_put"), sem("tr_taken")
        f_put, f_taken, b_put, b_taken = sem("f_put"), sem("f_taken"), sem("b_put"), sem("b_taken")
        weighted = sem("weighted")
        block = ctx.enter_context(nc.Block())
        chunks = [(lp, q) for lp in range(LP) for q in range(QN)]
        LAST = len(chunks) - 1
        F_BANKS = 5

        @block.sync
        def _(sp):
            for i in range(5):
                sp.dma_start(par[:, i], io["s4d_par"][:, i]).then_inc(k_loaded, 16)
            sp.dma_start(phase[:, :], io["phase"]).then_inc(k_loaded, 16)
            sp.dma_start(steps[:, :], io["steps"].partition_broadcast(P)).then_inc(k_loaded, 16)
            sp.dma_start(ident2[:, :], io["ident"]).then_inc(t_loaded, 16)
            sp.dma_start(skip[:, :], io["D_skipT"]).then_inc(t_loaded, 16)
            sp.dma_start(bias[:, :], io["ln_bT"]).then_inc(t_loaded, 16)
            sp.dma_start(kdft[:, :, :], io["kdft"]).then_inc(t_loaded, 16)
            sp.dma_start(prefix[:, :, :], io["prefix"]).then_inc(t_loaded, 16)
            sp.dma_start(w_bc[:, :, :], io["ln_w"].partition_broadcast(P)).then_inc(t_loaded, 16)
            for lp in range(LP):
                sp.wait_ge(k_taken, (lp + 1) * QN)
                for lay in (2 * lp, 2 * lp + 1):
                    for i in range(4):
                        dst = k_dram[lay].rearrange("(g i) (a b) -> i a g b", i=4, b=NB_)[i]
                        sp.dma_start(dst, k_out[32 * i:32 * i + 32, lay]).then_inc(k_stored, 16)
                sp.wait_ge(k_stored, 16 * 8 * (lp + 1))
                if lp > 0:
                    sp.wait_ge(tr_put, lp)
                sp.dma_start(k_hl[:, :, :], k_dram[2 * lp:2 * lp + 2].rearrange("n h l -> h n l")).then_inc(k_back, 16)

        @block.vector
        def _(dve):
            counts = {}

            def do(ins, s=None):
                s = s or dve_step
                counts[s] = counts.get(s, 0) + 1
                ins.then_inc(s, 1)
                dve.wait_ge(s, counts[s])

            def tt(out, a, b, op, s=None):
                do(nc.vector.tensor_tensor(out, a, b, op), s)

            def ts(out, a, s0, s1_, op0, op1=ALU.bypass, s=None):
                do(nc.vector.tensor_scalar(out, a, s0, s1_, op0, op1) if s1_ is not None
                   else nc.vector.tensor_scalar(out, a, s0, None, op0), s)

            C1 = 6.28125
            C2 = float(np.float32(TWO_PI - C1))
            C2 = math.floor(C2 * 2 ** 21) / 2 ** 21
            C3 = TWO_PI - C1 - C2

            f = lambda i: tmp[:, i].rearrange("p a b -> p (a b)")
            p_ = lambda i: par[:, i].rearrange("p a b -> p (a b)")
            DT, X, Y, TH, R, SN, SH, EM, ER, EI, T1, T2, T3 = (f(i) for i in range(13))

            def angles(ci):
                lp, q = chunks[ci]
                hs = slice(lp * D + q * QW, lp * D + (q + 1) * QW)
                for kind, width, unit, out, done in (("v", NB_, 1.0, r_v, v_angles), ("u", NA, float(NB_), r_u, u_angles)):
                    m = QW * width
                    a, t, r = ang[:, 0:m], near[:, 0:m], out[:, ci % 2, 0:m]
                    w3 = a.rearrange("p (h a) -> p h a", a=width)
                    st = steps[:, 0:width].unsqueeze(1).to_broadcast([P, QW, width])
                    src = Y if kind == "v" else T3
                    tt(w3, src[:, hs].unsqueeze(2).to_broadcast([P, QW, width]), st, ALU.mult)
                    if kind == "u" and ci >= 2:
                        dve.wait_ge(tables, ci - 1)
                    if kind == "v":
                        ts(a, a, phase[:, 0:1], None, ALU.add)
                        if ci >= 2:
                            dve.wait_ge(v_ready, ci - 1)
                    ts(t, a, MAGIC, None, ALU.add)
                    do(nc.vector.scalar_tensor_tensor(r, t, -MAGIC, a, ALU.add, ALU.subtract), done)

            def u_table(ci):
                lp, q = chunks[ci]
                hs = slice(lp * D + q * QW, lp * D + (q + 1) * QW)
                w3 = lambda t: t[:, ci % 2].rearrange("p (h a) -> p h a", a=NA)
                dve.wait_ge(squared, ci + 1)
                do(nc.vector.scalar_tensor_tensor(w3(r_u), w3(r_u), -0.5, EM[:, hs].unsqueeze(2).to_broadcast([P, QW, NA]),
                                                  ALU.add, ALU.mult))
                dve.wait_ge(sine_part, ci + 1)
                nc.vector.tensor_tensor(r_u[:, ci % 2], r_u[:, ci % 2], s_u[:, ci % 2], ALU.add).then_inc(waves, 1)

            dve.wait_ge(k_loaded, 16 * 7)
            dve.wait_ge(dt_done, 2)
            tt(Y, p_(2), DT, ALU.mult)
            do(nc.vector.scalar_tensor_tensor(X, p_(1), -1.0, DT, ALU.mult, ALU.mult), x_ready)
            ts(T1, Y, 1 / TWO_PI, None, ALU.mult)
            ts(T1, T1, MAGIC, -MAGIC, ALU.add, ALU.add)
            do(nc.vector.scalar_tensor_tensor(R, T1, -C1, Y, ALU.mult, ALU.add))
            do(nc.vector.scalar_tensor_tensor(R, T1, -C2, R, ALU.mult, ALU.add))
            do(nc.vector.scalar_tensor_tensor(R, T1, -C3, R, ALU.mult, ALU.add))
            ts(R, R, PI, -PI, ALU.min, ALU.max, s=angle_ready)
            ts(Y, R, 1 / TWO_PI, None, ALU.mult)
            ts(T3, Y, float(NB_), None, ALU.mult)
            angles(0)
            dve.wait_ge(act_small, 3)
            ts(T1, TH, -1.0, 1.0, ALU.mult, ALU.add)
            do(nc.vector.reciprocal(T1, T1))
            do(nc.vector.scalar_tensor_tensor(EM, TH, 2.0, T1, ALU.mult, ALU.mult))
            do(nc.vector.scalar_tensor_tensor(T2, SH, -2.0, SH, ALU.mult, ALU.mult))
            ts(T1, T2, 1.0, None, ALU.add)
            tt(ER, EM, T1, ALU.mult)
            tt(ER, ER, T2, ALU.add)
            do(nc.vector.scalar_tensor_tensor(EI, EM, 1.0, SN, ALU.add, ALU.mult))
            tt(T1, p_(1), p_(1), ALU.mult)
            tt(T2, p_(2), p_(2), ALU.mult)
            tt(T1, T1, T2, ALU.add)
            do(nc.vector.reciprocal(T1, T1))
            tt(T2, ER, p_(1), ALU.mult)
            tt(R, EI, p_(2), ALU.mult)
            tt(T2, R, T2, ALU.subtract)
            tt(T2, T2, T1, ALU.mult)
            tt(R, EI, p_(1), ALU.mult)
            tt(SN, ER, p_(2), ALU.mult)
            do(nc.vector.scalar_tensor_tensor(R, R, -1.0, SN, ALU.mult, ALU.subtract))
            tt(R, R, T1, ALU.mult)
            tt(SN, p_(3), T2, ALU.mult)
            tt(SH, p_(4), R, ALU.mult)
            tt(SN, SN, SH, ALU.subtract)
            ts(SN, SN, phase[:, 1:2], 2.0, ALU.mult, ALU.mult)
            tt(ER, p_(3), R, ALU.mult)
            tt(EI, p_(4), T2, ALU.mult)
            tt(ER, ER, EI, ALU.add)
            ts(ER, ER, -2.0, None, ALU.mult)
            ts(T1, ER, phase[:, 3:4], None, ALU.mult)
            do(nc.vector.scalar_tensor_tensor(EM, SN, phase[:, 2:3], T1, ALU.mult, ALU.add))
            ts(T1, ER, phase[:, 4:5], None, ALU.mult)
            do(nc.vector.scalar_tensor_tensor(TH, SN, phase[:, 5:6], T1, ALU.mult, ALU.add), coef_ready)
            for ci in range(len(chunks)):
                if ci < LAST:
                    angles(ci + 1)
                u_table(ci)
            dve.wait_ge(t_loaded, 16 * 6)
            for lay in range(NL):
                dve.wait_ge(f_taken, F_BANKS * (lay // 2 + 1))
                w12 = w_bc[:, lay, :].unsqueeze(1).to_broadcast([P, 12, D])
                nc.vector.tensor_tensor(kf[:, lay], kf[:, lay], w12, ALU.mult).then_inc(weighted, 1)

        @block.gpsimd
        def _(pool):
            pool.wait_ge(coef_ready, 1)
            for ci, (lp, q) in enumerate(chunks):
                hs = slice(lp * D + q * QW, lp * D + (q + 1) * QW)
                w3 = s_u[:, ci % 2].rearrange("p (h a) -> p h a", a=NA)
                coef = tmp[:, 3].rearrange("p a b -> p (a b)")[:, hs]
                pool.wait_ge(u_sine, ci + 1)
                nc.gpsimd.tensor_tensor(w3, w3, coef.unsqueeze(2).to_broadcast([P, QW, NA]), ALU.mult).then_inc(sine_part, 1)
                pool.wait_ge(v_sine, ci + 1)
                if ci == 0:
                    pool.wait_ge(ex_ready, 1)
                if ci >= 2:
                    pool.wait_ge(k_put, 2 * (ci - 1))
                nc.gpsimd.tensor_tensor(v_t[:, ci % 2].rearrange("p (h b) -> p h b", b=NB_),
                                        r_v[:, ci % 2].rearrange("p (h b) -> p h b", b=NB_), ex_v[:, hs, :],
                                        ALU.mult).then_inc(v_ready, 1)
                pool.wait_ge(waves, ci + 1)
                if ci == 0:
                    pool.wait_ge(ex_ready, 2)
                nc.gpsimd.tensor_tensor(u_t[:, ci % 2].rearrange("p (h a) -> p h a", a=NA),
                                        r_u[:, ci % 2].rearrange("p (h a) -> p h a", a=NA), ex_u[:, hs, :],
                                        ALU.mult).then_inc(tables, 1)

        @block.scalar
        def _(act):
            f = lambda i: tmp[:, i].rearrange("p a b -> p (a b)")
            act.wait_ge(k_loaded, 16 * 7)
            nc.scalar.activation(f(0), par[:, 0].rearrange("p a b -> p (a b)"), ACT.Exp).then_inc(dt_done, 1)
            nc.scalar.activation(par[:, 1].rearrange("p a b -> p (a b)"), par[:, 1].rearrange("p a b -> p (a b)"),
                                 ACT.Exp).then_inc(dt_done, 1)
            act.wait_ge(x_ready, 1)
            nc.scalar.activation(f(3), f(1), ACT.Tanh, scale=0.5).then_inc(act_small, 1)
            act.wait_ge(angle_ready, 1)
            nc.scalar.activation(f(5), f(4), ACT.Sin).then_inc(act_small, 1)
            nc.scalar.activation(f(6), f(4), ACT.Sin, scale=0.5).then_inc(act_small, 1)
            for b in range(NB_):
                last = nc.scalar.activation(ex_v[:, :, b], f(1), ACT.Exp, scale=float(b))
            last.then_inc(ex_ready, 1)
            for a in range(NA):
                last = nc.scalar.activation(ex_u[:, :, a], f(1), ACT.Exp, scale=float(NB_ * a))
            last.then_inc(ex_ready, 1)

            def sines(ci):
                act.wait_ge(v_angles, ci + 1)
                nc.scalar.activation(r_v[:, ci % 2], r_v[:, ci % 2], ACT.Sin, scale=-2 * PI).then_inc(v_sine, 1)
                act.wait_ge(u_angles, ci + 1)
                if ci >= 2:
                    act.wait_ge(tables, ci - 1)
                nc.scalar.activation(s_u[:, ci % 2], r_u[:, ci % 2], ACT.Sin, scale=-2 * PI).then_inc(u_sine, 1)
                nc.scalar.activation(r_u[:, ci % 2], r_u[:, ci % 2], ACT.Sin, scale=PI).then_inc(half_sine, 1)
                act.wait_ge(half_sine, ci + 1)
                nc.scalar.activation(r_u[:, ci % 2], r_u[:, ci % 2], ACT.Square).then_inc(squared, 1)

            def take(ci):
                lp, q = chunks[ci]
                for l2 in range(2):
                    act.wait_ge(k_put, 2 * ci + l2 + 1)
                    for i in range(4):
                        src = k_ps[ci % 2][l2][32 * i:32 * i + 32, :].rearrange("p (g e) -> p g e", e=4 * NB_)
                        last = nc.scalar.activation(k_out[32 * i:32 * i + 32, 2 * lp + l2, q * GR:(q + 1) * GR, :],
                                                    src[:, :, i * NB_:(i + 1) * NB_], ACT.Copy)
                last.then_inc(k_taken, 1)

            def finish(lp):
                act.wait_ge(t_loaded, 16 * 6)
                act.wait_ge(k_back, 16 * (lp + 1))
                for l2 in range(2):
                    last = nc.scalar.activation(k_hl[:, l2, 0:1], k_hl[:, l2, 0:1], ACT.Identity, bias=skip[:, 2 * lp + l2:2 * lp + l2 + 1])
                last.then_inc(skip_in, 1)
                act.wait_ge(tr_put, lp + 1)
                nc.scalar.activation(k_lh[:, :, :, :].rearrange("p c l d -> p l c d"),
                                     t_ps[:, :, :].rearrange("p l (c d) -> p l c d", c=C), ACT.Copy).then_inc(tr_taken, 1)

            def take_transform(lp, banks):
                pair = slice(2 * lp, 2 * lp + 2)
                for j in banks:
                    act.wait_ge(f_put, F_BANKS * lp + j + 1)
                    n = min(2, 9 - 2 * j)
                    src = f_ps[j % 2][:, 0:n * 2 * D].rearrange("p (c l d) -> p l c d", c=n, l=2)
                    last = nc.scalar.activation(kf[:, pair, 2 * j:2 * j + n, :], src, ACT.Copy)
                    if j < 2:
                        last = nc.scalar.activation(kf[:, pair, 8 + max(1, 2 * j):10 + 2 * j, :], src[:, :, 1 - j:2, :], ACT.Copy)
                    last.then_inc(f_taken, 1)

            def take_bias(lp):
                for l2 in range(2):
                    act.wait_ge(b_put, 2 * lp + l2 + 1)
                    nc.scalar.activation(bias_y[:, 2 * lp + l2, :], t_ps[:, l2, :], ACT.Copy,
                                         scale=bias[:, 2 * lp + l2:2 * lp + l2 + 1]).then_inc(b_taken, 1)

            sines(0)
            for ci in range(1, LAST):
                sines(ci)
                take(ci - 1)
            sines(LAST)
            take(LAST - 1)
            finish(0)
            take(LAST)
            for lp in range(LP):
                if lp > 0:
                    finish(lp)
                take_transform(lp, range(F_BANKS))
                take_bias(lp)

        @block.tensor
        def _(pe):
            def products(ci):
                pe.wait_ge(tables, ci + 1)
                pe.wait_ge(v_ready, ci + 1)
                if ci >= 2:
                    pe.wait_ge(k_taken, ci - 1)
                for l2 in range(2):
                    rows = slice(2 * NM * l2, 2 * NM * (l2 + 1))
                    for g in range(GR):
                        last = nc.tensor.matmul(k_ps[ci % 2][l2][:, g * 4 * NB_:(g + 1) * 4 * NB_],
                                                u_t[rows, ci % 2, g * 4 * NA:(g + 1) * 4 * NA],
                                                v_t[rows, ci % 2, g * 4 * NB_:(g + 1) * 4 * NB_], start=True, stop=True)
                    last.then_inc(k_put, 1)

            def transpose(lp):
                pe.wait_ge(skip_in, lp + 1)
                if lp > 0:
                    pe.wait_ge(b_taken, 2 * lp)
                for l2 in range(2):
                    for c in range(C):
                        last = nc.tensor.transpose(t_ps[:, l2, c * P:(c + 1) * P], k_hl[:, l2, c * P:(c + 1) * P], ident2[:, :])
                last.then_inc(tr_put, 1)
                pe.wait_ge(tr_taken, lp + 1)

            def transform(lp, banks):
                for j in banks:
                    idx = F_BANKS * lp + j
                    if idx >= 2:
                        pe.wait_ge(f_taken, idx - 1)
                    for i in range(min(2, 9 - 2 * j)):
                        ch = 2 * j + i
                        for c in range(C):
                            last = nc.tensor.matmul(f_ps[j % 2][:, i * 2 * D:(i + 1) * 2 * D], kdft[:, c, ch * P:(ch + 1) * P],
                                                    k_lh[:, c, :, :], start=c == 0, stop=c == C - 1)
                    last.then_inc(f_put, 1)

            def bias_sums(lp):
                for l2 in range(2):
                    for c, (lo, hi) in enumerate(((0, 4), (1, 4), (2, 4), (2, 3))):
                        last = nc.tensor.matmul(t_ps[:, l2, lo * P:hi * P], k_lh[:, c, l2, :], prefix[:, c, lo * P:hi * P],
                                                start=c == 0, stop=c == C - 1)
                    last.then_inc(b_put, 1)

            pe.wait_ge(t_loaded, 16 * 6)
            for ci in range(LAST):
                products(ci)
            transpose(0)
            products(LAST)
            for lp in range(LP):
                if lp > 0:
                    transpose(lp)
                transform(lp, range(F_BANKS))
                bias_sums(lp)


def s4d_and_experts(nc, io, x1_dram, out_dram, kf, bias_y, NG=B // 8):
    ctx = ExitStack()
    NS = 8
    HALF = S // 2

    def sb(name, shape, dt=FP32):
        return ctx.enter_context(nc.sbuf_tensor(name, shape, dt))

    def pb(name, shape, dt=FP32):
        return ctx.enter_context(nc.psum_tensor(name, shape, dt))

    def sem(name):
        return ctx.enter_context(nc.semaphore(name))

    with ctx:
        dft = sb("dft", [P, 12, P])
        idft = sb("idft", [P, 12, P])
        wout = sb("wout", [P, NL, 2 * D])
        rw = sb("rw", [P, E])
        ew = sb("ew", [P, E * D])
        rb = sb("rb", [P, E])
        ident3 = sb("ident3", [P, P])
        ones3 = sb("ones3", [P, P], BF16)
        NBIAS = NL * 2 * D + E * D
        bias_f = sb("bias_f", [P, NBIAS // P])
        bias_rest = sb("bias_rest", [P, 2, NBIAS // P])
        bias_parts = sb("bias_parts", [P, 3, NBIAS // P], BF16)
        bias3 = sb("bias3", [P, NBIAS], BF16)
        mhalf = sb("mhalf", [P, C])
        rev = sb("rev", [P, C, E])
        acc = sb("acc", [P, NS, C, D])
        h = sb("h", [P, NS, C, D])
        st2 = sb("st2", [P, NS, C, 6])
        mv2 = sb("mv2", [P, NS, C, 2])
        var2 = sb("var2", [P, NS, C])
        mneg = sb("mneg", [P, NS, C])
        rs2 = sb("rs2", [P, NS, C])
        mrs = sb("mrs", [P, NS, C])
        xmT = sb("xmT", [P, 2, S])
        odd = sb("odd", [P, 2, C, D])
        lg = sb("lg", [P, 8, C, E])
        lmx = sb("lmx", [P, 4, C])
        xh = sb("xh", [P, C, D])
        fold1 = sb("fold1", [P, 2, 2, D])
        fold2 = sb("fold2", [P, 2, 2, 2, D])
        pr = sb("pr", [P, 4, S])
        yc = sb("yc", [P, S])
        ys = sb("ys", [P, S])
        q_sb = sb("q_sb", [P, HALF])
        sym = sb("sym", [P, 2, 2, D])
        yT = sb("yT", [P, S])
        yb = sb("yb", [P, S])
        yg = sb("yg", [P, S])
        th = sb("th", [P, C, D])
        gt = sb("gt", [P, C, D])
        res = sb("res", [P, 2, C, D])
        xin = sb("xin", [P, NS, C, D])
        gates = sb("gates", [P, 2, C, E])
        scaled_z = sb("scaled_z", [P, 2, E // 2, D])
        part = sb("part", [P, C, D])
        z_ps = [pb(f"z_ps{i}", [P, 2 * S]) for i in range(2)]
        y_ps = [pb(f"y_ps{i}", [P, S]) for i in range(2)]
        w_ps = pb("w_ps", [P, C, 2 * D])

        s_loaded, s_setup, s_chain = sem("s_loaded"), sem("s_setup"), sem("s_chain")
        bias_setup = sem("bias_setup")
        bias_loaded, bias_rows, ew_loaded, dft_loaded = sem("bias_loaded"), sem("bias_rows"), sem("ew_loaded"), sem("dft_loaded")
        acc_in = [sem(f"acc_in{i}") for i in range(NS)]
        m_stat, m_mv, m_eps, m_pow, m_rstd, h_ready = (sem(n) for n in ("m_stat", "m_mv", "m_eps", "m_pow", "m_rstd", "h_ready"))
        xmT_put, xmT_taken, lg_put, lg_taken = sem("xmT_put"), sem("xmT_taken"), sem("lg_put"), sem("lg_taken")
        r_step, r_tanh, ex_put, sel, part_sum = sem("r_step"), sem("r_tanh"), sem("ex_put"), sem("sel"), sem("part_sum")
        l_stat, l_mv, l_eps, l_pow, l_rstd, xh_done = (sem(n) for n in ("l_stat", "l_mv", "l_eps", "l_pow", "l_rstd", "xh_done"))
        fwd_put, prod_s, prod_c, yc_done, ys_done = sem("fwd_put"), sem("prod_s"), sem("prod_c"), sem("yc_done"), sem("ys_done")
        fold2_done, inv_put, q_done, yT_done, yb_done, gelu_done = (sem(n) for n in ("fold2_done", "inv_put", "q_done", "yT_done",
                                                                                  "yb_done", "gelu_done"))
        fold1_done, sym_done = sem("fold1_done"), sem("sym_done")
        w_put, th_done, g_done, gated = sem("w_put"), sem("th_done"), sem("g_done"), sem("gated")
        gates_ready = sem("gates_ready")
        scaled, part_step, part_done, mixed = sem("scaled"), sem("part_step"), sem("part_done"), sem("mixed")
        res_done, out_stored = sem("res_done"), [sem(f"out_stored{i}") for i in range(2)]
        N_K = NS * NL
        E_DVE = E // 2

        def turn(handle, grp, k):
            handle.grp = grp
            handle.turn(grp * N_K + k, k % NS, k // NS, k)

        def group(handle, eng, grp, first):
            handle.start(grp, first)
            for s in range(NS):
                if not first:
                    for k in {0: (0,), 1: (1, 2), 2: (3,)}.get(s, ()):
                        turn(handle, grp - 1, N_K + k)
                if s == NS - 1:
                    turn(handle, grp, -4)
                handle.step(grp, s, first, range(C))
            turn(handle, grp, -3)
            handle.step(grp, NS, first, range(C))
            turn(handle, grp, -2)
            handle.step(grp, NS + 1, first, range(C // 2))
            turn(handle, grp, -1)
            handle.step(grp, NS + 1, first, range(C // 2, C))
            for k in range(NS - 4):
                turn(handle, grp, k)
            with eng.Fori(1, NL) as lay:
                for k in range(-4, NS - 4):
                    handle.turn(grp * N_K + lay * NS + k, k % NS, lay + k // NS, None)
            for k in range(N_K - 4, N_K):
                turn(handle, grp, k)

        def ahead(s):
            return (2, 3) if s == 1 else (s + 2,) if 2 <= s < NS - 2 else ()

        def live(k, back):
            return k is None or 0 <= k - back < N_K

        def stream(s, back):
            return (s - back) % NS

        def layer(lay, s, back):
            return lay + (s - back) // NS

        block = ctx.enter_context(nc.Block())

        def groups(handle, eng):
            handle.before()
            group(handle, eng, 0, True)
            if NG > 1:
                with eng.Fori(1, NG) as grp:
                    group(handle, eng, grp, False)
            for k in range(N_K, N_K + 4):
                turn(handle, NG - 1, k)

        @block.sync
        def _(sp):
            class Sync:
                def before(self):
                    self.load_batch(0, 0)
                    sp.dma_start(bias_f[:, :], io["biases"]).then_inc(bias_loaded, 16)
                    for dst, src in ((ident3[:, :], io["ident"]), (rw[:, :], io["router_w"]), (rb[:, :], io["router_b"].partition_broadcast(P)),
                                     (rev[:, :, :], io["rev"].partition_broadcast(P))):
                        sp.dma_start(dst, src).then_inc(s_loaded, 16)
                    sp.dma_start(ew[:, :], io["EW"]).then_inc(ew_loaded, 16)
                    for s in range(1, NS):
                        self.load_batch(s, s)
                    sp.wait_ge(bias_setup, 2)
                    for r in range(3):
                        sp.dma_start(bias3[32 * r:32 * r + 1, :], bias_parts[:, r, :]).then_inc(bias_rows, 16)
                    for dst, src in ((wout[:, :, :], io["WoutT"]), (dft[:, :, :], io["dft"]), (idft[:, :, :], io["idft"])):
                        sp.dma_start(dst, src).then_inc(dft_loaded, 16)

                def load_batch(self, n, s):
                    sp.dma_start(xin[:, s, 0:2], x1_dram[n, 0:HALF].rearrange("(c p) d -> p c d", p=P)).then_inc(acc_in[s], 16)
                    sp.dma_start(xin[:, s, 2], x1_dram[n, 3 * P:4 * P]).then_inc(acc_in[s], 16)
                    sp.dma_start(xin[:, s, 3], x1_dram[n, 2 * P:3 * P]).then_inc(acc_in[s], 16)

                def load(self, grp):
                    for s in range(NS):
                        sp.wait_ge(sel, at(grp, NS * C * E_DVE, (s + 1 - NS) * C * E_DVE))
                        self.load_batch(grp * NS + s, s)

                def store(self, grp):
                    for s in range(NS):
                        n = grp * NS + s
                        sp.wait_ge(res_done, at(n, 1, 1))
                        sp.dma_start(out_dram[n, 0:HALF].rearrange("(c p) d -> p c d", p=P), res[:, s % 2, 0:2]).then_inc(out_stored[s % 2], 16)
                        sp.dma_start(out_dram[n, 3 * P:4 * P], res[:, s % 2, 2]).then_inc(out_stored[s % 2], 16)
                        sp.dma_start(out_dram[n, 2 * P:3 * P], res[:, s % 2, 3]).then_inc(out_stored[s % 2], 16)
            sync = Sync()
            sync.before()
            if NG > 1:
                with sp.Fori(0, NG - 1) as grp:
                    sync.load(grp + 1)
                    sync.store(grp)
            sync.store(NG - 1)
            for s in range(2):
                sp.wait_ge(out_stored[s], 48 * NS * NG // 2)

        @block.gpsimd
        def _(pool):
            class Pool:
                def before(self):
                    nc.gpsimd.memset(mhalf[:, :], -0.5).then_inc(s_setup, 1)
                    nc.gpsimd.memset(ones3[:, :], 1.0).then_inc(s_setup, 1)
                    pool.wait_ge(s_setup, 2)

                def rstd(self, n, par, eps, power, done):
                    pool.wait_ge(eps, at(n, 1, 1))
                    pool.nop(nofuse=True)
                    nc.gpsimd.tensor_tensor(rs2[:, par], var2[:, par], mhalf[:, :], ALU.pow).then_inc(power, 1)
                    pool.wait_ge(power, at(n, 1, 1))
                    nc.gpsimd.tensor_tensor(mrs[:, par], mneg[:, par], rs2[:, par], ALU.mult).then_inc(done, 1)

                def sum_scaled(self, n, s, chunks):
                    for c in chunks:
                        pool.wait_ge(scaled, at(n, C, c + 1))
                        z = scaled_z[:, c % 2]
                        nc.gpsimd.tensor_tensor(z[:, 0:2], z[:, 0:2], z[:, 2:4], ALU.add).then_inc(part_step, 1)
                        pool.wait_ge(part_step, at(n, C, c + 1))
                        nc.gpsimd.tensor_tensor(part[:, c], z[:, 0], z[:, 1], ALU.add).then_inc(part_done, 1)
                    if C - 1 in chunks:
                        pool.wait_ge(part_done, at(n, C, C))
                        pool.wait_ge(sel, at(n, C * E_DVE, C * E_DVE))
                        nc.gpsimd.tensor_tensor(part[:, :, :], part[:, :, :], odd[:, s % 2], ALU.add).then_inc(part_sum, 1)
                        pool.wait_ge(part_sum, at(n, 1, 1))
                        nc.gpsimd.tensor_tensor(acc[:, s], acc[:, s], part[:, :, :], ALU.add).then_inc(mixed, 1)

                def start(self, grp, first):
                    for i in (0, 1):
                        self.rstd(grp * NS + i, i, m_eps, m_pow, m_rstd)

                def step(self, grp, s, first, chunks):
                    if s >= 2:
                        self.sum_scaled(grp * NS + s - 2, s - 2, chunks)
                    for i in ahead(s):
                        self.rstd(grp * NS + i, i, m_eps, m_pow, m_rstd)

                def turn(self, n, s, lay, k):
                    if live(k, 1):
                        pool.wait_ge(prod_s, at(n, 1, 0))
                        if not (isinstance(n, int) and n < 2):
                            pool.wait_ge(inv_put, at(n, 1, -1))
                        nc.gpsimd.tensor_tensor(ys[:, :], pr[:, 0], pr[:, 1], ALU.add).then_inc(ys_done, 1)
                    if live(k, 2):
                        pool.wait_ge(sym_done, at(n, 1, -1))
                        y4 = yT[:, :].rearrange("p (c t) -> p c t", c=C)
                        nc.gpsimd.tensor_tensor(y4[:, 0:2], sym[:, :, 0], sym[:, :, 1], ALU.add)
                        nc.gpsimd.tensor_tensor(y4[:, 2:4], sym[:, :, 0], sym[:, :, 1], ALU.subtract).then_inc(yT_done, 1)
                        pool.wait_ge(yT_done, at(n, 1, -1))
                        if not (isinstance(n, int) and n < 3):
                            pool.wait_ge(gelu_done, at(n, 1, -2))
                        pool.nop(nofuse=True)
                        nc.gpsimd.tensor_tensor(yb[:, :], yT[:, :], bias_y[:, layer(lay, s, 2), :], ALU.add).then_inc(yb_done, 1)
                    if live(k, -2):
                        pool.wait_ge(xh_done, at(n, 1, 3))
                        if not (isinstance(n, int) and n < -1):
                            pool.wait_ge(fold2_done, at(n, 1, 2))
                        nc.gpsimd.tensor_tensor(fold1[:, 0], xh[:, 0:2], xh[:, 2:4], ALU.add)
                        nc.gpsimd.tensor_tensor(fold1[:, 1], xh[:, 0:2], xh[:, 2:4], ALU.subtract).then_inc(fold1_done, 1)
                    if live(k, -4):
                        self.rstd(n + 4, stream(s, -4), l_eps, l_pow, l_rstd)

            groups(Pool(), pool)

        @block.scalar
        def _(act):
            class Scalar:
                def before(self):
                    pass

                def normalise(self, src, dst, n, par, rstd, done):
                    act.wait_ge(rstd, at(n, 1, 1))
                    for c in range(C):
                        last = nc.scalar.activation(dst[:, c, :], src[:, c, :], ACT.Identity, bias=mrs[:, par, c:c + 1],
                                                    scale=rs2[:, par, c:c + 1])
                    last.then_inc(done, 1)

                def scale(self, n, par, first, chunks):
                    for c in chunks:
                        act.wait_ge(gates_ready, at(n, 1, 1))
                        act.wait_ge(ex_put, at(n, C, c + 1))
                        if not (first and c < 2):
                            act.wait_ge(part_done, at(n, C, c - 1))
                        for e in range(E_DVE, E):
                            last = nc.scalar.activation(scaled_z[:, c % 2, e - E_DVE], z_ps[c % 2][:, e * D:(e + 1) * D], ACT.Copy,
                                                        scale=gates[:, par, c, e:e + 1])
                        last.then_inc(scaled, 1)

                def normalised(self, grp, s, first):
                    act.wait_ge(acc_in[s], at(grp, 48, 48))
                    if not first:
                        act.wait_ge(res_done, at(grp, NS, s - NS + 1))
                    self.normalise(xin[:, s], h[:, s], grp * NS + s, s, m_rstd, h_ready)

                def start(self, grp, first):
                    pass

                def step(self, grp, s, first, chunks):
                    n = grp * NS + s
                    if s == 0:
                        self.normalised(grp, 0, first)
                    if s > NS:
                        self.scale(n - 2, s % 2, False, chunks)
                    elif s >= 2:
                        self.scale(n - 2, s % 2, first and s == 2, range(C // 2))
                        for i in ahead(s - 1) if s > 2 else ():
                            self.normalised(grp, i, first)
                        self.scale(n - 2, s % 2, first and s == 2, range(C // 2, C))
                    if 1 <= s <= NS:
                        act.wait_ge(lg_taken, at(n, 1, 0))
                        nc.scalar.activation(lg[:, 2], lg[:, 1], ACT.Tanh, scale=0.5).then_inc(r_tanh, 1)
                    if s < NS:
                        act.wait_ge(xmT_put, at(n, 1, 1))
                        if not (first and s < 2):
                            act.wait_ge(ex_put, at(n, C, -C))
                        nc.scalar.activation(xmT[:, s % 2], y_ps[0][:, :], ACT.Copy).then_inc(xmT_taken, 1)
                    if s == 0:
                        self.normalised(grp, 1, first)
                    if s == 1:
                        for i in ahead(s):
                            self.normalised(grp, i, first)

                def turn(self, n, s, lay, k):
                    if live(k, 2):
                        act.wait_ge(inv_put, at(n, 1, -1))
                        if not (isinstance(n, int) and n < 3):
                            act.wait_ge(sym_done, at(n, 1, -2))
                        nc.scalar.activation(q_sb[:, :], y_ps[stream(s, 2) % 2][:, HALF:S], ACT.Copy).then_inc(q_done, 1)
                    if live(k, -2):
                        if not (isinstance(n, int) and n < -1):
                            act.wait_ge(fold1_done, at(n, 1, 2))
                        s1 = stream(s, -2)
                        self.normalise(h[:, s1], xh, n + 2, s1, l_rstd, xh_done)
                    if live(k, 3):
                        act.wait_ge(w_put, at(n, 1, -2))
                        if not (isinstance(n, int) and n < 4):
                            act.wait_ge(g_done, at(n, 1, -3))
                        nc.scalar.activation(th[:, :, :], w_ps[:, :, D:2 * D], ACT.Tanh, scale=0.5).then_inc(th_done, 1)
                    if live(k, 2):
                        act.wait_ge(yb_done, at(n, 1, -1))
                        if not (isinstance(n, int) and n < 3):
                            act.wait_ge(w_put, at(n, 1, -2))
                        nc.scalar.activation(yg[:, :], yb[:, :], ACT.Gelu_apprx_tanh).then_inc(gelu_done, 1)

            groups(Scalar(), act)

        @block.vector
        def _(dve):
            class Vector:
                def before(self):
                    linked = [0]

                    def link(ins):
                        linked[0] += 1
                        ins.then_inc(s_chain, 1)
                        dve.wait_ge(s_chain, linked[0])
                    nc.vector.memset(bias3[:, :].bitcast(FP32), 0.0).then_inc(bias_setup, 1)
                    dve.wait_ge(bias_loaded, 16)
                    link(nc.vector.tensor_copy(bias_parts[:, 0], bias_f[:, :]))
                    link(nc.vector.tensor_tensor(bias_rest[:, 0], bias_f[:, :], bias_parts[:, 0], ALU.subtract))
                    link(nc.vector.tensor_copy(bias_parts[:, 1], bias_rest[:, 0]))
                    link(nc.vector.tensor_tensor(bias_rest[:, 1], bias_rest[:, 0], bias_parts[:, 1], ALU.subtract))
                    nc.vector.tensor_copy(bias_parts[:, 2], bias_rest[:, 1]).then_inc(bias_setup, 1)
                    dve.wait_ge(s_loaded, 16 * 4)

                def stats(self, src, n, par, stat, mv, eps):
                    for c in range(C):
                        last = nc.vector.bn_stats(st2[:, par, c, :], src[:, c, :])
                    last.then_inc(stat, 1)
                    self.moments(n, par, stat, mv, eps)

                def moments(self, n, par, stat, mv, eps):
                    dve.wait_ge(stat, at(n, 1, 1))
                    dve.nop(nofuse=True)
                    for c in range(C):
                        last = nc.vector.bn_aggr(mv2[:, par, c, :], st2[:, par, c, :])
                    last.then_inc(mv, 1)
                    dve.wait_ge(mv, at(n, 1, 1))
                    nc.vector.tensor_scalar(mneg[:, par], mv2[:, par, :, 0], -1.0, None, ALU.mult)
                    nc.vector.tensor_scalar(var2[:, par], mv2[:, par, :, 1], EPS, None, ALU.add).then_inc(eps, 1)

                def route(self, n, par):
                    STEPS = 10

                    def after(k):
                        dve.wait_ge(r_step, at(n, STEPS, k))
                    bc = lambda t: t.unsqueeze(2).to_broadcast([P, C, E])
                    logit, shifted, tanh_, rank, best, low, inv, exp_ = (lg[:, i] for i in range(8))
                    top, top_rank, total, scale_ = (lmx[:, i] for i in range(4))
                    dve.wait_ge(lg_put, at(n, 1, 1))
                    nc.vector.tensor_tensor(logit, y_ps[1][:, 0:C * E].rearrange("p (c e) -> p c e", c=C),
                                            rb[:, :].unsqueeze(1).to_broadcast([P, C, E]), ALU.add).then_inc(r_step, 1)
                    after(1)
                    nc.vector.tensor_reduce(top, logit, AX.X, ALU.max).then_inc(r_step, 1)
                    after(2)
                    nc.vector.tensor_tensor(shifted, logit, bc(top), ALU.subtract).then_inc(lg_taken, 1)
                    dve.wait_ge(lg_taken, at(n, 1, 1))
                    nc.vector.scalar_tensor_tensor(rank, shifted, 0.0, rev[:, :, :], ALU.is_ge, ALU.mult).then_inc(r_step, 1)
                    after(3)
                    nc.vector.tensor_reduce(top_rank, rank, AX.X, ALU.max).then_inc(r_step, 1)
                    dve.wait_ge(r_tanh, at(n, 1, 1))
                    nc.vector.tensor_scalar(low, tanh_, -1.0, 1.0, ALU.mult, ALU.add).then_inc(r_step, 1)
                    after(4)
                    nc.vector.tensor_tensor(best, rank, bc(top_rank), ALU.is_equal).then_inc(r_step, 1)
                    after(5)
                    nc.vector.reciprocal(inv, low).then_inc(r_step, 1)
                    after(7)
                    nc.vector.scalar_tensor_tensor(exp_, tanh_, 1.0, inv, ALU.add, ALU.mult).then_inc(r_step, 1)
                    after(8)
                    nc.vector.tensor_reduce(total, exp_, AX.X, ALU.add).then_inc(r_step, 1)
                    after(9)
                    nc.vector.reciprocal(scale_, total).then_inc(r_step, 1)
                    after(10)
                    nc.vector.tensor_tensor(gates[:, par], best, bc(scale_), ALU.mult).then_inc(gates_ready, 1)

                def choose(self, n, s, chunks):
                    dve.wait_ge(gates_ready, at(n, 1, 1))
                    if 0 in chunks and not (isinstance(n, int) and n < 2):
                        dve.wait_ge(mixed, at(n, 1, -1))
                    for c in chunks:
                        dve.wait_ge(ex_put, at(n, C, c + 1))
                        for e in range(E_DVE):
                            gate = gates[:, s % 2, c, e:e + 1]
                            src = z_ps[c % 2][:, e * D:(e + 1) * D]
                            if e >= 2:
                                dve.wait_ge(sel, at(n, C * E_DVE, c * E_DVE + e - 1))
                            if e == 1:
                                ins = nc.vector.tensor_scalar(odd[:, s % 2, c, :], src, gate, None, ALU.mult)
                            else:
                                dst = acc[:, s, c, :] if e % 2 == 0 else odd[:, s % 2, c, :]
                                ins = nc.vector.scalar_tensor_tensor(dst, src, gate, xin[:, s, c, :] if e == 0 else dst, ALU.mult, ALU.add)
                            ins.then_inc(sel, 1)

                def statistics(self, grp, s):
                    n = grp * NS + s
                    dve.wait_ge(acc_in[s], at(grp, 48, 48))
                    self.stats(xin[:, s], n, s, m_stat, m_mv, m_eps)

                def start(self, grp, first):
                    self.statistics(grp, 0)
                    self.statistics(grp, 1)

                def step(self, grp, s, first, chunks):
                    n = grp * NS + s
                    if s < 2:
                        for i in ahead(s):
                            self.statistics(grp, i)
                    elif s > NS:
                        self.choose(n - 2, s - 2, chunks)
                    else:
                        self.choose(n - 2, s - 2, range(C // 2))
                        for i in ahead(s):
                            self.statistics(grp, i)
                        self.choose(n - 2, s - 2, range(C // 2, C))
                    if 1 <= s <= NS:
                        self.route(n - 1, (s - 1) % 2)

                def turn(self, n, s, lay, k):
                    if live(k, 4):
                        s4 = stream(s, 4)
                        dve.wait_ge(th_done, at(n, 1, -3))
                        nc.vector.scalar_tensor_tensor(gt[:, :, :], th[:, :, :], 1.0, w_ps[:, :, 0:D], ALU.add,
                                                       ALU.mult).then_inc(g_done, 1)
                    if live(k, 1):
                        ly = layer(lay, s, 1)
                        cur = stream(s, 1) % 2
                        zc, zs = z_ps[cur][:, 0:S], z_ps[cur][:, S:2 * S]
                        a1, bb, a2 = (kf[:, ly, 4 * i:4 * i + 4, :].rearrange("p c d -> p (c d)") for i in range(3))
                        dve.wait_ge(fwd_put, at(n, 1, 0))
                        if not (isinstance(n, int) and n < 2):
                            dve.wait_ge(ys_done, at(n, 1, -1))
                        nc.vector.tensor_tensor(pr[:, 0], zc, bb, ALU.mult)
                        nc.vector.tensor_tensor(pr[:, 1], zs, a2, ALU.mult).then_inc(prod_s, 1)
                    if live(k, 4):
                        dve.wait_ge(g_done, at(n, 1, -3))
                        nc.vector.scalar_tensor_tensor(h[:, s4], gt[:, :, :], 0.5, h[:, s4], ALU.mult, ALU.add).then_inc(gated, 1)
                    if live(k, 1):
                        nc.vector.tensor_tensor(pr[:, 2], zc, a1, ALU.mult)
                        nc.vector.tensor_tensor(pr[:, 3], zs, bb, ALU.mult).then_inc(prod_c, 1)
                    if live(k, 2):
                        dve.wait_ge(q_done, at(n, 1, -1))
                        if not (isinstance(n, int) and n < 3):
                            dve.wait_ge(yT_done, at(n, 1, -2))
                        p_ = y_ps[stream(s, 2) % 2][:, 0:HALF]
                        nc.vector.tensor_tensor(sym[:, 0].rearrange("p a d -> p (a d)"), p_, q_sb[:, :], ALU.add)
                        nc.vector.tensor_tensor(sym[:, 1].rearrange("p a d -> p (a d)"), p_, q_sb[:, :], ALU.subtract).then_inc(sym_done, 1)
                    if live(k, 1):
                        dve.wait_ge(prod_c, at(n, 1, 0))
                        if not (isinstance(n, int) and n < 2):
                            dve.wait_ge(inv_put, at(n, 1, -1))
                        nc.vector.tensor_tensor(yc[:, :], pr[:, 2], pr[:, 3], ALU.subtract).then_inc(yc_done, 1)
                    if k is not None and N_K - NS <= k - 4 < N_K:
                        dve.wait_ge(gated, at(n, 1, -3))
                        dve.wait_ge(mixed, at(self.grp, NS, NS))
                        self.finish(s4, k - 4 - (N_K - NS))
                    if live(k, -4):
                        s4 = stream(s, -4)
                        if k == -4:
                            dve.wait_ge(h_ready, at(self.grp, NS, NS))
                        if k is None or k >= 4:
                            dve.wait_ge(gated, at(n, 1, -3))
                        for c in range(C):
                            last = nc.vector.bn_stats(st2[:, s4, c, :], h[:, s4, c, :])
                        last.then_inc(l_stat, 1)
                    if live(k, -1):
                        cur = stream(s, -1) % 2
                        dve.wait_ge(fold1_done, at(n, 1, 2))
                        if not (isinstance(n, int) and n < 1):
                            dve.wait_ge(fwd_put, at(n, 1, 0))
                        nc.vector.tensor_tensor(fold2[:, cur, :, 0], fold1[:, :, 0], fold1[:, :, 1], ALU.add)
                        nc.vector.tensor_tensor(fold2[:, cur, :, 1], fold1[:, :, 0], fold1[:, :, 1], ALU.subtract).then_inc(fold2_done, 1)
                    if live(k, -4):
                        self.moments(n + 4, s4, l_stat, l_mv, l_eps)

                def finish(self, s, i):
                    m = self.grp * NS + i
                    if not (isinstance(m, int) and m < 2):
                        dve.wait_ge(out_stored[s % 2], at(self.grp, 48 * NS // 2, 48 * (i // 2)))
                    nc.vector.tensor_tensor(res[:, s % 2], acc[:, s], h[:, s], ALU.add).then_inc(res_done, 1)

            groups(Vector(), dve)

        @block.tensor
        def _(pe):
            mm = nc.tensor.matmul

            class Tensor:
                def before(self):
                    pe.wait_ge(s_setup, 2)
                    pe.wait_ge(s_loaded, 16 * 4)

                def transpose(self, n, s, grp, first):
                    pe.wait_ge(h_ready, at(n, 1, 1))
                    if not (first and s == 0):
                        pe.wait_ge(xmT_taken, at(n, 1, 0))
                    if s == 0 and not first:
                        pe.wait_ge(sym_done, at(grp, N_K, -1))
                    for c in range(C):
                        last = nc.tensor.transpose(y_ps[0][:, c * P:(c + 1) * P], h[:, s, c, :], ident3[:, :])
                    last.then_inc(xmT_put, 1)

                def logits(self, n, s, grp, first):
                    pe.wait_ge(xmT_taken, at(n, 1, 1))
                    if not (first and s == 0):
                        pe.wait_ge(lg_taken, at(n, 1, 0))
                    if s == 0 and not first:
                        pe.wait_ge(sym_done, at(grp, N_K, 0))
                    for c in range(C):
                        last = mm(y_ps[1][:, c * E:(c + 1) * E], xmT[:, s % 2, c * P:(c + 1) * P], rw[:, :], start=True, stop=True)
                    last.then_inc(lg_put, 1)

                def experts(self, n, s, c, grp, first):
                    if c >= 2 or not (first and s == 0):
                        pe.wait_ge(sel, at(n, C * E_DVE, (c - 1) * E_DVE))
                        pe.wait_ge(scaled, at(n, C, c - 1))
                    if s == 0 and c == 0 and first:
                        pe.wait_ge(ew_loaded, 16)
                        pe.wait_ge(bias_rows, 48)
                    if s == 0 and c < 2 and not first:
                        pe.wait_ge(prod_c, at(grp, N_K, c - 1))
                    for j in range(2):
                        o = z_ps[c % 2][:, j * S:(j + 1) * S]
                        mm(o, xmT[:, s % 2, c * P:(c + 1) * P], ew[:, j * S:(j + 1) * S], start=True, stop=False)
                        last = mm(o, ones3[0:96, :], bias3[0:96, NL * 2 * D + j * S:NL * 2 * D + (j + 1) * S],
                                  start=False, stop=True)
                    last.then_inc(ex_put, 1)

                def start(self, grp, first):
                    pass

                def step(self, grp, s, first, chunks):
                    n = grp * NS + s
                    if s == 1:
                        self.logits(n - 1, 0, grp, first)
                    if s < NS:
                        self.transpose(n, s, grp, first)
                    if 1 <= s <= NS:
                        for c in range(C):
                            self.experts(n - 1, s - 1, c, grp, first)
                            if c == 1 and s < NS:
                                self.logits(n, s, grp, first)
                    if s == NS and first:
                        pe.wait_ge(dft_loaded, 48)

                def turn(self, n, s, lay, k):
                    if live(k, 0):
                        cur = s % 2
                        pe.wait_ge(fold2_done, at(n, 1, 1))
                        if k is not None and k < 2:
                            pe.wait_ge(sel, at(self.grp, NS * C * E_DVE, (NS * C + k - 1) * E_DVE))
                            pe.wait_ge(scaled, at(self.grp, NS * C, NS * C + k - 1))
                            pe.wait_ge(lg_taken, at(self.grp, NS, NS))
                        if not (isinstance(n, int) and n < 2):
                            pe.wait_ge(prod_c, at(n, 1, -1))
                        ss, sd, ds, dd = (fold2[:, cur, i, j] for i in range(2) for j in range(2))
                        rows = [[(0, ss)], [(1, sd)], [(2, ds), (4, dd)], [(3, ds), (5, dd)],
                                [(6, dd)], [(7, ds)], [(8, ss), (10, sd)], [(9, ss), (11, sd)]]
                        for col, terms in enumerate(rows):
                            for i, (block_, src) in enumerate(terms):
                                last = mm(z_ps[cur][:, col * P:(col + 1) * P], dft[:, block_, :], src,
                                          start=i == 0, stop=i == len(terms) - 1)
                        last.then_inc(fwd_put, 1)
                    if live(k, 3):
                        ly = layer(lay, s, 3)
                        pe.wait_ge(gelu_done, at(n, 1, -2))
                        if not (isinstance(n, int) and n < 4):
                            pe.wait_ge(g_done, at(n, 1, -3))
                            pe.wait_ge(th_done, at(n, 1, -3))
                        for c in range(C):
                            mm(w_ps[:, c, :], yg[:, c * P:(c + 1) * P], wout[:, ly, :], start=True, stop=False)
                            last = mm(w_ps[:, c, :], ones3[0:96, :],
                                      bias3[0:96, 0:NL * 2 * D].rearrange("p (l o) -> p l o", l=NL)[:, ly, :], start=False, stop=True)
                        last.then_inc(w_put, 1)
                    if live(k, 1):
                        pe.wait_ge(yc_done, at(n, 1, 0))
                        pe.wait_ge(ys_done, at(n, 1, 0))
                        if not (isinstance(n, int) and n < 3):
                            pe.wait_ge(sym_done, at(n, 1, -2))
                        parts_ = [[(0, yc, 0), (8, ys, 2), (9, ys, 3)], [(7, ys, 1), (2, yc, 2), (3, yc, 3)],
                                  [(1, yc, 1), (10, ys, 2), (11, ys, 3)], [(6, ys, 0), (4, yc, 2), (5, yc, 3)]]
                        for col, terms in enumerate(parts_):
                            for i, (block_, src, f) in enumerate(terms):
                                last = mm(y_ps[stream(s, 1) % 2][:, col * P:(col + 1) * P], src[:, f * P:(f + 1) * P],
                                          idft[:, block_, :], start=i == 0, stop=i == 2)
                        last.then_inc(inv_put, 1)

            groups(Tensor(), pe)


def program(nc, io, out):
    x1_dram = nc.dram_tensor("x1_scratch", (B, S, D), FP32, kind="Internal").ap()
    k_dram = nc.dram_tensor("k_scratch", (NL, D, S), FP32, kind="Internal").ap()
    with nc.sbuf_tensor("kf", [P, NL, 12, D], FP32) as kf, nc.sbuf_tensor("bias_y", [P, NL, S], FP32) as bias_y:
        conv_kernels(nc, io, k_dram, kf, bias_y)
        attention(nc, io, x1_dram)
        s4d_and_experts(nc, io, x1_dram, out, kf, bias_y)


def kernel(**inputs):
    import numpy as _np
    import concourse.bacc as _bacc
    from concourse import mybir as _mybir
    from concourse.bass_utils import run_bass_kernel_spmd as _run

    nc = _bacc.Bacc("TRN2", target_bir_lowering=False, num_devices=1)
    g = {k: _np.asarray(v) for k, v in inputs.items()}
    arrays = dict(shape_constants())
    arrays["x"] = g["L0_attn_x"][:, TOKENS]
    wqk = g["L0_attn_W_qkv"][:2 * D].reshape(2, H, HD, D).transpose(0, 2, 1, 3).reshape(2 * D, D)
    arrays["WqkvT"] = _np.concatenate([wqk, g["L0_attn_W_qkv"][2 * D:]]).T
    arrays["WoT"] = g["L0_attn_W_o"].T
    arrays["W1T"] = g["L0_ffn_W1"].T
    arrays["W2T"] = g["L0_ffn_W2"].T.reshape(NF, P, D).transpose(1, 0, 2)
    arrays["b1"] = g["L0_ffn_b1"].reshape(NF, P).T
    arrays["b2"] = g["L0_ffn_b2"]
    arrays["ln_w"] = g["L1_attn_ln_w"]
    modes = [_np.broadcast_to(g["L1_attn_log_dt"][:, None, :], (NL, NM, D))]
    modes += [g["L1_attn_" + k].transpose(0, 2, 1) for k in ("A_re_log", "A_im", "C_re", "C_im")]
    modes = _np.stack(modes).reshape(5, NL // 2, 2, 1, NM, D)
    arrays["s4d_par"] = _np.broadcast_to(modes, (5, NL // 2, 2, 2, NM, D)).transpose(2, 3, 4, 0, 1, 5).reshape(P, 5, NL // 2, D)
    arrays["D_skipT"], arrays["ln_bT"] = g["L1_attn_D_skip"].T, g["L1_attn_ln_b"].T
    arrays["WoutT"] = g["L1_attn_W_out"].transpose(2, 0, 1)
    arrays["biases"] = _np.concatenate([g["L1_attn_b_out"].reshape(-1), g["L1_ffn_expert_b"].reshape(-1)]).reshape(P, -1)
    arrays["router_w"], arrays["router_b"] = g["L1_ffn_router_w"], g["L1_ffn_router_b"]
    arrays["EW"] = g["L1_ffn_expert_w"].transpose(1, 0, 2).reshape(D, E * D)
    arrays = {"in_" + k: _np.ascontiguousarray(v) for k, v in arrays.items()}
    io = {k[3:]: nc.dram_tensor(k, v.shape, _mybir.dt.from_np(v.dtype), kind="ExternalInput").ap() for k, v in arrays.items()}
    out = nc.dram_tensor("out", (B, S, D), _mybir.dt.float32, kind="ExternalOutput").ap()
    program(nc, io, out)
    r = _run(nc, [arrays], core_ids=[0])
    got = r.results[0]["out"]
    back = _np.argsort(TOKENS)
    return _np.ascontiguousarray(_np.asarray(got)[:, back])
```
